# Optimizing a Trainium2 kernel written in Bass

```python
import numpy as np
import jax
import jax.numpy as jnp

def _softmax(x, axis=-1):
    return jax.nn.softmax(x, axis=axis)

def _gelu(x):
    return jax.nn.gelu(x, approximate=True)

def _silu(x):
    return jax.nn.silu(x)

def _sigmoid(x):
    return jax.nn.sigmoid(x)

def _layernorm(x, axis=-1, eps=1e-05):
    m = jnp.mean(x, axis=axis, keepdims=True)
    v = jnp.var(x, axis=axis, keepdims=True)
    return (x - m) / jnp.sqrt(v + eps)

def _scatter_add(tgt, idx, src, axis=0):
    return tgt.at[idx].add(src)

def _segment_sum(src, seg, n):
    return jax.ops.segment_sum(src, seg, n)
kernel_name = 'mk_adj_preln_d4_adj_r2_f3cd3f'

def setup_inputs(seed: int=0):
    np.random.seed(seed)
    _w = jnp.asarray

    def _rec_inputs():
        import jax
        import jax.numpy as jnp
        _gk = jax.random.key(seed)
        x = -0.0002928 + 1 * jax.random.normal(jax.random.fold_in(_gk, 1), (2048, 512), jnp.float32)
        _a = jax.random.bernoulli(jax.random.fold_in(_gk, 2), 0.0078125, (2048, 2048))
        _a = jnp.logical_or(_a, jnp.swapaxes(_a, -1, -2))
        _a = jnp.logical_or(_a, jnp.eye(2048, dtype=bool))
        _af = _a.astype(jnp.float32)
        adj = _af
        return (x, adj)
    x, adj = _rec_inputs()

    def _L0_gnn_setup():
        import jax, jax.numpy as jnp
        import numpy as np
        N = 2048
        D_IN = 512
        H = 16
        DH = D_IN // H
        ALPHA = 0.2
        MASK_VAL = -65500.0
        key = jax.random.key(seed)
        ks = jax.random.split(key, 7)
        x = jax.random.normal(ks[0], (N, D_IN), dtype=jnp.float32)
        adj = jax.random.randint(ks[1], (N, N), 0, 2).astype(jnp.float32)
        s = 1.0 / np.sqrt(D_IN)
        W_seq = jax.random.normal(ks[2], (D_IN, D_IN), dtype=jnp.float32) * s
        a1 = jax.random.normal(ks[3], (DH,), dtype=jnp.float32) / np.sqrt(DH)
        a2 = jax.random.normal(ks[4], (DH,), dtype=jnp.float32) / np.sqrt(DH)
        W_out = jax.random.normal(ks[5], (D_IN, D_IN), dtype=jnp.float32) * s
        b_out = jax.random.normal(ks[6], (D_IN,), dtype=jnp.float32) * 0.01
        return {'x': x, 'adj': adj, 'W_seq': W_seq, 'a1': a1, 'a2': a2, 'W_out': W_out, 'b_out': b_out}
    _L0_gnn_all = _L0_gnn_setup()
    _L0_gnn_in = {k: v for k, v in _L0_gnn_all.items() if k in ('W_seq', 'a1', 'a2', 'W_out', 'b_out')}
    del _L0_gnn_all

    def _L1_gnn_setup():
        import jax, jax.numpy as jnp
        import numpy as np
        D_IN, D_ATTN, STEPS = (512, 64, 2)
        P_TOP, TAU, LN_EPS = (0.9, 1.0, 1e-05)
        N = 2048

        def _xavier(key, shape):
            fan_in, fan_out = (shape[0], shape[1])
            lim = jnp.sqrt(6.0 / (fan_in + fan_out))
            return jax.random.uniform(key, shape, jnp.float32, -lim, lim)

        def _adj_from_feats(Xa, W1, W2, W3):
            Q = Xa @ W1
            K = Xa @ W3
            logits = Q @ W2 @ K.T / TAU
            n = logits.shape[1]
            order = jnp.argsort(-logits, axis=1)
            vals = jnp.take_along_axis(logits, order, axis=1)
            probs = jax.nn.softmax(vals, axis=1)
            csum = jnp.cumsum(probs, axis=1)
            k_i = jnp.sum(csum < P_TOP, axis=1) + 1
            keep = jnp.arange(n)[None, :] < k_i[:, None]
            masked_sorted = jnp.where(keep, vals, -jnp.inf)
            rows = jnp.arange(n)[:, None]
            masked = jnp.full_like(logits, -jnp.inf).at[rows, order].set(masked_sorted)
            return jax.nn.softmax(masked, axis=1)
        key = jax.random.key(seed)
        ks = jax.random.split(key, 12)
        X = jax.random.normal(ks[0], (N, D_IN), jnp.float32)
        S = jax.random.uniform(ks[1], (N, N), jnp.float32)
        W1 = _xavier(ks[2], (D_IN, D_ATTN))
        W3 = _xavier(ks[3], (D_IN, D_ATTN))
        W2 = _xavier(ks[4], (D_ATTN, D_ATTN))
        U1_0 = _xavier(ks[5], (D_IN, D_IN))
        U1_1 = _xavier(ks[6], (D_IN, D_IN))
        U2_0 = _xavier(ks[7], (D_IN, D_IN))
        U2_1 = _xavier(ks[8], (D_IN, D_IN))
        gamma = jnp.ones((D_IN,), jnp.float32)
        beta = jnp.zeros((D_IN,), jnp.float32)
        return {'X': X, 'S': S, 'W1': W1, 'W2': W2, 'W3': W3, 'U1_0': U1_0, 'U1_1': U1_1, 'U2_0': U2_0, 'U2_1': U2_1, 'gamma': gamma, 'beta': beta}
    _L1_gnn_all = _L1_gnn_setup()
    _L1_gnn_in = {k: v for k, v in _L1_gnn_all.items() if k in ('W1', 'W2', 'W3', 'U1_0', 'U1_1', 'U2_0', 'U2_1', 'gamma', 'beta')}
    del _L1_gnn_all

    def _L2_gnn_setup():
        import jax, jax.numpy as jnp
        import numpy as np
        ALPHA = 0.2
        NEG = -9000000000000000.0
        N, NFEAT, NHID, NHEADS = (2048, 512, 64, 8)
        EMB = NHID * NHEADS
        key = jax.random.key(seed)
        ks = jax.random.split(key, 16)
        x = jax.random.normal(ks[0], (N, NFEAT), dtype=jnp.float32)
        adj = (jax.random.uniform(ks[1], (N, N)) < 0.01).astype(jnp.float32)
        adj = jnp.maximum(adj, jnp.eye(N, dtype=jnp.float32))
        s = 0.05
        W = jax.random.normal(ks[2], (NHEADS, NFEAT, NHID), dtype=jnp.float32) * s
        a1 = jax.random.normal(ks[3], (NHEADS, NHID), dtype=jnp.float32) * s
        a2 = jax.random.normal(ks[4], (NHEADS, NHID), dtype=jnp.float32) * s
        W1 = jax.random.normal(ks[5], (EMB // 2, EMB), dtype=jnp.float32) * s
        b1 = jnp.zeros((EMB // 2,), dtype=jnp.float32)
        W2 = jax.random.normal(ks[6], (NFEAT // 4, EMB // 2), dtype=jnp.float32) * s
        b2 = jnp.zeros((NFEAT // 4,), dtype=jnp.float32)
        W3 = jax.random.normal(ks[7], (NFEAT // 2, NFEAT // 4), dtype=jnp.float32) * s
        b3 = jnp.zeros((NFEAT // 2,), dtype=jnp.float32)
        W4 = jax.random.normal(ks[8], (NFEAT, NFEAT // 2), dtype=jnp.float32) * s
        b4 = jnp.zeros((NFEAT,), dtype=jnp.float32)
        return {'x': x, 'adj': adj, 'W': W, 'a1': a1, 'a2': a2, 'W1': W1, 'b1': b1, 'W2': W2, 'b2': b2, 'W3': W3, 'b3': b3, 'W4': W4, 'b4': b4}
    _L2_gnn_all = _L2_gnn_setup()
    _L2_gnn_in = {k: v for k, v in _L2_gnn_all.items() if k in ('W', 'a1', 'a2', 'W1', 'b1', 'W2', 'b2', 'W3', 'b3', 'W4', 'b4')}
    del _L2_gnn_all

    def _L3_gnn_setup():
        import jax, jax.numpy as jnp
        import numpy as np
        import math
        SENT_DIM = 512
        N_SENT = 2048
        key = jax.random.key(seed)
        ks = jax.random.split(key, 8)
        D = SENT_DIM
        s = 1.0 / math.sqrt(D)
        return {'sent_embed': jax.random.normal(ks[0], (N_SENT, D), dtype=jnp.float32), 'adj_tensor': jax.random.randint(ks[1], (N_SENT, N_SENT), 0, 2).astype(jnp.float32), 'W_q': jax.random.uniform(ks[2], (D, D), jnp.float32, -s, s), 'b_q': jax.random.uniform(ks[3], (D,), jnp.float32, -s, s), 'W_k': jax.random.uniform(ks[4], (D, D), jnp.float32, -s, s), 'b_k': jax.random.uniform(ks[5], (D,), jnp.float32, -s, s), 'W_v': jax.random.uniform(ks[6], (D, D), jnp.float32, -s, s), 'b_v': jax.random.uniform(ks[7], (D,), jnp.float32, -s, s)}
    _L3_gnn_all = _L3_gnn_setup()
    _L3_gnn_in = {k: v for k, v in _L3_gnn_all.items() if k in ('W_q', 'b_q', 'W_k', 'b_k', 'W_v', 'b_v')}
    del _L3_gnn_all
    return {'x': x, 'adj': adj, 'L0_gnn_W_seq': _L0_gnn_in['W_seq'], 'L0_gnn_a1': _L0_gnn_in['a1'], 'L0_gnn_a2': _L0_gnn_in['a2'], 'L0_gnn_W_out': _L0_gnn_in['W_out'], 'L0_gnn_b_out': _L0_gnn_in['b_out'], 'L1_gnn_W1': _L1_gnn_in['W1'], 'L1_gnn_W2': _L1_gnn_in['W2'], 'L1_gnn_W3': _L1_gnn_in['W3'], 'L1_gnn_U1_0': _L1_gnn_in['U1_0'], 'L1_gnn_U1_1': _L1_gnn_in['U1_1'], 'L1_gnn_U2_0': _L1_gnn_in['U2_0'], 'L1_gnn_U2_1': _L1_gnn_in['U2_1'], 'L1_gnn_gamma': _L1_gnn_in['gamma'], 'L1_gnn_beta': _L1_gnn_in['beta'], 'L2_gnn_W': _L2_gnn_in['W'], 'L2_gnn_a1': _L2_gnn_in['a1'], 'L2_gnn_a2': _L2_gnn_in['a2'], 'L2_gnn_W1': _L2_gnn_in['W1'], 'L2_gnn_b1': _L2_gnn_in['b1'], 'L2_gnn_W2': _L2_gnn_in['W2'], 'L2_gnn_b2': _L2_gnn_in['b2'], 'L2_gnn_W3': _L2_gnn_in['W3'], 'L2_gnn_b3': _L2_gnn_in['b3'], 'L2_gnn_W4': _L2_gnn_in['W4'], 'L2_gnn_b4': _L2_gnn_in['b4'], 'L3_gnn_W_q': _L3_gnn_in['W_q'], 'L3_gnn_b_q': _L3_gnn_in['b_q'], 'L3_gnn_W_k': _L3_gnn_in['W_k'], 'L3_gnn_b_k': _L3_gnn_in['b_k'], 'L3_gnn_W_v': _L3_gnn_in['W_v'], 'L3_gnn_b_v': _L3_gnn_in['b_v']}

def reference(x, adj, L0_gnn_W_seq, L0_gnn_a1, L0_gnn_a2, L0_gnn_W_out, L0_gnn_b_out, L1_gnn_W1, L1_gnn_W2, L1_gnn_W3, L1_gnn_U1_0, L1_gnn_U1_1, L1_gnn_U2_0, L1_gnn_U2_1, L1_gnn_gamma, L1_gnn_beta, L2_gnn_W, L2_gnn_a1, L2_gnn_a2, L2_gnn_W1, L2_gnn_b1, L2_gnn_W2, L2_gnn_b2, L2_gnn_W3, L2_gnn_b3, L2_gnn_W4, L2_gnn_b4, L3_gnn_W_q, L3_gnn_b_q, L3_gnn_W_k, L3_gnn_b_k, L3_gnn_W_v, L3_gnn_b_v):
    import jax
    import jax.numpy as jnp

    def _L0_gnn_ref(x, adj, W_seq, a1, a2, W_out, b_out):
        import jax, jax.numpy as jnp
        import numpy as np
        N = 2048
        D_IN = 512
        H = 16
        DH = D_IN // H
        ALPHA = 0.2
        MASK_VAL = -65500.0
        seq = (x @ W_seq).reshape(N, H, DH)
        score1 = jnp.einsum('nhd,d->hn', seq, a1)
        score2 = jnp.einsum('nhd,d->hn', seq, a2)
        scores = score1[:, :, None] + score2[:, None, :]
        scores = jax.nn.leaky_relu(scores, negative_slope=ALPHA)
        scores = scores + (1.0 - adj)[None, :, :] * MASK_VAL
        attn = jax.nn.softmax(scores, axis=-1)
        hidden = jnp.einsum('hij,jhd->ihd', attn, seq).reshape(N, D_IN)
        hidden = hidden @ W_out + b_out
        return jax.nn.elu(hidden)

    def _L1_gnn_ref(X, S, W1, W2, W3, U1_0, U1_1, U2_0, U2_1, gamma, beta):
        import jax, jax.numpy as jnp
        import numpy as np
        D_IN, D_ATTN, STEPS = (512, 64, 2)
        P_TOP, TAU, LN_EPS = (0.9, 1.0, 1e-05)
        N = 2048

        def _xavier(key, shape):
            fan_in, fan_out = (shape[0], shape[1])
            lim = jnp.sqrt(6.0 / (fan_in + fan_out))
            return jax.random.uniform(key, shape, jnp.float32, -lim, lim)

        def _adj_from_feats(Xa, W1, W2, W3):
            Q = Xa @ W1
            K = Xa @ W3
            logits = Q @ W2 @ K.T / TAU
            n = logits.shape[1]
            order = jnp.argsort(-logits, axis=1)
            vals = jnp.take_along_axis(logits, order, axis=1)
            probs = jax.nn.softmax(vals, axis=1)
            csum = jnp.cumsum(probs, axis=1)
            k_i = jnp.sum(csum < P_TOP, axis=1) + 1
            keep = jnp.arange(n)[None, :] < k_i[:, None]
            masked_sorted = jnp.where(keep, vals, -jnp.inf)
            rows = jnp.arange(n)[:, None]
            masked = jnp.full_like(logits, -jnp.inf).at[rows, order].set(masked_sorted)
            return jax.nn.softmax(masked, axis=1)
        n = X.shape[0]
        S = S + jnp.eye(n, dtype=X.dtype)
        R = S / jnp.clip(S.sum(axis=1, keepdims=True), 1e-12)
        Z = jnp.zeros_like(X)
        Xf, Xa = (X, X)
        U1s, U2s = ((U1_0, U1_1), (U2_0, U2_1))
        for s in range(STEPS):
            A = _adj_from_feats(Xa, W1, W2, W3)
            Xf = R @ Xf
            Xa = A @ Xa
            Z = Z + (Xf @ U1s[s] + Xa @ U2s[s])
        Y = X + Z
        mu = Y.mean(axis=-1, keepdims=True)
        var = Y.var(axis=-1, keepdims=True)
        return (Y - mu) * jax.lax.rsqrt(var + LN_EPS) * gamma + beta

    def _L2_gnn_ref(x, adj, W, a1, a2, W1, b1, W2, b2, W3, b3, W4, b4):
        import jax, jax.numpy as jnp
        import numpy as np
        ALPHA = 0.2
        NEG = -9000000000000000.0
        N, NFEAT, NHID, NHEADS = (2048, 512, 64, 8)
        EMB = NHID * NHEADS
        Wh = jnp.einsum('nf,hfd->hnd', x, W)
        e_src = jnp.einsum('hnd,hd->hn', Wh, a1)
        e_dst = jnp.einsum('hnd,hd->hn', Wh, a2)
        e = jax.nn.leaky_relu(e_src[:, :, None] + e_dst[:, None, :], ALPHA)
        e = jnp.where(adj[None] > 0, e, NEG)
        att = jax.nn.softmax(e, axis=-1)
        h = jnp.einsum('hnm,hmd->hnd', att, Wh)
        h = jax.nn.elu(h)
        enc = jnp.transpose(h, (1, 0, 2)).reshape(x.shape[0], -1)
        out = jax.nn.relu(enc @ W1.T + b1)
        out = jax.nn.relu(out @ W2.T + b2)
        out = jax.nn.relu(out @ W3.T + b3)
        out = out @ W4.T + b4
        return out

    def _L3_gnn_ref(sent_embed, adj_tensor, W_q, b_q, W_k, b_k, W_v, b_v):
        import jax, jax.numpy as jnp
        import numpy as np
        import math
        SENT_DIM = 512
        N_SENT = 2048
        q = sent_embed @ W_q.T + b_q
        k = sent_embed @ W_k.T + b_k
        v = sent_embed @ W_v.T + b_v
        scale = 1.0 / math.sqrt(sent_embed.shape[-1])
        z = scale * (q @ k.T)
        spare_z = z * adj_tensor
        spare_z = jnp.where(spare_z == 0.0, jnp.asarray(-10000.0, spare_z.dtype), spare_z)
        attn = jax.nn.softmax(spare_z, axis=1)
        out = attn @ v
        return jax.nn.relu(out)
    h = jnp.maximum(_layernorm(x, axis=-1), 0.0)
    x = x + _L0_gnn_ref(h, adj, L0_gnn_W_seq, L0_gnn_a1, L0_gnn_a2, L0_gnn_W_out, L0_gnn_b_out)
    h = jnp.maximum(_layernorm(x, axis=-1), 0.0)
    x = x + _L1_gnn_ref(h, adj, L1_gnn_W1, L1_gnn_W2, L1_gnn_W3, L1_gnn_U1_0, L1_gnn_U1_1, L1_gnn_U2_0, L1_gnn_U2_1, L1_gnn_gamma, L1_gnn_beta)
    h = jnp.maximum(_layernorm(x, axis=-1), 0.0)
    x = x + _L2_gnn_ref(h, adj, L2_gnn_W, L2_gnn_a1, L2_gnn_a2, L2_gnn_W1, L2_gnn_b1, L2_gnn_W2, L2_gnn_b2, L2_gnn_W3, L2_gnn_b3, L2_gnn_W4, L2_gnn_b4)
    h = jnp.maximum(_layernorm(x, axis=-1), 0.0)
    x = x + _L3_gnn_ref(h, adj, L3_gnn_W_q, L3_gnn_b_q, L3_gnn_W_k, L3_gnn_b_k, L3_gnn_W_v, L3_gnn_b_v)
    return x

_drawn_inputs = setup_inputs


def setup_inputs(seed=0):
    import zlib

    import numpy as np

    out = dict(_drawn_inputs(seed))
    spreads = {'L1_gnn_gamma': (1.0, 0.2),
     'L1_gnn_beta': (0.0, 0.1),
     'L2_gnn_b1': (0.0, 0.8),
     'L2_gnn_b2': (0.0, 0.61),
     'L2_gnn_b3': (0.0, 0.1),
     'L2_gnn_b4': (0.0, 0.1)}
    factors = {'L0_gnn_b_out': 3.594,
     'L2_gnn_a1': 64.0,
     'L2_gnn_a2': 22.442,
     'L3_gnn_W_q': 8.0,
     'L3_gnn_b_q': 29.023,
     'L3_gnn_W_k': 8.0,
     'L3_gnn_b_k': 64.0,
     'L3_gnn_b_v': 5.339}
    for name, (base, spread) in spreads.items():
        noise = np.random.default_rng([zlib.crc32(name.encode()), seed]).standard_normal(out[name].shape)
        drawn = base * np.exp(spread * noise) if base else spread * noise
        out[name] = jnp.asarray(drawn.astype(out[name].dtype))
    for name, factor in factors.items():
        out[name] = (out[name] * factor).astype(out[name].dtype)
    return out
```

```python
from contextlib import ExitStack

import numpy as np

import concourse.bass as bass
from concourse import mybir

F32 = mybir.dt.float32
BF16 = mybir.dt.bfloat16
ALU = mybir.AluOpType
ACT = mybir.ActivationFunctionType
AX = mybir.AxisListType

N = 2048
D = 512
P = 128
NT = N // P
KC = D // P
PARTS = 3
EPS = 1e-5


class Link:

    def __init__(self, eng, sem, base=0):
        self.eng, self.sem, self.base, self.k = eng, sem, base, 0

    def __call__(self, ins):
        self.k += 1
        ins.then_inc(self.sem, 1)
        self.eng.wait_ge(self.sem, self.base + self.k)


def cols(t, width):
    return bass.ds(t * width, width)


class Program:

    def __init__(self, nc):
        self.nc = nc
        self.n = 0
        self.ticks = nc.alloc_semaphore("ticks")

    def stage(self):
        self.ctx = ExitStack()
        self.n += 1
        sems = self.sems = []

        def free():
            for s in sems:
                self.nc.gpsimd.sem_clear(s)
                self.nc.release_semaphore(s)
        self.ctx.callback(free)
        return self.ctx

    def sb(self, name, shape, dt=F32):
        return self.ctx.enter_context(self.nc.sbuf_tensor(f"{name}_{self.n}", shape, dt))

    def ps(self, name, shape, dt=F32):
        return self.ctx.enter_context(self.nc.psum_tensor(f"{name}_{self.n}", shape, dt))

    def sem(self, name):
        sem = self.nc.alloc_semaphore(f"{name}_{self.n}")
        if not name.rstrip("01").endswith("stored"):
            self.sems.append(sem)
        return sem

    def passed(self, eng):
        eng.sem_inc(self.ticks, 1)

    def block(self):
        return self.ctx.enter_context(self.nc.Block())


def constants(pr, c):
    nc = pr.nc
    with pr.stage():
        filled = pr.sem("filled")
        block = pr.block()

        @block.gpsimd
        def _(pool):
            nc.gpsimd.memset(c["id32"][:], 0.0).then_inc(filled, 1)
            nc.gpsimd.memset(c["id16"][:], 0.0).then_inc(filled, 1)
            nc.gpsimd.memset(c["ones16"][:], 1.0)
            nc.gpsimd.memset(c["zero16"][:], 0.0)
            nc.gpsimd.memset(c["eps"][:], EPS)
            pool.wait_ge(filled, 2)
            for m in (c["id32"], c["id16"]):
                nc.gpsimd.affine_select(out=m[:], in_=m[:], compare_op=ALU.not_equal, fill=1.0, base=0,
                                        pattern=[[-1, P]], channel_multiplier=1)


def transpose_adjacency(pr, c, adj, adjT_dram):
    nc = pr.nc
    adjT = c["adjT"]
    with pr.stage():
        raw = [pr.sb(f"raw{u}", [P, N]) for u in range(2)]
        cast = [pr.sb(f"cast{u}", [P, N], BF16) for u in range(2)]
        turned = [pr.ps(f"turned{u}", [P, NT, P], BF16) for u in range(2)]
        loaded = [pr.sem(f"loaded{u}") for u in range(2)]
        cast_done = pr.sem("cast_done")
        turn_done = pr.sem("turn_done")
        kept = pr.sem("kept")
        stored = pr.sem("stored")
        block = pr.block()

        @block.sync
        def _(sp):
            for u in range(2):
                sp.dma_start(raw[u][:], adj[cols(u, P), :]).then_inc(loaded[u], 16)
            with sp.Fori(1, NT // 2) as i:
                for u in range(2):
                    sp.wait_ge(cast_done, 2 * i + u + 1)
                    sp.dma_start(raw[u][:], adj[cols(2 * i + u, P), :]).then_inc(loaded[u], 16)
            sp.wait_ge(kept, NT + 2)
            sp.dma_start(adjT_dram.rearrange("(t p) n -> p t n", p=P), adjT[:]).then_inc(stored, 16)
            sp.wait_ge(stored, 16)

        @block.vector
        def _(dve):
            dve.sem_inc(cast_done, 2)
            with dve.Fori(0, NT // 2) as i:
                for u in range(2):
                    dve.wait_ge(loaded[u], 16 * i + 16)
                    dve.wait_ge(turn_done, 2 * i + u + 1)
                    nc.vector.tensor_copy(cast[u][:], raw[u][:]).then_inc(cast_done, 1)

        @block.tensor
        def _(pe):
            pe.sem_inc(turn_done, 2)
            with pe.Fori(0, NT // 2) as i:
                for u in range(2):
                    pe.wait_ge(cast_done, 2 * i + u + 3)
                    pe.wait_ge(kept, 2 * i + u + 1)
                    for j in range(NT):
                        ins = nc.tensor.transpose(turned[u][:, j, :], cast[u][:, j * P:(j + 1) * P], c["id16"][:])
                    ins.then_inc(turn_done, 1)

        @block.scalar
        def _(act):
            act.sem_inc(kept, 2)
            with act.Fori(0, NT // 2) as i:
                for u in range(2):
                    act.wait_ge(turn_done, 2 * i + u + 3)
                    nc.scalar.copy(adjT[:, :, cols(2 * i + u, P)], turned[u][:]).then_inc(kept, 1)


def reload_adjacency(pr, c, adjT_dram):
    with pr.stage():
        loaded = pr.sem("loaded")
        block = pr.block()

        @block.sync
        def _(sp):
            sp.dma_start(c["adjT"][:], adjT_dram.rearrange("(t p) n -> p t n", p=P)).then_inc(loaded, 16)
            sp.wait_ge(loaded, 16)


def norm_and_turn(pr, c, x_dram, h_dram=None):
    nc = pr.nc
    f = {}
    x = [pr.sb(f"x{u}", [P, D]) for u in range(2)]
    h = [pr.sb(f"h{u}", [P, D]) for u in range(2)]
    hT = [pr.sb(f"hT{u}", [P, KC, P]) for u in range(2)]
    stats = [pr.sb(f"stats{u}", [P, 6]) for u in range(2)]
    mv = [pr.sb(f"mv{u}", [P, 2]) for u in range(2)]
    std = [pr.sb(f"std{u}", [P, 1]) for u in range(2)]
    rstd = [pr.sb(f"rstd{u}", [P, 1]) for u in range(2)]
    turned = pr.ps("hturned", [P, KC, P])
    x_loaded = [pr.sem(f"x_loaded{u}") for u in range(2)]
    mv_done, std_done, h_done = pr.sem("mv_done"), pr.sem("std_done"), pr.sem("h_done")
    turn_done, hT_done = pr.sem("turn_done"), pr.sem("hT_done")
    order = pr.sem("order")

    def load(sp):
        for u in range(2):
            sp.dma_start(x[u][:], x_dram[cols(u, P), :]).then_inc(x_loaded[u], 16)
        with sp.Fori(1, NT // 2) as i:
            for u in range(2):
                sp.wait_ge(h_done, 2 * i + u + 1)
                sp.dma_start(x[u][:], x_dram[cols(2 * i + u, P), :]).then_inc(x_loaded[u], 16)

    def dve_step(dve, i, u, h_used, h_stored=None):
        link = Link(dve, order, (2 * i + u) * 4)
        dve.wait_ge(x_loaded[u], 16 * i + 16)
        link(nc.vector.bn_stats(stats[u][:], x[u][:]))
        pr.passed(dve)
        nc.vector.bn_aggr(mv[u][:], stats[u][:]).then_inc(mv_done, 1)
        dve.wait_ge(mv_done, 2 * i + u + 1)
        dve.wait_ge(std_done, 2 * i + u + 1)
        link(nc.vector.reciprocal(rstd[u][:], std[u][:]))
        for s in h_used:
            dve.wait_ge(s, 2 * i + u + 1)
        if h_stored:
            dve.wait_ge(h_stored[u], 16 * i)
        link(nc.vector.tensor_scalar(h[u][:], x[u][:], mv[u][:, 0:1], rstd[u][:, 0:1], ALU.subtract, ALU.mult))
        link(nc.vector.tensor_scalar(h[u][:], h[u][:], 0.0, None, ALU.max))
        dve.sem_inc(h_done, 1)

    def act_std(act, i, u):
        act.wait_ge(mv_done, 2 * i + u + 1)
        nc.scalar.activation(std[u][:], mv[u][:, 1:2], ACT.Sqrt, bias=c["eps"][:, 0:1]).then_inc(std_done, 1)

    def pe_turn(pe, i, u):
        pe.wait_ge(h_done, 2 * i + u + 3)
        pe.wait_ge(hT_done, 2 * i + u + 2)
        for k in range(KC):
            ins = nc.tensor.transpose(turned[:, k, :], h[u][:, k * P:(k + 1) * P], c["id32"][:])
        ins.then_inc(turn_done, 1)

    def act_hT(act, i, u, hT_used):
        act.wait_ge(turn_done, 2 * i + u + 3)
        act.wait_ge(hT_used, 2 * i + u + 1)
        nc.scalar.copy(hT[u][:], turned[:]).then_inc(hT_done, 1)

    f.update(x=x, h=h, hT=hT, h_done=h_done, turn_done=turn_done, hT_done=hT_done, std_done=std_done,
             load=load, dve_step=dve_step, act_std=act_std, pe_turn=pe_turn, act_hT=act_hT)
    return f


def heads_project(pr, c, x_dram, w, a1, a2, seq_dram, scores, H, DH):
    nc = pr.nc
    with pr.stage():
        f = norm_and_turn(pr, c, x_dram)
        wsb = pr.sb("w", [P, KC, D])
        arow = pr.sb("arow", [P, 2, D])
        seq = [pr.sb(f"seq{u}", [P, D]) for u in range(2)]
        prod = [pr.sb(f"prod{v}", [P, H, DH]) for v in range(2)]
        proj = [pr.ps(f"proj{u}", [P, D]) for u in range(2)]
        w_loaded, a_loaded = pr.sem("w_loaded"), pr.sem("a_loaded")
        proj_done, seq_done, scored = pr.sem("proj_done"), pr.sem("seq_done"), pr.sem("scored")
        stored = [pr.sem(f"stored{u}") for u in range(2)]
        order = pr.sem("order_scores")
        block = pr.block()

        @block.sync
        def _(sp):
            sp.dma_start(wsb[:], w.rearrange("(k p) n -> p k n", p=P)).then_inc(w_loaded, 16)
            for v, a in enumerate((a1, a2)):
                sp.dma_start(arow[:, v, :], a.broadcast_to([P, D])).then_inc(a_loaded, 16)
            f["load"](sp)

        @block.gpsimd
        def _(pool):
            with pool.Fori(0, NT // 2) as i:
                for u in range(2):
                    pool.wait_ge(seq_done, 2 * i + u + 3)
                    pool.dma_start(seq_dram[cols(2 * i + u, P), :], seq[u][:]).then_inc(stored[u], 16)
            for u in range(2):
                pool.wait_ge(stored[u], 16 * (NT // 2))

        @block.vector
        def _(dve):
            dve.sem_inc(f["h_done"], 2)
            dve.sem_inc(scored, 2)
            dve.wait_ge(a_loaded, 32)
            with dve.Fori(0, NT // 2) as i:
                for u in range(2):
                    t = 2 * i + u
                    f["dve_step"](dve, i, u, [f["turn_done"]])
                    dve.wait_ge(seq_done, t + 3)
                    link = Link(dve, order, t * 3)
                    for v in range(2):
                        ins = nc.vector.tensor_tensor(prod[v][:].rearrange("p h d -> p (h d)"), seq[u][:],
                                                      arow[:, v, :], ALU.mult)
                        if v == 0:
                            ins.then_inc(order, 1)
                            link.k += 1
                        else:
                            link(ins)
                    nc.vector.tensor_reduce(scores[:, 0, t, :], prod[0][:], AX.X, ALU.add)
                    link(nc.vector.tensor_reduce(scores[:, 1, t, :], prod[1][:], AX.X, ALU.add))
                    dve.sem_inc(scored, 1)

        @block.tensor
        def _(pe):
            pe.sem_inc(f["turn_done"], 2)
            pe.sem_inc(proj_done, 2)
            pe.wait_ge(w_loaded, 16)
            with pe.Fori(0, NT // 2) as i:
                for u in range(2):
                    t = 2 * i + u
                    f["pe_turn"](pe, i, u)
                    pe.wait_ge(f["hT_done"], t + 3)
                    pe.wait_ge(seq_done, t + 1)
                    for k in range(KC):
                        ins = nc.tensor.matmul(proj[u][:], f["hT"][u][:, k, :], wsb[:, k, :],
                                               start=(k == 0), stop=(k == KC - 1))
                    ins.then_inc(proj_done, 1)

        @block.scalar
        def _(act):
            act.sem_inc(f["hT_done"], 2)
            act.sem_inc(seq_done, 2)
            with act.Fori(0, NT // 2) as i:
                for u in range(2):
                    t = 2 * i + u
                    f["act_std"](act, i, u)
                    f["act_hT"](act, i, u, proj_done)
                    act.wait_ge(proj_done, t + 3)
                    act.wait_ge(scored, t + 1)
                    act.wait_ge(stored[u], 16 * i)
                    nc.scalar.copy(seq[u][:], proj[u][:]).then_inc(seq_done, 1)


def heads_factors(pr, c, scores, fac, arow_dram, H):
    nc = pr.nc
    with pr.stage():
        top = pr.sb("top", [P, H])
        top_all = pr.sb("top_all", [P, H])
        work = [pr.sb(f"work{v}", [P, NT, H]) for v in range(3)]
        rows = pr.sb("rows", [H, N])
        turned = pr.ps("turned", [H, NT, P])
        order, top_done, all_done = pr.sem("order"), pr.sem("top_done"), pr.sem("all_done")
        turn_done, rows_done, stored = pr.sem("turn_done"), pr.sem("rows_done"), pr.sem("stored")
        a, b = scores[:, 0], scores[:, 1]
        wide = top_all[:].unsqueeze(1).broadcast_to([P, NT, H])
        block = pr.block()

        @block.vector
        def _(dve):
            link = Link(dve, order)
            nc.vector.tensor_reduce(top[:], b.rearrange("p t h -> p h t"), AX.X, ALU.max).then_inc(top_done, 1)
            nc.vector.tensor_scalar(fac[:, 4], b, -1.0, None, ALU.mult)
            dve.wait_ge(all_done, 1)
            nc.vector.tensor_tensor(work[0][:], b, wide, ALU.subtract).then_inc(order, 1)
            link.k += 1
            link(nc.vector.tensor_tensor(work[1][:], a, wide, ALU.add))
            link(nc.vector.tensor_scalar(work[2][:], work[1][:], 0.0, None, ALU.min))
            link(nc.vector.tensor_scalar(work[1][:], work[1][:], 0.0, None, ALU.max))

        @block.gpsimd
        def _(pool):
            pool.wait_ge(top_done, 1)
            nc.gpsimd.partition_all_reduce(top_all[:], top[:], P, bass.bass_isa.ReduceOp.max).then_inc(all_done, 1)

        @block.tensor
        def _(pe):
            for t in range(NT):
                ins = nc.tensor.transpose(turned[:, t, :], scores[:, 0, t, :], c["id32"][:])
            ins.then_inc(turn_done, 1)

        @block.scalar
        def _(act):
            act.wait_ge(order, 4)
            nc.scalar.activation(fac[:, 0], work[0][:], ACT.Exp)
            nc.scalar.activation(fac[:, 1], work[0][:], ACT.Exp, scale=0.2)
            nc.scalar.activation(fac[:, 2], work[2][:], ACT.Exp, scale=0.8)
            nc.scalar.activation(fac[:, 3], work[1][:], ACT.Exp, scale=-0.8)
            act.wait_ge(turn_done, 1)
            nc.scalar.copy(rows[:], turned[:].rearrange("h t p -> h (t p)")).then_inc(rows_done, 1)

        @block.sync
        def _(sp):
            sp.wait_ge(rows_done, 1)
            sp.dma_start(arow_dram[0:H, :], rows[:]).then_inc(stored, 16)
            sp.wait_ge(stored, 16)


def heads_attend(pr, c, fac, seq_dram, arow_dram, hid_dram, H, DH, g, HG):
    nc = pr.nc
    adjT = c["adjT"]
    W = DH + 1
    CG = HG * DH
    per = 512 // (2 * W)
    banks = -(-NT // per)
    h0 = g * HG
    with pr.stage():
        R = pr.sb("R", [P, NT, PARTS, HG * 2 * W], BF16)
        T = pr.sb("T", [P, NT, HG, W])
        hid = pr.sb("hid", [P, NT, HG, DH])

        with pr.nc.sbuf_tensor(f"split0_{pr.n}", [P, HG, 2, W], F32) as r0, \
                pr.nc.sbuf_tensor(f"split1_{pr.n}", [P, HG, 2, W], F32) as r1, \
                pr.nc.sbuf_tensor(f"seq0_{pr.n}", [P, HG, DH], F32) as s0, \
                pr.nc.sbuf_tensor(f"seq1_{pr.n}", [P, HG, DH], F32) as s1:
            rest, seq = [r0, r1], [s0, s1]
            loaded = [pr.sem(f"loaded{u}") for u in range(2)]
            order, hi_done, split_done = pr.sem("order"), pr.sem("hi_done"), pr.sem("split_done")
            with nc.Block() as block:
                @block.sync
                def _(sp):
                    for u in range(2):
                        sp.dma_start(seq[u][:], seq_dram[cols(u, P), g * CG:(g + 1) * CG]
                                     .rearrange("p (h d) -> p h d", d=DH)).then_inc(loaded[u], 16)
                    with sp.Fori(1, NT // 2) as i:
                        for u in range(2):
                            sp.wait_ge(split_done, 2 * i + u + 1)
                            sp.dma_start(seq[u][:], seq_dram[cols(2 * i + u, P), g * CG:(g + 1) * CG]
                                         .rearrange("p (h d) -> p h d", d=DH)).then_inc(loaded[u], 16)

                @block.vector
                def _(dve):
                    dve.sem_inc(split_done, 2)
                    with dve.Fori(0, NT // 2) as i:
                        for u in range(2):
                            t = 2 * i + u
                            dve.wait_ge(loaded[u], 16 * i + 16)
                            dve.wait_ge(hi_done, (t + 1) * PARTS)
                            link = Link(dve, order, t * (3 + PARTS))
                            for v in range(2):
                                factor = fac[:, v, t, h0:h0 + HG].unsqueeze(2)
                                nc.vector.tensor_tensor(rest[u][:, :, v, 0:DH], seq[u][:],
                                                        factor.broadcast_to([P, HG, DH]), ALU.mult).then_inc(order, 1)
                                ins = nc.vector.tensor_copy(rest[u][:, :, v, DH:W], factor)
                                if v == 0:
                                    ins.then_inc(order, 1)
                            link.k = 3
                            link(ins)
                            for p in range(1, PARTS):
                                dve.wait_ge(hi_done, (t + 2) * PARTS + p)
                                link(nc.vector.tensor_tensor(rest[u][:].rearrange("p h v w -> p (h v w)"),
                                                             rest[u][:].rearrange("p h v w -> p (h v w)"),
                                                             R[:, t, p - 1, :], ALU.subtract))
                            dve.sem_inc(split_done, 1)

                @block.scalar
                def _(act):
                    act.sem_inc(hi_done, 2 * PARTS)
                    with act.Fori(0, NT // 2) as i:
                        for u in range(2):
                            t = 2 * i + u
                            for p in range(PARTS):
                                act.wait_ge(order, t * (3 + PARTS) + 4 + p)
                                nc.scalar.copy(R[:, t, p, :], rest[u][:].rearrange("p h v w -> p (h v w)")) \
                                    .then_inc(hi_done, 1)

        R5 = R[:].rearrange("p t s (h v w) -> p t s h v w", v=2, w=W)
        with nc.psum_tensor(f"total0_{pr.n}", [P, HG * W], F32) as t0, \
                nc.psum_tensor(f"total1_{pr.n}", [P, HG * W], F32) as t1:
            total = [t0, t1]
            total_done, T_done = pr.sem("total_done"), pr.sem("T_done")
            with nc.Block() as block:
                @block.tensor
                def _(pe):
                    with pe.Fori(0, NT // 2) as i:
                        for u in range(2):
                            t = 2 * i + u
                            pe.wait_ge(T_done, t + 1)
                            for j in range(NT):
                                for p in range(PARTS):
                                    ins = nc.tensor.matmul(total[u][:].rearrange("p (h w) -> p h w", w=W),
                                                           adjT[:, j, cols(t, P)], R5[:, j, p, :, 1, :],
                                                           start=(j + p == 0), stop=(j == NT - 1 and p == PARTS - 1))
                            ins.then_inc(total_done, 1)

                @block.scalar
                def _(act):
                    act.sem_inc(T_done, 2)
                    with act.Fori(0, NT // 2) as i:
                        for u in range(2):
                            act.wait_ge(total_done, 2 * i + u + 1)
                            nc.scalar.copy(T[:, 2 * i + u].rearrange("p h w -> p (h w)"), total[u][:]).then_inc(T_done, 1)

        NM = 4
        arow = [pr.sb(f"arow{u}", [P, N]) for u in range(2)]
        M = [pr.sb(f"M{m}", [P, N], BF16) for m in range(NM)]
        S = pr.sb("S", [P, NT, 2, W])
        q = pr.sb("q", [P, NT, W])
        den = pr.sb("den", [P, NT, 1])
        acc = [pr.ps(f"acc{k}", [P, per, 2, W]) for k in range(banks)]
        a_loaded = [pr.sem(f"a_loaded{u}") for u in range(2)]
        mask_done, mask_used = pr.sem("mask_done"), pr.sem("mask_used")
        sums_done, sums_read, mixed = pr.sem("sums_done"), pr.sem("sums_read"), pr.sem("mixed")
        order = pr.sem("order_mix")
        block = pr.block()
        hid_stored = pr.sem("hid_stored")

        @block.sync
        def _(sp):
            for u in range(2):
                sp.dma_start(arow[u][:], arow_dram[h0 + u:h0 + u + 1, :].broadcast_to([P, N])).then_inc(a_loaded[u], 16)
            with sp.Fori(1, HG // 2) as i:
                for u in range(2):
                    sp.wait_ge(mask_done, (2 * i + u - 1) * NT)
                    sp.dma_start(arow[u][:], arow_dram[bass.ds(h0 + 2 * i + u, 1), :].broadcast_to([P, N])) \
                        .then_inc(a_loaded[u], 16)
            sp.wait_ge(mixed, HG)
            sp.dma_start(hid_dram.rearrange("(t p) n -> p t n", p=P)[:, :, g * CG:(g + 1) * CG],
                         hid[:].rearrange("p t h d -> p t (h d)")).then_inc(hid_stored, 16)
            sp.wait_ge(hid_stored, 16)

        @block.vector
        def _(dve):
            with dve.Fori(0, HG // 2) as i:
                for u in range(2):
                    h = 2 * i + u
                    dve.wait_ge(a_loaded[u], 16 * i + 16)
                    for j in range(NT):
                        dve.wait_ge(mask_used, h * NT + j + 1)
                        nc.vector.scalar_tensor_tensor(out=M[j % NM][:], in0=arow[u][:],
                                                       scalar=fac[:, 4, j, bass.ds(h0 + h, 1)],
                                                       in1=adjT[:, j, :], op0=ALU.is_gt, op1=ALU.mult) \
                            .then_inc(mask_done, 1)
                    dve.wait_ge(sums_read, (h + 1) * banks)
                    link = Link(dve, order, h * 5)
                    link(nc.vector.tensor_tensor(q[:], T[:, :, bass.ds(h, 1), :].rearrange("p t h w -> p t (h w)"),
                                                 S[:, :, 1, :], ALU.subtract))
                    nc.vector.tensor_tensor(q[:], q[:], fac[:, 3, :, bass.ds(h0 + h, 1)].broadcast_to([P, NT, W]),
                                            ALU.mult).then_inc(order, 1)
                    link.k += 1
                    link(nc.vector.tensor_tensor(S[:, :, 0, :], S[:, :, 0, :],
                                                 fac[:, 2, :, bass.ds(h0 + h, 1)].broadcast_to([P, NT, W]), ALU.mult))
                    link(nc.vector.tensor_tensor(q[:], q[:], S[:, :, 0, :], ALU.add))
                    link(nc.vector.reciprocal(den[:], q[:, :, DH:W]))
                    nc.vector.tensor_tensor(hid[:, :, bass.ds(h, 1), :].rearrange("p t h d -> p t (h d)"),
                                            q[:, :, 0:DH], den[:].broadcast_to([P, NT, DH]), ALU.mult) \
                        .then_inc(mixed, 1)
                    dve.wait_ge(mixed, h + 1)

        @block.tensor
        def _(pe):
            pe.sem_inc(mask_used, NM)
            with pe.Fori(0, HG) as h:
                pe.wait_ge(sums_read, h * banks)
                for k in range(banks):
                    nc.tensor.matmul(acc[k][:].rearrange("p i v w -> p (i v w)"), c["zero16"][:, 0:P],
                                     c["zero16"][:, 0:per * 2 * W], start=True, stop=False, skip_group_check=True)
                with pe.Fori(0, NT // NM) as jq:
                    for m in range(NM):
                        j = NM * jq + m
                        pe.wait_ge(mask_done, h * NT + j + 1)
                        for t in range(NT):
                            for p in range(PARTS):
                                ins = nc.tensor.matmul(acc[t // per][:, t % per].rearrange("p v w -> p (v w)"),
                                                       M[m][:, t * P:(t + 1) * P],
                                                       R[:, bass.ds(j, 1), p, cols(h, 2 * W)].rearrange("p t w -> p (t w)"),
                                                       start=False, stop=False, skip_group_check=True)
                        ins.then_inc(mask_used, 1)
                for k in range(banks):
                    ins = nc.tensor.matmul(acc[k][:].rearrange("p i v w -> p (i v w)"), c["zero16"][:, 0:P],
                                           c["zero16"][:, 0:per * 2 * W], start=False, stop=True, skip_group_check=True)
                ins.then_inc(sums_done, 1)

        @block.scalar
        def _(act):
            with act.Fori(0, HG) as h:
                act.wait_ge(sums_done, h + 1)
                act.wait_ge(mixed, h)
                for k in range(banks):
                    n = min(per, NT - k * per)
                    nc.scalar.copy(S[:, k * per:k * per + n], acc[k][:, 0:n]).then_inc(sums_read, 1)



def tile_loads(pr, sp_loads):
    def run(eng, freed):
        for u in range(2):
            for buf, src, sem in sp_loads:
                eng.dma_start(buf[u][:], src(u)).then_inc(sem[u], 16)
        with eng.Fori(1, NT // 2) as i:
            for u in range(2):
                for s in freed:
                    eng.wait_ge(s, 2 * i + u + 1)
                for buf, src, sem in sp_loads:
                    eng.dma_start(buf[u][:], src(2 * i + u)).then_inc(sem[u], 16)
    return run


def heads_out(pr, c, hid_dram, x_dram, out_dram, w, brow):
    nc = pr.nc
    with pr.stage():
        wsb, bsb = pr.sb("w", [P, KC, D]), pr.sb("b", [P, D])
        hid, x, y, low, e = ([pr.sb(f"{n}{u}", [P, D]) for u in range(2)] for n in ("hid", "x", "y", "low", "e"))
        hT = [pr.sb(f"hT{u}", [P, KC, P]) for u in range(2)]
        turned = pr.ps("turned", [P, KC, P])
        prod = [pr.ps(f"prod{u}", [P, D]) for u in range(2)]
        w_loaded = pr.sem("w_loaded")
        hid_loaded, x_loaded, stored = ([pr.sem(f"{n}{u}") for u in range(2)] for n in ("hid_loaded", "x_loaded", "stored"))
        turn_done, hT_done, prod_done, low_done, e_done, out_done, order = (
            pr.sem(n) for n in ("turn_done", "hT_done", "prod_done", "low_done", "e_done", "out_done", "order"))
        block = pr.block()

        @block.sync
        def _(sp):
            sp.dma_start(wsb[:], w.rearrange("(k p) n -> p k n", p=P)).then_inc(w_loaded, 16)
            sp.dma_start(bsb[:], brow.broadcast_to([P, D])).then_inc(w_loaded, 16)
            tile_loads(pr, [(hid, lambda t: hid_dram[cols(t, P), :], hid_loaded),
                            (x, lambda t: x_dram[cols(t, P), :], x_loaded)])(sp, [out_done])

        @block.gpsimd
        def _(pool):
            with pool.Fori(0, NT // 2) as i:
                for u in range(2):
                    pool.wait_ge(out_done, 2 * i + u + 3)
                    pool.dma_start(out_dram[cols(2 * i + u, P), :], y[u][:]).then_inc(stored[u], 16)
            for u in range(2):
                pool.wait_ge(stored[u], 16 * (NT // 2))

        @block.tensor
        def _(pe):
            pe.sem_inc(turn_done, 2)
            pe.sem_inc(prod_done, 2)
            pe.wait_ge(w_loaded, 32)
            with pe.Fori(0, NT // 2) as i:
                for u in range(2):
                    t = 2 * i + u
                    pe.wait_ge(hid_loaded[u], 16 * i + 16)
                    pe.wait_ge(hT_done, t + 2)
                    for k in range(KC):
                        ins = nc.tensor.transpose(turned[:, k, :], hid[u][:, k * P:(k + 1) * P], c["id32"][:])
                    ins.then_inc(turn_done, 1)
                    pe.wait_ge(hT_done, t + 3)
                    pe.wait_ge(low_done, t + 1)
                    for k in range(KC):
                        ins = nc.tensor.matmul(prod[u][:], hT[u][:, k, :], wsb[:, k, :], start=(k == 0), stop=(k == KC - 1))
                    ins.then_inc(prod_done, 1)

        @block.scalar
        def _(act):
            act.sem_inc(hT_done, 2)
            act.sem_inc(e_done, 2)
            with act.Fori(0, NT // 2) as i:
                for u in range(2):
                    t = 2 * i + u
                    act.wait_ge(turn_done, t + 3)
                    act.wait_ge(prod_done, t + 1)
                    nc.scalar.copy(hT[u][:], turned[:]).then_inc(hT_done, 1)
                    act.wait_ge(low_done, t + 3)
                    nc.scalar.activation(e[u][:], low[u][:], ACT.Exp).then_inc(e_done, 1)

        @block.vector
        def _(dve):
            dve.sem_inc(low_done, 2)
            dve.sem_inc(out_done, 2)
            dve.wait_ge(w_loaded, 32)
            with dve.Fori(0, NT // 2) as i:
                for u in range(2):
                    t = 2 * i + u
                    link = Link(dve, order, t * 3)
                    dve.wait_ge(prod_done, t + 3)
                    dve.wait_ge(stored[u], 16 * i)
                    link(nc.vector.tensor_tensor(y[u][:], prod[u][:], bsb[:], ALU.add))
                    nc.vector.tensor_scalar(low[u][:], y[u][:], 0.0, None, ALU.min).then_inc(low_done, 1)
                    link(nc.vector.tensor_scalar(y[u][:], y[u][:], 0.0, None, ALU.max))
                    dve.wait_ge(e_done, t + 3)
                    link(nc.vector.scalar_tensor_tensor(out=y[u][:], in0=e[u][:], scalar=-1.0, in1=y[u][:],
                                                        op0=ALU.add, op1=ALU.add))
                    dve.wait_ge(x_loaded[u], 16 * i + 16)
                    nc.vector.tensor_tensor(y[u][:], y[u][:], x[u][:], ALU.add).then_inc(out_done, 1)


def features_keys(pr, c, x_dram, h_dram, w1, w2, w3, QW, K):
    nc = pr.nc
    with pr.stage():
        f = norm_and_turn(pr, c, x_dram)
        w1s, w3s, w2s = pr.sb("w1", [P, KC, 64]), pr.sb("w3", [P, KC, 64]), pr.sb("w2", [64, 64])
        qT = pr.sb("qT", [64, P])
        kq = pr.ps("kq", [64, 2, P])
        qw = pr.ps("qw", [64, P])
        w_loaded = pr.sem("w_loaded")
        stored = [pr.sem(f"stored{u}") for u in range(2)]
        kq_done, q_done, qw_done, copied = (pr.sem(n) for n in ("kq_done", "q_done", "qw_done", "copied"))
        block = pr.block()

        @block.sync
        def _(sp):
            sp.dma_start(w1s[:], w1.rearrange("(k p) n -> p k n", p=P)).then_inc(w_loaded, 16)
            sp.dma_start(w3s[:], w3.rearrange("(k p) n -> p k n", p=P)).then_inc(w_loaded, 16)
            sp.dma_start(w2s[:], w2).then_inc(w_loaded, 16)
            f["load"](sp)

        @block.gpsimd
        def _(pool):
            with pool.Fori(0, NT // 2) as i:
                for u in range(2):
                    pool.wait_ge(f["h_done"], 2 * i + u + 3)
                    pool.dma_start(h_dram[cols(2 * i + u, P), :], f["h"][u][:]).then_inc(stored[u], 16)
            for u in range(2):
                pool.wait_ge(stored[u], 16 * (NT // 2))

        @block.vector
        def _(dve):
            dve.sem_inc(f["h_done"], 2)
            with dve.Fori(0, NT // 2) as i:
                for u in range(2):
                    f["dve_step"](dve, i, u, [f["turn_done"]], stored)

        @block.tensor
        def _(pe):
            pe.sem_inc(f["turn_done"], 2)
            pe.sem_inc(kq_done, 2)
            pe.wait_ge(w_loaded, 48)
            with pe.Fori(0, NT // 2) as i:
                for u in range(2):
                    t = 2 * i + u
                    f["pe_turn"](pe, i, u)
                    pe.wait_ge(f["hT_done"], t + 3)
                    pe.wait_ge(copied, t)
                    for v, ws in enumerate((w3s, w1s)):
                        for k in range(KC):
                            ins = nc.tensor.matmul(kq[:, v, :], ws[:, k, :], f["hT"][u][:, k, :],
                                                   start=(k == 0), stop=(k == KC - 1))
                    ins.then_inc(kq_done, 1)
                    pe.wait_ge(q_done, t + 1)
                    pr.passed(pe)
                    nc.tensor.matmul(qw[:], w2s[:], qT[:], start=True, stop=True).then_inc(qw_done, 1)

        @block.scalar
        def _(act):
            act.sem_inc(f["hT_done"], 2)
            with act.Fori(0, NT // 2) as i:
                for u in range(2):
                    t = 2 * i + u
                    f["act_std"](act, i, u)
                    f["act_hT"](act, i, u, kq_done)
                    act.wait_ge(kq_done, t + 3)
                    nc.scalar.copy(qT[:], kq[:, 1, :]).then_inc(q_done, 1)
                    nc.scalar.copy(K[:, cols(t, P)], kq[:, 0, :])
                    act.wait_ge(qw_done, t + 1)
                    nc.scalar.copy(QW[:, cols(t, P)], qw[:]).then_inc(copied, 1)


def walk(pr, c, s, xf_dram, xf_new, z_dram, z_new, u1):
    nc = pr.nc
    adjT = c["adjT"]
    with pr.stage():
        XP = pr.sb("XP", [P, NT, PARTS, D], BF16)

        with nc.sbuf_tensor(f"rest0_{pr.n}", [P, D], F32) as r0, nc.sbuf_tensor(f"rest1_{pr.n}", [P, D], F32) as r1:
            rest = [r0, r1]
            loaded = [pr.sem(f"loaded{u}") for u in range(2)]
            order, cast_done, split_done = pr.sem("order"), pr.sem("cast_done"), pr.sem("split_done")
            with nc.Block() as block:
                @block.sync
                def _(sp):
                    tile_loads(pr, [(rest, lambda t: xf_dram[cols(t, P), :], loaded)])(sp, [split_done])

                @block.vector
                def _(dve):
                    with dve.Fori(0, NT // 2) as i:
                        for u in range(2):
                            t = 2 * i + u
                            dve.wait_ge(loaded[u], 16 * i + 16)
                            for p in range(1, PARTS):
                                dve.wait_ge(cast_done, t * (PARTS - 1) + p)
                                nc.vector.tensor_tensor(rest[u][:], rest[u][:], XP[:, t, p - 1, :], ALU.subtract) \
                                    .then_inc(order, 1)

                @block.scalar
                def _(act):
                    act.sem_inc(split_done, 2)
                    with act.Fori(0, NT // 2) as i:
                        for u in range(2):
                            t = 2 * i + u
                            act.wait_ge(loaded[u], 16 * i + 16)
                            for p in range(PARTS):
                                if p:
                                    act.wait_ge(order, t * (PARTS - 1) + p)
                                nc.scalar.copy(XP[:, t, p, :], rest[u][:]) \
                                    .then_inc(cast_done if p < PARTS - 1 else split_done, 1)

        usb = pr.sb("u1", [P, KC, D])
        xf, z, new, zo = ([pr.sb(f"{n}{u}", [P, D]) for u in range(2)] for n in ("xf", "z", "new", "zo"))
        nT = [pr.sb(f"nT{u}", [P, KC, P]) for u in range(2)]
        inv = [pr.sb(f"inv{u}", [P, 1]) for u in range(2)]
        acc = [pr.ps(f"acc{u}", [P, D]) for u in range(2)]
        deg = [pr.ps(f"deg{u}", [P, 2]) for u in range(2)]
        turned = pr.ps("turned", [P, KC, P])
        prod = pr.ps("prod", [P, D])
        u_loaded = pr.sem("u_loaded")
        xf_loaded, z_loaded, n_stored, z_stored = ([pr.sem(f"{n}{u}") for u in range(2)]
                                                   for n in ("xf_loaded", "z_loaded", "n_stored", "z_stored"))
        acc_done, new_done, turn_done, nT_done, prod_done, z_done, order = (
            pr.sem(n) for n in ("acc_done", "new_done", "turn_done", "nT_done", "prod_done", "z_done", "order_walk"))
        block = pr.block()

        @block.sync
        def _(sp):
            sp.dma_start(usb[:], u1.rearrange("(k p) n -> p k n", p=P)).then_inc(u_loaded, 16)
            tile_loads(pr, [(xf, lambda t: xf_dram[cols(t, P), :], xf_loaded),
                            (z, lambda t: z_dram[cols(t, P), :], z_loaded)])(sp, [new_done, z_done])

        @block.gpsimd
        def _(pool):
            with pool.Fori(0, NT // 2) as i:
                for u in range(2):
                    t = 2 * i + u
                    pool.wait_ge(new_done, t + 3)
                    pool.dma_start(xf_new[cols(t, P), :], new[u][:]).then_inc(n_stored[u], 16)
                    pool.wait_ge(z_done, t + 3)
                    pr.passed(pool)
                    pool.dma_start(z_new[cols(t, P), :], zo[u][:]).then_inc(z_stored[u], 16)
            for u in range(2):
                pool.wait_ge(n_stored[u], 16 * (NT // 2))
                pool.wait_ge(z_stored[u], 16 * (NT // 2))

        @block.tensor
        def _(pe):
            def product(t, u):
                pe.wait_ge(new_done, t + 1)
                for j in range(NT):
                    lhs = adjT[:, j, cols(t, P)]
                    nc.tensor.matmul(deg[u][:], lhs, c["ones16"][:], start=(j == 0), stop=(j == NT - 1))
                    for p in range(PARTS):
                        ins = nc.tensor.matmul(acc[u][:], lhs, XP[:, j, p, :], start=(j + p == 0),
                                               stop=(j == NT - 1 and p == PARTS - 1))
                ins.then_inc(acc_done, 1)

            def project(t, u):
                pe.wait_ge(new_done, t + 3)
                pe.wait_ge(nT_done, t + 2)
                for k in range(KC):
                    ins = nc.tensor.transpose(turned[:, k, :], new[u][:, k * P:(k + 1) * P], c["id32"][:])
                ins.then_inc(turn_done, 1)
                pe.wait_ge(nT_done, t + 3)
                pe.wait_ge(z_done, t + 2)
                for k in range(KC):
                    ins = nc.tensor.matmul(prod[:], nT[u][:, k, :], usb[:, k, :], start=(k == 0), stop=(k == KC - 1))
                ins.then_inc(prod_done, 1)

            pe.sem_inc(turn_done, 2)
            pe.sem_inc(prod_done, 2)
            pe.wait_ge(u_loaded, 16)
            product(0, 0)
            with pe.Fori(0, NT // 2 - 1) as i:
                for u in range(2):
                    product(2 * i + u + 1, 1 - u)
                    project(2 * i + u, u)
            product(NT - 1, 1)
            project(NT - 2, 0)
            project(NT - 1, 1)

        @block.scalar
        def _(act):
            act.sem_inc(nT_done, 2)
            with act.Fori(0, NT // 2) as i:
                for u in range(2):
                    t = 2 * i + u
                    act.wait_ge(turn_done, t + 3)
                    act.wait_ge(prod_done, t + 1)
                    nc.scalar.copy(nT[u][:], turned[:]).then_inc(nT_done, 1)

        @block.vector
        def _(dve):
            dve.sem_inc(new_done, 2)
            dve.sem_inc(z_done, 2)
            with dve.Fori(0, NT // 2) as i:
                for u in range(2):
                    t = 2 * i + u
                    link = Link(dve, order, t * 3)
                    dve.wait_ge(acc_done, t + 1)
                    link(nc.vector.tensor_scalar(inv[u][:], deg[u][:, 0:1], 1.0, 1e-12, ALU.add, ALU.max))
                    link(nc.vector.reciprocal(inv[u][:], inv[u][:]))
                    dve.wait_ge(xf_loaded[u], 16 * i + 16)
                    dve.wait_ge(n_stored[u], 16 * i)
                    dve.wait_ge(turn_done, t + 1)
                    link(nc.vector.tensor_tensor(new[u][:], acc[u][:], xf[u][:], ALU.add))
                    nc.vector.tensor_scalar(new[u][:], new[u][:], inv[u][:, 0:1], None, ALU.mult).then_inc(new_done, 1)
                    dve.wait_ge(prod_done, t + 3)
                    dve.wait_ge(z_loaded[u], 16 * i + 16)
                    dve.wait_ge(z_stored[u], 16 * i)
                    nc.vector.tensor_tensor(zo[u][:], prod[:], z[u][:], ALU.add).then_inc(z_done, 1)


P_TOP = 0.9
FIRST = 13
ALL = 24
WIDTH = 9.94


def top_attention(pr, c, last, xa_dram, xa_new, z_dram, z_new, u2, QW, K, w1, w2, w3, QWn, Kn):
    nc = pr.nc
    G = 4
    NG = NT // G
    with pr.stage():
        Xa = pr.sb("Xa", [P, NT, D])
        E = [pr.sb(f"E{u}", [P, G, N]) for u in range(2)]
        below = [pr.sb(f"below{u}", [P, N]) for u in range(2)]
        junk = [below[k // 2][:].bitcast(BF16)[:, (k % 2) * N:(k % 2 + 1) * N] for k in range(4)]
        WT = [pr.sb(f"WT{u}", [P, NT, P]) for u in range(2)]
        usb = pr.sb("u2", [P, KC, D])
        w1s, w3s, w2s = pr.sb("w1", [P, KC, 64]), pr.sb("w3", [P, KC, 64]), pr.sb("w2", [64, 64])
        qs = [pr.sb(f"qs{u}", [64, P]) for u in range(G)]
        qT = pr.sb("qT", [64, P])
        ratio = pr.sb("ratio", [P, ALL])
        mx, nmx, S, goal, lo, th, F, hit, kept, low_sum, unres, thr = (
            pr.sb(n, [P, G]) for n in ("mx", "nmx", "S", "goal", "lo", "th", "F", "hit", "kept", "low_sum", "unres", "thr"))
        inv = [pr.sb(f"inv{u}", [P, G]) for u in range(2)]
        top8, sum8a, sum8b, in8 = (pr.sb(n, [P, G, 8]) for n in ("top8", "sum8a", "sum8b", "in8"))
        flag, flagT = pr.sb("flag", [P, 32]), pr.sb("flagT", [P, 32])
        flag1, flag4 = pr.sb("flag1", [P, 1]), pr.sb("flag4", [1, 4])
        flagi = pr.sb("flagi", [1, 1], mybir.dt.int32)
        z, zo, new, ys = ([pr.sb(f"{n}{u}", [P, D]) for u in range(2)] for n in ("z", "zo", "new", "ys"))
        nT = pr.sb("nT", [P, KC, P])
        zps = pr.ps("zps", [P, N])
        tw = [pr.ps(f"tw{u}", [P, 4, P]) for u in range(2)]
        o = pr.ps("o", [P, D])
        y = pr.ps("y", [P, D])
        w_loaded, x_loaded, steps_set = pr.sem("w_loaded"), pr.sem("x_loaded"), pr.sem("steps_set")
        z_loaded, n_stored, z_stored = ([pr.sem(f"{n}{u}") for u in range(2)] for n in ("z_loaded", "n_stored", "z_stored"))
        (qs_done, logits_done, logits_kept, max_done, exp_done, masked, inv_done, order, order2, order3, turn_done, quad_done,
         pv_done, new_done, y_done, ys_done, z_done, kq_done, q_done, qw_done, copied) = (pr.sem(n) for n in (
             "qs_done", "logits_done", "logits_kept", "max_done", "exp_done", "masked", "inv_done", "order_group",
             "order_rounds", "order_rest", "turn_done", "quad_done", "pv_done", "new_done", "y_done", "ys_done", "z_done",
             "kq_done", "q_done", "qw_done", "copied"))
        QUADS = NT // 4 + 1
        block = pr.block()

        def in_groups(eng, ahead, behind):
            ahead(0, 0)
            with eng.Fori(0, NG // 2 - 1) as i:
                ahead(2 * i + 1, 1)
                behind(2 * i, 0)
                ahead(2 * i + 2, 0)
                behind(2 * i + 1, 1)
            ahead(NG - 1, 1)
            behind(NG - 2, 0)
            behind(NG - 1, 1)

        @block.sync
        def _(sp):
            sp.dma_start(w1s[:], w1.rearrange("(k p) n -> p k n", p=P)).then_inc(w_loaded, 16)
            sp.dma_start(w3s[:], w3.rearrange("(k p) n -> p k n", p=P)).then_inc(w_loaded, 16)
            sp.dma_start(w2s[:], w2).then_inc(w_loaded, 16)
            sp.dma_start(usb[:], u2.rearrange("(k p) n -> p k n", p=P)).then_inc(w_loaded, 16)
            sp.dma_start(Xa[:], xa_dram.rearrange("(t p) n -> p t n", p=P)).then_inc(x_loaded, 16)
            tile_loads(pr, [(z, lambda t: z_dram[cols(t, P), :], z_loaded)])(sp, [z_done])

        @block.gpsimd
        def _(pool):
            for k in range(ALL):
                ins = nc.gpsimd.memset(ratio[:, k:k + 1], float(np.exp(WIDTH / 2 ** (k + 1))))
            nc.gpsimd.memset(flag[:], 0.0).then_inc(steps_set, 1)
            pool.sem_inc(z_done, 2)
            with pool.Fori(0, NT // 2) as i:
                for u in range(2):
                    t = 2 * i + u
                    pool.wait_ge(new_done, t + 3)
                    pool.dma_start(xa_new[cols(t, P), :], new[u][:]).then_inc(n_stored[u], 16)
                    pool.wait_ge(ys_done, t + 3)
                    pool.wait_ge(z_loaded[u], 16 * i + 16)
                    pool.wait_ge(z_stored[u], 16 * i)
                    nc.gpsimd.tensor_tensor(zo[u][:], ys[u][:], z[u][:], ALU.add).then_inc(z_done, 1)
                    pool.wait_ge(z_done, t + 3)
                    pr.passed(pool)
                    pool.dma_start(z_new[cols(t, P), :], zo[u][:]).then_inc(z_stored[u], 16)
            for u in range(2):
                pool.wait_ge(n_stored[u], 16 * (NT // 2))
                pool.wait_ge(z_stored[u], 16 * (NT // 2))

        @block.tensor
        def _(pe):
            def logits(g, v):
                for u in range(G):
                    t = G * g + u
                    pe.wait_ge(qs_done, t + 1)
                    pe.wait_ge(logits_kept, t)
                    for n in range(4):
                        ins = nc.tensor.matmul(zps[:, n * 512:(n + 1) * 512], qs[u][:], K[:, n * 512:(n + 1) * 512],
                                               start=True, stop=True)
                    ins.then_inc(logits_done, 1)

            def values(g, v):
                for u in range(G):
                    t = G * g + u
                    pe.wait_ge(masked, t + 1)
                    for q in range(4):
                        pe.wait_ge(quad_done, t * QUADS + q + 1)
                        for k in range(4):
                            b = 4 * q + k
                            ins = nc.tensor.transpose(tw[(u * QUADS + q) % 2][:, k, :], E[v][:, u, b * P:(b + 1) * P], c["id32"][:])
                        ins.then_inc(turn_done, 1)
                    pe.wait_ge(copied, t)
                    for q in range(4):
                        pe.wait_ge(quad_done, t * QUADS + q + 3)
                        for j in range(4 * q, 4 * q + 4):
                            ins = nc.tensor.matmul(o[:], WT[u % 2][:, j, :], Xa[:, j, :], start=(j == 0), stop=(j == NT - 1))
                    ins.then_inc(pv_done, 1)
                    pe.wait_ge(new_done, t + 3)
                    for k in range(KC):
                        ins = nc.tensor.transpose(tw[(u * QUADS + 4) % 2][:, k, :], new[u % 2][:, k * P:(k + 1) * P], c["id32"][:])
                    ins.then_inc(turn_done, 1)
                    pe.wait_ge(quad_done, (t + 1) * QUADS + 2)
                    pe.wait_ge(ys_done, t + 2)
                    for k in range(KC):
                        ins = nc.tensor.matmul(y[:], nT[:, k, :], usb[:, k, :], start=(k == 0), stop=(k == KC - 1))
                    ins.then_inc(y_done, 1)
                    if not last:
                        for w, ws in enumerate((w3s, w1s)):
                            for k in range(KC):
                                ins = nc.tensor.matmul(o[0:64, w * P:(w + 1) * P], ws[:, k, :], nT[:, k, :],
                                                       start=(k == 0), stop=(k == KC - 1))
                        ins.then_inc(kq_done, 1)
                        pe.wait_ge(q_done, t + 1)
                        pr.passed(pe)
                        nc.tensor.matmul(o[0:64, 2 * P:3 * P], w2s[:], qT[:], start=True, stop=True).then_inc(qw_done, 1)

            pe.wait_ge(w_loaded, 64)
            pe.wait_ge(x_loaded, 16)
            in_groups(pe, logits, values)

        @block.scalar
        def _(act):
            def keep_logits(g, v):
                for u in range(G):
                    nc.scalar.copy(qs[u][:], QW[:, cols(G * g + u, P)]).then_inc(qs_done, 1)
                for u in range(G):
                    t = G * g + u
                    act.wait_ge(logits_done, t + 1)
                    nc.scalar.copy(E[v][:, u, :], zps[:]).then_inc(logits_kept, 1)

            def exps(g, v):
                for u in range(G):
                    t = G * g + u
                    act.wait_ge(max_done, t + 1)
                    nc.scalar.activation(E[v][:, u, :], E[v][:, u, :], ACT.Exp, bias=nmx[:, u:u + 1],
                                         accum_out=S[:, u:u + 1]).then_inc(exp_done, 1)

            def serve(g, v):
                act.wait_ge(inv_done, g + 1)
                for u in range(G):
                    t = G * g + u
                    for q in range(4):
                        act.wait_ge(turn_done, t * QUADS + q + 1)
                        nc.scalar.copy(WT[u % 2][:, 4 * q:4 * q + 4, :], tw[(u * QUADS + q) % 2][:]).then_inc(quad_done, 1)
                    act.wait_ge(pv_done, t + 1)
                    act.wait_ge(n_stored[u % 2], (2 * g + u // 2) * 16)
                    ins = nc.scalar.activation(new[u % 2][:], o[:], ACT.Copy, scale=inv[v][:, u:u + 1]).then_inc(new_done, 1)
                    act.wait_ge(turn_done, (t + 1) * QUADS)
                    nc.scalar.copy(nT[:], tw[(u * QUADS + 4) % 2][:]).then_inc(quad_done, 1)
                    act.wait_ge(y_done, t + 1)
                    act.wait_ge(z_done, t + 1)
                    nc.scalar.copy(ys[u % 2][:], y[:]).then_inc(ys_done, 1)
                    if last:
                        act.wait_ge(new_done, t + 3)
                        act.sem_inc(copied, 1)
                    else:
                        act.wait_ge(kq_done, t + 1)
                        nc.scalar.copy(Kn[:, cols(t, P)], o[0:64, 0:P])
                        nc.scalar.copy(qT[:], o[0:64, P:2 * P]).then_inc(q_done, 1)
                        act.wait_ge(qw_done, t + 1)
                        nc.scalar.copy(QWn[:, cols(t, P)], o[0:64, 2 * P:3 * P]).then_inc(copied, 1)

            act.sem_inc(quad_done, 2)
            act.sem_inc(new_done, 2)
            act.sem_inc(ys_done, 2)
            keep_logits(0, 0)
            exps(0, 0)
            with act.Fori(0, NG // 2 - 1) as i:
                keep_logits(2 * i + 1, 1)
                serve(2 * i, 0)
                exps(2 * i + 1, 1)
                keep_logits(2 * i + 2, 0)
                serve(2 * i + 1, 1)
                exps(2 * i + 2, 0)
            keep_logits(NG - 1, 1)
            serve(NG - 2, 0)
            exps(NG - 1, 1)
            serve(NG - 1, 1)

        @block.vector
        def _(dve):
            def halve(Ev, k, link):
                link(nc.vector.tensor_scalar(th[:], lo[:], ratio[:, bass.ds(k, 1)], None, ALU.mult))
                for u in range(G):
                    ins = nc.vector.scalar_tensor_tensor(out=junk[u], in0=Ev[:, u, :], scalar=th[:, u:u + 1],
                                                         in1=Ev[:, u, :], op0=ALU.is_ge, op1=ALU.mult,
                                                         accum_out=F[:, u:u + 1])
                link(ins)
                link(nc.vector.tensor_tensor(hit[:], F[:], goal[:], ALU.is_ge))
                link(nc.vector.tensor_tensor(hit[:], hit[:], th[:], ALU.mult))
                link(nc.vector.tensor_tensor(lo[:], lo[:], hit[:], ALU.max))

            def single_out(Ev, halvings, link):
                link(nc.vector.tensor_scalar(th[:], lo[:], float(np.exp(WIDTH / 2 ** halvings)) * (1 + 1e-6), None, ALU.mult))
                for u in range(G):
                    link(nc.vector.scalar_tensor_tensor(out=below[u % 2][:], in0=Ev[:, u, :], scalar=th[:, u:u + 1],
                                                        in1=Ev[:, u, :], op0=ALU.is_lt, op1=ALU.mult,
                                                        accum_out=low_sum[:, u:u + 1]))
                    pr.passed(dve)
                    link(nc.vector.max(top8[:, u, :], below[u % 2][:]))
                link(nc.vector.tensor_copy(sum8a[:, :, 0:1], top8[:, :, 0:1]))
                link(nc.vector.tensor_tensor(sum8a[:, :, 1:8], top8[:, :, 1:8], top8[:, :, 0:7], ALU.add))
                link(nc.vector.tensor_copy(sum8b[:, :, 0:2], sum8a[:, :, 0:2]))
                link(nc.vector.tensor_tensor(sum8b[:, :, 2:8], sum8a[:, :, 2:8], sum8a[:, :, 0:6], ALU.add))
                link(nc.vector.tensor_copy(sum8a[:, :, 0:4], sum8b[:, :, 0:4]))
                link(nc.vector.tensor_tensor(sum8a[:, :, 4:8], sum8b[:, :, 4:8], sum8b[:, :, 0:4], ALU.add))
                link(nc.vector.tensor_tensor(F[:], goal[:], S[:], ALU.subtract))
                link(nc.vector.tensor_tensor(F[:], F[:], low_sum[:], ALU.add))
                link(nc.vector.tensor_tensor(in8[:], sum8a[:], F[:].unsqueeze(2).broadcast_to([P, G, 8]), ALU.is_lt))
                link(nc.vector.tensor_copy(unres[:].unsqueeze(2), in8[:, :, 7:8]))
                link(nc.vector.tensor_scalar(in8[:, :, 0:7], in8[:, :, 0:7], -4.0, 4.0, ALU.mult, ALU.add))
                link(nc.vector.tensor_tensor(sum8b[:, :, 1:8], in8[:, :, 0:7], top8[:, :, 1:8], ALU.max))
                link(nc.vector.tensor_copy(sum8b[:, :, 0:1], top8[:, :, 0:1]))
                link(nc.vector.tensor_reduce(thr[:], sum8b[:], AX.X, ALU.min))

            HALVE, SINGLE = 5, 23
            BODY = G + 2 + SINGLE + 8 + 1

            def search(g, v):
                Ev = E[v]
                link = Link(dve, order, g * BODY)
                for u in range(G):
                    t = G * g + u
                    dve.wait_ge(logits_kept, t + 1)
                    link(nc.vector.tensor_reduce(mx[:, u:u + 1], Ev[:, u, :], AX.X, ALU.max))
                    nc.vector.tensor_scalar(nmx[:, u:u + 1], mx[:, u:u + 1], -1.0, None, ALU.mult).then_inc(max_done, 1)
                dve.wait_ge(exp_done, G * (g + 1))
                link(nc.vector.memset(lo[:], float(np.exp(-WIDTH))))
                link(nc.vector.tensor_scalar(goal[:], S[:], P_TOP, None, ALU.mult))
                pr.passed(dve)
                with dve.Fori(0, FIRST) as k:
                    inner = Link(dve, order2, (g * FIRST + k) * HALVE)
                    halve(Ev, k, inner)
                    assert inner.k == HALVE
                n = link.k
                single_out(Ev, FIRST, link)
                assert link.k - n == SINGLE, link.k - n
                link(nc.vector.tensor_reduce(flag[:, 0:1], unres[:], AX.X, ALU.max))
                link(nc.vector.transpose(flagT[:], flag[:]))
                link(nc.vector.tensor_reduce(flag1[:], flagT[:], AX.X, ALU.max))
                for q in range(4):
                    link(nc.vector.tensor_copy(flag4[0:1, q:q + 1], flag1[32 * q:32 * q + 1, :]))
                link(nc.vector.tensor_reduce(flagi[:], flag4[:], AX.X, ALU.max))
                pr.passed(dve)
                with dve.If(dve.value_load(flagi[0:1, 0:1], min_val=0, max_val=1) > 0):
                    with dve.Fori(FIRST, ALL) as k:
                        inner = Link(dve, order3, (k - FIRST) * HALVE)
                        halve(Ev, k, inner)
                    inner = Link(dve, order3, (ALL - FIRST) * HALVE)
                    single_out(Ev, ALL, inner)
                    inner(nc.vector.tensor_tensor(hit[:], lo[:], thr[:], ALU.subtract))
                    inner(nc.vector.tensor_tensor(hit[:], hit[:], unres[:], ALU.mult))
                    inner(nc.vector.tensor_tensor(thr[:], thr[:], hit[:], ALU.add))
                    dve.sem_clear(order3)
                for u in range(G):
                    ins = nc.vector.scalar_tensor_tensor(out=Ev[:, u, :], in0=Ev[:, u, :], scalar=thr[:, u:u + 1],
                                                         in1=Ev[:, u, :], op0=ALU.is_ge, op1=ALU.mult,
                                                         accum_out=kept[:, u:u + 1]).then_inc(masked, 1)
                dve.wait_ge(masked, G * (g + 1))
                nc.vector.reciprocal(inv[v][:], kept[:]).then_inc(inv_done, 1)
                dve.wait_ge(inv_done, g + 1)
                link.k += 1
                dve.sem_inc(order, 1)
                assert link.k == BODY, (link.k, BODY)

            dve.wait_ge(steps_set, 1)
            with dve.Fori(0, NG // 2) as i:
                search(2 * i, 0)
                search(2 * i + 1, 1)


def norm_add(pr, c, z_dram, x_dram, out_dram, gamma, beta):
    nc = pr.nc
    with pr.stage():
        rows = pr.sb("rows", [P, 2, D])
        z, x, y = ([pr.sb(f"{n}{u}", [P, D]) for u in range(2)] for n in ("z", "x", "y"))
        stats = [pr.sb(f"stats{u}", [P, 6]) for u in range(2)]
        mv = [pr.sb(f"mv{u}", [P, 2]) for u in range(2)]
        std, rstd = ([pr.sb(f"{n}{u}", [P, 1]) for u in range(2)] for n in ("std", "rstd"))
        z_loaded, x_loaded, stored = ([pr.sem(f"{n}{u}") for u in range(2)] for n in ("z_loaded", "x_loaded", "stored"))
        r_loaded, mv_done, std_done, out_done, order = (
            pr.sem(n) for n in ("r_loaded", "mv_done", "std_done", "out_done", "order"))
        block = pr.block()

        @block.sync
        def _(sp):
            sp.dma_start(rows[:, 0, :], gamma.broadcast_to([P, D])).then_inc(r_loaded, 16)
            sp.dma_start(rows[:, 1, :], beta.broadcast_to([P, D])).then_inc(r_loaded, 16)
            tile_loads(pr, [(z, lambda t: z_dram[cols(t, P), :], z_loaded),
                            (x, lambda t: x_dram[cols(t, P), :], x_loaded)])(sp, [out_done])

        @block.gpsimd
        def _(pool):
            with pool.Fori(0, NT // 2) as i:
                for u in range(2):
                    pool.wait_ge(out_done, 2 * i + u + 3)
                    pool.dma_start(out_dram[cols(2 * i + u, P), :], y[u][:]).then_inc(stored[u], 16)
            for u in range(2):
                pool.wait_ge(stored[u], 16 * (NT // 2))

        @block.scalar
        def _(act):
            with act.Fori(0, NT // 2) as i:
                for u in range(2):
                    act.wait_ge(mv_done, 2 * i + u + 1)
                    nc.scalar.activation(std[u][:], mv[u][:, 1:2], ACT.Sqrt, bias=c["eps"][:, 0:1]).then_inc(std_done, 1)

        @block.vector
        def _(dve):
            dve.sem_inc(out_done, 2)
            dve.wait_ge(r_loaded, 32)
            with dve.Fori(0, NT // 2) as i:
                for u in range(2):
                    t = 2 * i + u
                    link = Link(dve, order, t * 5)
                    dve.wait_ge(z_loaded[u], 16 * i + 16)
                    link(nc.vector.bn_stats(stats[u][:], z[u][:]))
                    pr.passed(dve)
                    nc.vector.bn_aggr(mv[u][:], stats[u][:]).then_inc(mv_done, 1)
                    dve.wait_ge(mv_done, t + 1)
                    dve.wait_ge(std_done, t + 1)
                    link(nc.vector.reciprocal(rstd[u][:], std[u][:]))
                    dve.wait_ge(stored[u], 16 * i)
                    link(nc.vector.tensor_scalar(y[u][:], z[u][:], mv[u][:, 0:1], rstd[u][:, 0:1], ALU.subtract, ALU.mult))
                    link(nc.vector.tensor_tensor(y[u][:], y[u][:], rows[:, 0, :], ALU.mult))
                    link(nc.vector.tensor_tensor(y[u][:], y[u][:], rows[:, 1, :], ALU.add))
                    dve.wait_ge(x_loaded[u], 16 * i + 16)
                    nc.vector.tensor_tensor(y[u][:], y[u][:], x[u][:], ALU.add).then_inc(out_done, 1)


def heads_mlp(pr, c, hid_dram, x_dram, out_dram, w1, w2, w3, w4, b1, b2, b3, b4):
    nc = pr.nc
    with pr.stage():
        w1s, w2s, w3s, w4s = (pr.sb("w1", [P, KC, 256]), pr.sb("w2", [P, 2, 128]), pr.sb("w3", [P, 256]),
                              pr.sb("w4", [P, 2, D]))
        b1s, b2s, b3s, b4s = pr.sb("b1", [P, 2]), pr.sb("b2", [P, 1]), pr.sb("b3", [P, 2]), pr.sb("b4", [P, D])
        hid, x, low, e, y = ([pr.sb(f"{n}{u}", [P, D]) for u in range(2)] for n in ("hid", "x", "low", "e", "y"))
        hT = pr.sb("hT", [P, KC, P])
        o1s, o2s, o3s = pr.sb("o1s", [P, 2, P]), pr.sb("o2s", [P, P]), pr.sb("o3s", [P, 2, P])
        turned, o1, o2, o3, o4 = (pr.ps("turned", [P, KC, P]), pr.ps("o1", [P, 2, P]), pr.ps("o2", [P, P]),
                                  pr.ps("o3", [P, 2, P]), pr.ps("o4", [P, D]))
        w_loaded = pr.sem("w_loaded")
        hid_loaded, x_loaded, stored = ([pr.sem(f"{n}{u}") for u in range(2)] for n in ("hid_loaded", "x_loaded", "stored"))
        low_done, e_done, elu_done, turn_done, hT_done, out_done, order = (
            pr.sem(n) for n in ("low_done", "e_done", "elu_done", "turn_done", "hT_done", "out_done", "order"))
        l_done = [pr.sem(f"l{k}_done") for k in range(1, 5)]
        r_done = [pr.sem(f"r{k}_done") for k in range(1, 4)]
        block = pr.block()

        @block.sync
        def _(sp):
            for dst, src in ((w1s, w1.rearrange("(k p) n -> p k n", p=P)), (w2s, w2.rearrange("(k p) n -> p k n", p=P)),
                             (w3s, w3), (w4s, w4.rearrange("(k p) n -> p k n", p=P)), (b1s, b1), (b2s, b2), (b3s, b3),
                             (b4s, b4.broadcast_to([P, D]))):
                sp.dma_start(dst[:], src).then_inc(w_loaded, 16)
            tile_loads(pr, [(hid, lambda t: hid_dram[cols(t, P), :], hid_loaded),
                            (x, lambda t: x_dram[cols(t, P), :], x_loaded)])(sp, [out_done])

        @block.gpsimd
        def _(pool):
            with pool.Fori(0, NT // 2) as i:
                for u in range(2):
                    pool.wait_ge(out_done, 2 * i + u + 3)
                    pool.dma_start(out_dram[cols(2 * i + u, P), :], y[u][:]).then_inc(stored[u], 16)
            for u in range(2):
                pool.wait_ge(stored[u], 16 * (NT // 2))

        @block.tensor
        def _(pe):
            pe.wait_ge(w_loaded, 128)
            with pe.Fori(0, NT // 2) as i:
                for u in range(2):
                    t = 2 * i + u
                    pe.wait_ge(elu_done, t + 1)
                    pe.wait_ge(hT_done, t)
                    for k in range(KC):
                        ins = nc.tensor.transpose(turned[:, k, :], hid[u][:, k * P:(k + 1) * P], c["id32"][:])
                    ins.then_inc(turn_done, 1)
                    pe.wait_ge(hT_done, t + 1)
                    for m in range(2):
                        for k in range(KC):
                            ins = nc.tensor.matmul(o1[:, m, :], w1s[:, k, m * P:(m + 1) * P], hT[:, k, :],
                                                   start=(k == 0), stop=(k == KC - 1))
                    ins.then_inc(l_done[0], 1)
                    pe.wait_ge(r_done[0], t + 1)
                    for k in range(2):
                        ins = nc.tensor.matmul(o2[:], w2s[:, k, :], o1s[:, k, :], start=(k == 0), stop=(k == 1))
                    ins.then_inc(l_done[1], 1)
                    pe.wait_ge(r_done[1], t + 1)
                    for m in range(2):
                        ins = nc.tensor.matmul(o3[:, m, :], w3s[:, m * P:(m + 1) * P], o2s[:], start=True, stop=True)
                    ins.then_inc(l_done[2], 1)
                    pe.wait_ge(r_done[2], t + 1)
                    pe.wait_ge(out_done, t + 2)
                    for k in range(2):
                        ins = nc.tensor.matmul(o4[:], o3s[:, k, :], w4s[:, k, :], start=(k == 0), stop=(k == 1))
                    ins.then_inc(l_done[3], 1)

        @block.scalar
        def _(act):
            act.wait_ge(w_loaded, 128)
            with act.Fori(0, NT // 2) as i:
                for u in range(2):
                    t = 2 * i + u
                    act.wait_ge(low_done, t + 1)
                    nc.scalar.activation(e[u][:], low[u][:], ACT.Exp).then_inc(e_done, 1)
                    act.wait_ge(turn_done, t + 1)
                    nc.scalar.copy(hT[:], turned[:]).then_inc(hT_done, 1)
                    act.wait_ge(l_done[0], t + 1)
                    for m in range(2):
                        ins = nc.scalar.activation(o1s[:, m, :], o1[:, m, :], ACT.Relu, bias=b1s[:, m:m + 1])
                    ins.then_inc(r_done[0], 1)
                    act.wait_ge(l_done[1], t + 1)
                    nc.scalar.activation(o2s[:], o2[:], ACT.Relu, bias=b2s[:, 0:1]).then_inc(r_done[1], 1)
                    act.wait_ge(l_done[2], t + 1)
                    for m in range(2):
                        ins = nc.scalar.activation(o3s[:, m, :], o3[:, m, :], ACT.Relu, bias=b3s[:, m:m + 1])
                    ins.then_inc(r_done[2], 1)

        @block.vector
        def _(dve):
            dve.sem_inc(out_done, 2)
            dve.wait_ge(w_loaded, 128)
            with dve.Fori(0, NT // 2) as i:
                for u in range(2):
                    t = 2 * i + u
                    link = Link(dve, order, t * 2)
                    dve.wait_ge(hid_loaded[u], 16 * i + 16)
                    nc.vector.tensor_scalar(low[u][:], hid[u][:], 0.0, None, ALU.min).then_inc(low_done, 1)
                    dve.wait_ge(e_done, t + 1)
                    link(nc.vector.tensor_scalar(hid[u][:], hid[u][:], 0.0, None, ALU.max))
                    nc.vector.scalar_tensor_tensor(out=hid[u][:], in0=e[u][:], scalar=-1.0, in1=hid[u][:],
                                                   op0=ALU.add, op1=ALU.add).then_inc(elu_done, 1)
                    dve.wait_ge(l_done[3], t + 1)
                    dve.wait_ge(stored[u], 16 * i)
                    link(nc.vector.tensor_tensor(y[u][:], o4[:], b4s[:], ALU.add))
                    dve.wait_ge(x_loaded[u], 16 * i + 16)
                    nc.vector.tensor_tensor(y[u][:], y[u][:], x[u][:], ALU.add).then_inc(out_done, 1)


def project_qkv(pr, c, x_dram, wq, wk, wv, bq, bk, bv, q_dram, kT, V):
    nc = pr.nc
    with pr.stage():
        f = norm_and_turn(pr, c, x_dram)
        w = [pr.sb(f"w{n}", [P, KC, D]) for n in "qkv"]
        bqs, bks, bvs = pr.sb("bq", [P, KC]), pr.sb("bk", [P, KC]), pr.sb("bv", [P, D])
        qT = [pr.sb(f"qT{u}", [P, KC, P]) for u in range(2)]
        qp, kp, vp = pr.ps("qp", [P, KC, P]), pr.ps("kp", [P, KC, P]), pr.ps("vp", [P, D])
        w_loaded = pr.sem("w_loaded")
        stored = [pr.sem(f"stored{u}") for u in range(2)]
        q_done, k_done, v_done, q_out, k_out, v_out = (pr.sem(n) for n in ("q_done", "k_done", "v_done", "q_out", "k_out", "v_out"))
        block = pr.block()

        @block.sync
        def _(sp):
            for dst, src in zip(w, (wq, wk, wv)):
                sp.dma_start(dst[:], src.rearrange("(k p) n -> p k n", p=P)).then_inc(w_loaded, 16)
            sp.dma_start(bqs[:], bq).then_inc(w_loaded, 16)
            sp.dma_start(bks[:], bk).then_inc(w_loaded, 16)
            sp.dma_start(bvs[:], bv.broadcast_to([P, D])).then_inc(w_loaded, 16)
            f["load"](sp)

        @block.gpsimd
        def _(pool):
            with pool.Fori(0, NT // 2) as i:
                for u in range(2):
                    t = 2 * i + u
                    pool.wait_ge(q_out, t + 1)
                    pool.dma_start(q_dram[cols(t, P), :], qT[u][:].rearrange("p k n -> p (k n)")).then_inc(stored[u], 16)
            for u in range(2):
                pool.wait_ge(stored[u], 16 * (NT // 2))

        @block.vector
        def _(dve):
            dve.sem_inc(f["h_done"], 2)
            dve.wait_ge(w_loaded, 96)
            with dve.Fori(0, NT // 2) as i:
                for u in range(2):
                    t = 2 * i + u
                    f["dve_step"](dve, i, u, [f["turn_done"]])
                    dve.wait_ge(v_done, t + 3)
                    nc.vector.tensor_tensor(V[:, t, :], vp[:], bvs[:], ALU.add).then_inc(v_out, 1)

        @block.tensor
        def _(pe):
            pe.sem_inc(f["turn_done"], 2)
            pe.sem_inc(v_done, 2)
            pe.wait_ge(w_loaded, 96)
            with pe.Fori(0, NT // 2) as i:
                for u in range(2):
                    t = 2 * i + u
                    f["pe_turn"](pe, i, u)
                    pe.wait_ge(f["hT_done"], t + 3)
                    for ws, dst, done, out in ((w[0], qp, q_done, q_out), (w[1], kp, k_done, k_out)):
                        pe.wait_ge(out, t)
                        for m in range(KC):
                            for k in range(KC):
                                ins = nc.tensor.matmul(dst[:, m, :], ws[:, k, m * P:(m + 1) * P], f["hT"][u][:, k, :],
                                                       start=(k == 0), stop=(k == KC - 1))
                        ins.then_inc(done, 1)
                    pe.wait_ge(v_out, t)
                    for k in range(KC):
                        ins = nc.tensor.matmul(vp[:], f["hT"][u][:, k, :], w[2][:, k, :], start=(k == 0), stop=(k == KC - 1))
                    ins.then_inc(v_done, 1)

        @block.scalar
        def _(act):
            act.sem_inc(f["hT_done"], 2)
            act.wait_ge(w_loaded, 96)
            with act.Fori(0, NT // 2) as i:
                for u in range(2):
                    t = 2 * i + u
                    f["act_std"](act, i, u)
                    f["act_hT"](act, i, u, v_done)
                    act.wait_ge(q_done, t + 1)
                    act.wait_ge(stored[u], 16 * i)
                    for m in range(KC):
                        ins = nc.scalar.activation(qT[u][:, m, :], qp[:, m, :], ACT.Identity, bias=bqs[:, m:m + 1])
                    ins.then_inc(q_out, 1)
                    act.wait_ge(k_done, t + 1)
                    for m in range(KC):
                        ins = nc.scalar.activation(kT[:, m, cols(t, P)], kp[:, m, :], ACT.Identity, bias=bks[:, m:m + 1])
                    ins.then_inc(k_out, 1)


def masked_attention(pr, c, q_dram, kT, V, adj, x_dram, out_dram):
    nc = pr.nc
    SCALE = float(D) ** -0.5
    with pr.stage():
        qT = [pr.sb(f"qT{u}", [P, KC, P]) for u in range(2)]
        a = [pr.sb(f"a{u}", [P, N]) for u in range(2)]
        z, zero, e = pr.sb("z", [P, N]), pr.sb("zero", [P, N]), [pr.sb(f"e{u}", [P, N]) for u in range(2)]
        eT = pr.sb("eT", [P, NT, P])
        x, y = ([pr.sb(f"{n}{u}", [P, D]) for u in range(2)] for n in ("x", "y"))
        mx, nmx, S, inv = ([pr.sb(f"{n}{u}", [P, 1]) for u in range(2)] for n in ("mx", "nmx", "S", "inv"))
        zps = pr.ps("zps", [P, N])
        tw = [pr.ps(f"tw{u}", [P, 4, P]) for u in range(2)]
        o = pr.ps("o", [P, D])
        q_loaded, a_loaded, x_loaded, stored = ([pr.sem(f"{n}{u}") for u in range(2)]
                                                for n in ("q_loaded", "a_loaded", "x_loaded", "stored"))
        z_done, z_read, max_done, exp_done, turn_done, quad_done, pv_done, out_done, order = (
            pr.sem(n) for n in ("z_done", "z_read", "max_done", "exp_done", "turn_done", "quad_done", "pv_done",
                                "out_done", "order"))
        block = pr.block()

        @block.sync
        def _(sp):
            tile_loads(pr, [(qT, lambda t: q_dram[cols(t, P), :].rearrange("p (k n) -> p k n", n=P), q_loaded),
                            (a, lambda t: adj[cols(t, P), :], a_loaded),
                            (x, lambda t: x_dram[cols(t, P), :], x_loaded)])(sp, [z_done, out_done])

        @block.gpsimd
        def _(pool):
            with pool.Fori(0, NT // 2) as i:
                for u in range(2):
                    pool.wait_ge(out_done, 2 * i + u + 3)
                    pool.dma_start(out_dram[cols(2 * i + u, P), :], y[u][:]).then_inc(stored[u], 16)
            for u in range(2):
                pool.wait_ge(stored[u], 16 * (NT // 2))

        @block.tensor
        def _(pe):
            def logits(i, u):
                t = 2 * i + u
                pe.wait_ge(q_loaded[u], 16 * i + 16)
                pe.wait_ge(z_read, t)
                for n in range(4):
                    for k in range(KC):
                        ins = nc.tensor.matmul(zps[:, n * 512:(n + 1) * 512], qT[u][:, k, :], kT[:, k, n * 512:(n + 1) * 512],
                                               start=(k == 0), stop=(k == KC - 1))
                ins.then_inc(z_done, 1)

            def values(i, u):
                t = 2 * i + u
                pe.wait_ge(exp_done, t + 3)
                for q in range(4):
                    pe.wait_ge(quad_done, 4 * t + q + 1)
                    for k in range(4):
                        b = 4 * q + k
                        ins = nc.tensor.transpose(tw[q % 2][:, k, :], e[u][:, b * P:(b + 1) * P], c["id32"][:])
                    ins.then_inc(turn_done, 1)
                pe.wait_ge(out_done, t + 2)
                for q in range(4):
                    pe.wait_ge(quad_done, 4 * t + q + 3)
                    for j in range(4 * q, 4 * q + 4):
                        ins = nc.tensor.matmul(o[:], eT[:, j, :], V[:, j, :], start=(j == 0), stop=(j == NT - 1))
                ins.then_inc(pv_done, 1)

            pe.sem_inc(z_done, 2)
            pe.sem_inc(pv_done, 2)
            logits(0, 0)
            with pe.Fori(0, NT // 2 - 1) as i:
                logits(i, 1)
                values(i, 0)
                logits(i + 1, 0)
                values(i, 1)
            logits(NT // 2 - 1, 1)
            values(NT // 2 - 1, 0)
            values(NT // 2 - 1, 1)

        @block.scalar
        def _(act):
            def exps(i, u):
                t = 2 * i + u
                act.wait_ge(max_done, t + 1)
                act.wait_ge(pv_done, t + 1)
                act.wait_ge(out_done, t + 1)
                nc.scalar.activation(e[u][:], z[:], ACT.Exp, bias=nmx[u][:, 0:1], accum_out=S[u][:, 0:1]).then_inc(exp_done, 1)

            def copies(i, u):
                t = 2 * i + u
                act.wait_ge(pv_done, t + 2)
                for q in range(4):
                    act.wait_ge(turn_done, 4 * t + q + 1)
                    nc.scalar.copy(eT[:, 4 * q:4 * q + 4, :], tw[q % 2][:]).then_inc(quad_done, 1)

            act.sem_inc(exp_done, 2)
            act.sem_inc(quad_done, 2)
            exps(0, 0)
            with act.Fori(0, NT // 2 - 1) as i:
                copies(i, 0)
                exps(i, 1)
                copies(i, 1)
                exps(i + 1, 0)
            copies(NT // 2 - 1, 0)
            exps(NT // 2 - 1, 1)
            copies(NT // 2 - 1, 1)

        @block.vector
        def _(dve):
            def scores(i, u):
                t = 2 * i + u
                link = Link(dve, order, t * 5)
                dve.wait_ge(z_done, t + 3)
                dve.wait_ge(a_loaded[u], 16 * i + 16)
                dve.wait_ge(exp_done, t + 2)
                nc.vector.scalar_tensor_tensor(out=z[:], in0=zps[:], scalar=SCALE, in1=a[u][:], op0=ALU.mult,
                                               op1=ALU.mult).then_inc(z_read, 1)
                dve.wait_ge(z_read, t + 1)
                link(nc.vector.tensor_scalar(zero[:], z[:], 0.0, -10000.0, ALU.is_equal, ALU.mult))
                link(nc.vector.tensor_tensor(z[:], z[:], zero[:], ALU.add))
                link(nc.vector.tensor_reduce(mx[u][:], z[:], AX.X, ALU.max))
                nc.vector.tensor_scalar(nmx[u][:], mx[u][:], -1.0, None, ALU.mult).then_inc(max_done, 1)

            def result(i, u):
                t = 2 * i + u
                link = Link(dve, order, t * 5 + 3)
                dve.wait_ge(pv_done, t + 3)
                link(nc.vector.reciprocal(inv[u][:], S[u][:]))
                dve.wait_ge(stored[u], 16 * i)
                link(nc.vector.tensor_scalar(y[u][:], o[:], inv[u][:, 0:1], 0.0, ALU.mult, ALU.max))
                dve.wait_ge(x_loaded[u], 16 * i + 16)
                nc.vector.tensor_tensor(y[u][:], y[u][:], x[u][:], ALU.add).then_inc(out_done, 1)

            dve.sem_inc(out_done, 2)
            with dve.Fori(0, NT // 2) as i:
                for u in range(2):
                    scores(i, u)
                    result(i, u)


def layout(inputs):
    a = {k: np.asarray(v) for k, v in inputs.items()}
    ins = {"x": a["x"], "adj": a["adj"]}
    ins["w0"] = a["L0_gnn_W_seq"]
    ins["a01"] = np.tile(a["L0_gnn_a1"], 16).reshape(1, D)
    ins["a02"] = np.tile(a["L0_gnn_a2"], 16).reshape(1, D)
    ins["w0o"] = a["L0_gnn_W_out"]
    ins["b0o"] = a["L0_gnn_b_out"].reshape(1, D)
    for n in ("W1", "W2", "W3", "U1_0", "U1_1", "U2_0", "U2_1"):
        ins[f"l1_{n}"] = a[f"L1_gnn_{n}"]
    ins["gamma"] = a["L1_gnn_gamma"].reshape(1, D)
    ins["beta"] = a["L1_gnn_beta"].reshape(1, D)
    ins["w2h"] = np.transpose(a["L2_gnn_W"], (1, 0, 2)).reshape(D, D)
    ins["a21"] = a["L2_gnn_a1"].reshape(1, D)
    ins["a22"] = a["L2_gnn_a2"].reshape(1, D)
    for n in ("W1", "W2", "W3", "W4"):
        ins[f"l2_{n}"] = a[f"L2_gnn_{n}"].T
    for n in ("b1", "b2", "b3"):
        ins[f"l2_{n}"] = a[f"L2_gnn_{n}"].reshape(-1, P).T
    ins["l2_b4"] = a["L2_gnn_b4"].reshape(1, D)
    for n in "qkv":
        ins[f"l3_W{n}"] = a[f"L3_gnn_W_{n}"].T
    for n in "qk":
        ins[f"l3_b{n}"] = a[f"L3_gnn_b_{n}"].reshape(KC, P).T
    ins["l3_bv"] = a["L3_gnn_b_v"].reshape(1, D)
    return {k: np.ascontiguousarray(v) for k, v in ins.items()}


def build(nc, ins, out, stop=99):
    pr = Program(nc)
    root = ExitStack()
    with root:
        def sb(name, shape, dt=F32):
            return root.enter_context(nc.sbuf_tensor(name, shape, dt))

        def dram(name, shape=(N, D), dt=F32):
            return nc.dram_tensor(name, list(shape), dt, kind="Internal").ap()
        c = dict(id32=sb("id32", [P, P]), id16=sb("id16", [P, P], BF16), ones16=sb("ones16", [P, 2], BF16),
                 zero16=sb("zero16", [P, 512], BF16), eps=sb("eps", [P, 1]))
        adjT_dram = dram("adjT_dram", [N, N], BF16)
        seq_dram, hid_dram = dram("seq_dram"), dram("hid_dram")
        arow_dram = dram("arow_dram", [16, N])
        x1, x2, x3 = dram("x1"), dram("x2"), dram("x3")
        h_dram, xf1, xf2, xa1, xa2 = (dram(n) for n in ("h_dram", "xf1", "xf2", "xa1", "xa2"))
        z1, z2, z3, z4 = (dram(n) for n in ("z1", "z2", "z3", "z4"))
        q_dram = dram("q_dram")
        constants(pr, c)

        def heads_layer(x, w, a1, a2, H, DH, groups):
            with nc.sbuf_tensor(f"scores_{pr.n}", [P, 2, NT, H], F32) as scores, \
                    nc.sbuf_tensor(f"fac_{pr.n}", [P, 5, NT, H], F32) as fac:
                heads_project(pr, c, x, w, a1, a2, seq_dram, scores, H, DH)
                heads_factors(pr, c, scores, fac, arow_dram, H)
                for g in range(groups):
                    heads_attend(pr, c, fac, seq_dram, arow_dram, hid_dram, H, DH, g, H // groups)

        with nc.sbuf_tensor("adjT", [P, NT, N], BF16) as adjT:
            c["adjT"] = adjT
            transpose_adjacency(pr, c, ins["adj"], adjT_dram)
            heads_layer(ins["x"], ins["w0"], ins["a01"], ins["a02"], 16, 32, 2)
            heads_out(pr, c, hid_dram, ins["x"], x1, ins["w0o"], ins["b0o"])
            if stop == 0:
                return
            w = [ins[f"l1_{n}"] for n in ("W1", "W2", "W3")]
            with nc.sbuf_tensor("keys", [64, 2, N], F32) as ks:
                features_keys(pr, c, x1, h_dram, *w, ks[:, 0], ks[:, 1])
            walk(pr, c, 0, h_dram, xf1, h_dram, z1, ins["l1_U1_0"])
            walk(pr, c, 1, xf1, xf2, z1, z2, ins["l1_U1_1"])
            if stop == 1:
                return
        with nc.sbuf_tensor("keys2", [64, 4, N], F32) as ks:
            features_keys(pr, c, x1, h_dram, *w, ks[:, 0], ks[:, 1])
            top_attention(pr, c, False, h_dram, xa1, z2, z3, ins["l1_U2_0"], ks[:, 0], ks[:, 1], *w, ks[:, 2], ks[:, 3])
            top_attention(pr, c, True, xa1, xa2, z3, z4, ins["l1_U2_1"], ks[:, 2], ks[:, 3], *w, None, None)
        norm_add(pr, c, z4, x1, x2, ins["gamma"], ins["beta"])
        if stop == 2:
            return
        with nc.sbuf_tensor("adjT2", [P, NT, N], BF16) as adjT:
            c["adjT"] = adjT
            reload_adjacency(pr, c, adjT_dram)
            heads_layer(x2, ins["w2h"], ins["a21"], ins["a22"], 8, 64, 2)
        heads_mlp(pr, c, hid_dram, x2, x3, *(ins[f"l2_{n}"] for n in ("W1", "W2", "W3", "W4", "b1", "b2", "b3", "b4")))
        if stop == 3:
            return
        with nc.sbuf_tensor("kT", [P, KC, N], F32) as kT, nc.sbuf_tensor("V", [P, NT, D], F32) as V:
            project_qkv(pr, c, x3, *(ins[f"l3_W{n}"] for n in "qkv"), *(ins[f"l3_b{n}"] for n in "qkv"), q_dram, kT, V)
            masked_attention(pr, c, q_dram, kT, V, ins["adj"], x3, out)


def kernel(**inputs):
    import concourse.bacc as bacc
    from concourse.bass_utils import run_bass_kernel_spmd

    nc = bacc.Bacc("TRN2", target_bir_lowering=False, num_devices=1)
    arrays = {f"in_{k}": v for k, v in layout(inputs).items()}
    ins = {k[3:]: nc.dram_tensor(k, v.shape, mybir.dt.from_np(v.dtype), kind="ExternalInput").ap()
           for k, v in arrays.items()}
    out = nc.dram_tensor("out_0", (N, D), F32, kind="ExternalOutput").ap()
    build(nc, ins, out)
    r = run_bass_kernel_spmd(nc, [arrays], core_ids=[0])
    return r.results[0]["out_0"]
```

```python
from contextlib import ExitStack

import numpy as np

import concourse.bass as bass
from concourse import mybir

F32 = mybir.dt.float32
BF16 = mybir.dt.bfloat16
ALU = mybir.AluOpType
ACT = mybir.ActivationFunctionType
AX = mybir.AxisListType

N = 2048
D = 512
P = 128
NT = N // P
KC = D // P
PARTS = 3
EPS = 1e-5


class Link:

    def __init__(self, eng, sem, base=0):
        self.eng, self.sem, self.base, self.k = eng, sem, base, 0

    def __call__(self, ins):
        self.k += 1
        ins.then_inc(self.sem, 1)
        self.eng.wait_ge(self.sem, self.base + self.k)


def one_ahead(eng, ahead, behind):
    ahead(0, 0)
    with eng.Fori(0, NT // 2 - 1) as i:
        ahead(i, 1)
        behind(i, 0)
        ahead(i + 1, 0)
        behind(i, 1)
    ahead(NT // 2 - 1, 1)
    behind(NT // 2 - 1, 0)
    behind(NT // 2 - 1, 1)


def cols(t, width):
    return bass.ds(t * width, width)


class Program:

    def __init__(self, nc):
        self.nc = nc
        self.n = 0
        self.ticks = nc.alloc_semaphore("ticks")

    def stage(self):
        self.ctx = ExitStack()
        self.n += 1
        sems = self.sems = []

        def free():
            for s in sems:
                self.nc.gpsimd.sem_clear(s)
                self.nc.release_semaphore(s)
        self.ctx.callback(free)
        return self.ctx

    def sb(self, name, shape, dt=F32):
        return self.ctx.enter_context(self.nc.sbuf_tensor(f"{name}_{self.n}", shape, dt))

    def ps(self, name, shape, dt=F32):
        return self.ctx.enter_context(self.nc.psum_tensor(f"{name}_{self.n}", shape, dt))

    def sem(self, name):
        sem = self.nc.alloc_semaphore(f"{name}_{self.n}")
        if not name.rstrip("01").endswith("stored"):
            self.sems.append(sem)
        return sem

    def passed(self, eng):
        eng.sem_inc(self.ticks, 1)

    def block(self):
        return self.ctx.enter_context(self.nc.Block())


def constants(pr, c):
    nc = pr.nc
    with pr.stage():
        filled = pr.sem("filled")
        block = pr.block()

        @block.gpsimd
        def _(pool):
            nc.gpsimd.memset(c["id32"][:], 0.0).then_inc(filled, 1)
            nc.gpsimd.memset(c["id16"][:], 0.0).then_inc(filled, 1)
            nc.gpsimd.memset(c["ones16"][:], 1.0)
            nc.gpsimd.memset(c["zero16"][:], 0.0)
            nc.gpsimd.memset(c["eps"][:], EPS)
            pool.wait_ge(filled, 2)
            for m in (c["id32"], c["id16"]):
                nc.gpsimd.affine_select(out=m[:], in_=m[:], compare_op=ALU.not_equal, fill=1.0, base=0,
                                        pattern=[[-1, P]], channel_multiplier=1)


def transpose_adjacency(pr, c, adj, adjT_dram):
    nc = pr.nc
    adjT = c["adjT"]
    with pr.stage():
        raw = [pr.sb(f"raw{u}", [P, N]) for u in range(2)]
        cast = [pr.sb(f"cast{u}", [P, N], BF16) for u in range(2)]
        turned = [pr.ps(f"turned{u}", [P, NT, P], BF16) for u in range(2)]
        loaded = [pr.sem(f"loaded{u}") for u in range(2)]
        cast_done = pr.sem("cast_done")
        turn_done = pr.sem("turn_done")
        kept = pr.sem("kept")
        stored = pr.sem("stored")
        block = pr.block()

        @block.sync
        def _(sp):
            for u in range(2):
                sp.dma_start(raw[u][:], adj[cols(u, P), :]).then_inc(loaded[u], 16)
            with sp.Fori(1, NT // 2) as i:
                for u in range(2):
                    sp.wait_ge(cast_done, 2 * i + u + 1)
                    sp.dma_start(raw[u][:], adj[cols(2 * i + u, P), :]).then_inc(loaded[u], 16)
            sp.wait_ge(kept, NT + 2)
            sp.dma_start(adjT_dram.rearrange("(t p) n -> p t n", p=P), adjT[:]).then_inc(stored, 16)
            sp.wait_ge(stored, 16)

        @block.vector
        def _(dve):
            dve.sem_inc(cast_done, 2)
            with dve.Fori(0, NT // 2) as i:
                for u in range(2):
                    dve.wait_ge(loaded[u], 16 * i + 16)
                    dve.wait_ge(turn_done, 2 * i + u + 1)
                    nc.vector.tensor_copy(cast[u][:], raw[u][:]).then_inc(cast_done, 1)

        @block.tensor
        def _(pe):
            pe.sem_inc(turn_done, 2)
            with pe.Fori(0, NT // 2) as i:
                for u in range(2):
                    pe.wait_ge(cast_done, 2 * i + u + 3)
                    pe.wait_ge(kept, 2 * i + u + 1)
                    for j in range(NT):
                        ins = nc.tensor.transpose(turned[u][:, j, :], cast[u][:, j * P:(j + 1) * P], c["id16"][:])
                    ins.then_inc(turn_done, 1)

        @block.scalar
        def _(act):
            act.sem_inc(kept, 2)
            with act.Fori(0, NT // 2) as i:
                for u in range(2):
                    act.wait_ge(turn_done, 2 * i + u + 3)
                    nc.scalar.copy(adjT[:, :, cols(2 * i + u, P)], turned[u][:]).then_inc(kept, 1)


def reload_adjacency(pr, c, adjT_dram):
    with pr.stage():
        loaded = pr.sem("loaded")
        block = pr.block()

        @block.sync
        def _(sp):
            sp.dma_start(c["adjT"][:], adjT_dram.rearrange("(t p) n -> p t n", p=P)).then_inc(loaded, 16)
            sp.wait_ge(loaded, 16)


def carry(pr, dst, src):
    with pr.stage():
        carried = pr.sem("carried_stored")
        block = pr.block()

        @block.sync
        def _(sp):
            sp.dma_start(dst, src).then_inc(carried, 16)
            sp.wait_ge(carried, 16)


def norm_and_turn(pr, c, x_dram, h_dram=None):
    nc = pr.nc
    f = {}
    x = [pr.sb(f"x{u}", [P, D]) for u in range(2)]
    h = [pr.sb(f"h{u}", [P, D]) for u in range(2)]
    hT = [pr.sb(f"hT{u}", [P, KC, P]) for u in range(2)]
    stats = [pr.sb(f"stats{u}", [P, 6]) for u in range(2)]
    mv = [pr.sb(f"mv{u}", [P, 2]) for u in range(2)]
    std = [pr.sb(f"std{u}", [P, 1]) for u in range(2)]
    rstd = [pr.sb(f"rstd{u}", [P, 1]) for u in range(2)]
    turned = pr.ps("hturned", [P, KC, P])
    x_loaded = [pr.sem(f"x_loaded{u}") for u in range(2)]
    mv_done, std_done, h_done = pr.sem("mv_done"), pr.sem("std_done"), pr.sem("h_done")
    turn_done, hT_done = pr.sem("turn_done"), pr.sem("hT_done")
    order = pr.sem("order")

    def load(sp):
        for u in range(2):
            sp.dma_start(x[u][:], x_dram[cols(u, P), :]).then_inc(x_loaded[u], 16)
        with sp.Fori(1, NT // 2) as i:
            for u in range(2):
                sp.wait_ge(h_done, 2 * i + u + 1)
                sp.dma_start(x[u][:], x_dram[cols(2 * i + u, P), :]).then_inc(x_loaded[u], 16)

    def dve_step(dve, i, u, h_used, h_stored=None):
        link = Link(dve, order, (2 * i + u) * 4)
        dve.wait_ge(x_loaded[u], 16 * i + 16)
        link(nc.vector.bn_stats(stats[u][:], x[u][:]))
        pr.passed(dve)
        nc.vector.bn_aggr(mv[u][:], stats[u][:]).then_inc(mv_done, 1)
        dve.wait_ge(mv_done, 2 * i + u + 1)
        dve.wait_ge(std_done, 2 * i + u + 1)
        link(nc.vector.reciprocal(rstd[u][:], std[u][:]))
        for s in h_used:
            dve.wait_ge(s, 2 * i + u + 1)
        if h_stored:
            dve.wait_ge(h_stored[u], 16 * i)
        link(nc.vector.tensor_scalar(h[u][:], x[u][:], mv[u][:, 0:1], rstd[u][:, 0:1], ALU.subtract, ALU.mult))
        link(nc.vector.tensor_scalar(h[u][:], h[u][:], 0.0, None, ALU.max))
        dve.sem_inc(h_done, 1)

    def act_std(act, i, u):
        act.wait_ge(mv_done, 2 * i + u + 1)
        nc.scalar.activation(std[u][:], mv[u][:, 1:2], ACT.Sqrt, bias=c["eps"][:, 0:1]).then_inc(std_done, 1)

    def pe_turn(pe, i, u):
        pe.wait_ge(h_done, 2 * i + u + 3)
        pe.wait_ge(hT_done, 2 * i + u + 2)
        for k in range(KC):
            ins = nc.tensor.transpose(turned[:, k, :], h[u][:, k * P:(k + 1) * P], c["id32"][:])
        ins.then_inc(turn_done, 1)

    def act_hT(act, i, u, hT_used):
        act.wait_ge(turn_done, 2 * i + u + 3)
        act.wait_ge(hT_used, 2 * i + u + 1)
        nc.scalar.copy(hT[u][:], turned[:]).then_inc(hT_done, 1)

    f.update(x=x, h=h, hT=hT, h_done=h_done, turn_done=turn_done, hT_done=hT_done, std_done=std_done,
             load=load, dve_step=dve_step, act_std=act_std, pe_turn=pe_turn, act_hT=act_hT)
    return f


def heads_project(pr, c, x_dram, w, a1, a2, seq_dram, scores, H, DH):
    nc = pr.nc
    with pr.stage():
        f = norm_and_turn(pr, c, x_dram)
        wsb = pr.sb("w", [P, KC, D])
        arow = pr.sb("arow", [P, 2, D])
        seq = [pr.sb(f"seq{u}", [P, D]) for u in range(2)]
        prod = [pr.sb(f"prod{v}", [P, H, DH]) for v in range(2)]
        proj = [pr.ps(f"proj{u}", [P, D]) for u in range(2)]
        w_loaded, a_loaded = pr.sem("w_loaded"), pr.sem("a_loaded")
        proj_done, seq_done, scored = pr.sem("proj_done"), pr.sem("seq_done"), pr.sem("scored")
        stored = [pr.sem(f"stored{u}") for u in range(2)]
        order = pr.sem("order_scores")
        block = pr.block()

        @block.sync
        def _(sp):
            sp.dma_start(wsb[:], w.rearrange("(k p) n -> p k n", p=P)).then_inc(w_loaded, 16)
            for v, a in enumerate((a1, a2)):
                sp.dma_start(arow[:, v, :], a.broadcast_to([P, D])).then_inc(a_loaded, 16)
            f["load"](sp)

        @block.gpsimd
        def _(pool):
            with pool.Fori(0, NT // 2) as i:
                for u in range(2):
                    pool.wait_ge(seq_done, 2 * i + u + 3)
                    pool.dma_start(seq_dram[cols(2 * i + u, P), :], seq[u][:]).then_inc(stored[u], 16)
            for u in range(2):
                pool.wait_ge(stored[u], 16 * (NT // 2))

        @block.vector
        def _(dve):
            dve.sem_inc(f["h_done"], 2)
            dve.sem_inc(scored, 2)
            dve.wait_ge(a_loaded, 32)

            def score(i, u):
                t = 2 * i + u
                dve.wait_ge(seq_done, t + 3)
                link = Link(dve, order, t * 3)
                for v in range(2):
                    ins = nc.vector.tensor_tensor(prod[v][:].rearrange("p h d -> p (h d)"), seq[u][:],
                                                  arow[:, v, :], ALU.mult)
                    if v == 0:
                        ins.then_inc(order, 1)
                        link.k += 1
                    else:
                        link(ins)
                nc.vector.tensor_reduce(scores[:, 0, t, :], prod[0][:], AX.X, ALU.add)
                link(nc.vector.tensor_reduce(scores[:, 1, t, :], prod[1][:], AX.X, ALU.add))
                dve.sem_inc(scored, 1)

            one_ahead(dve, lambda i, u: f["dve_step"](dve, i, u, [f["turn_done"]]), score)

        @block.tensor
        def _(pe):
            pe.sem_inc(f["turn_done"], 2)
            pe.sem_inc(proj_done, 2)
            pe.wait_ge(w_loaded, 16)

            def project(i, u):
                t = 2 * i + u
                pe.wait_ge(f["hT_done"], t + 3)
                pe.wait_ge(seq_done, t + 1)
                for k in range(KC):
                    ins = nc.tensor.matmul(proj[u][:], f["hT"][u][:, k, :], wsb[:, k, :],
                                           start=(k == 0), stop=(k == KC - 1))
                ins.then_inc(proj_done, 1)

            one_ahead(pe, lambda i, u: f["pe_turn"](pe, i, u), project)

        @block.scalar
        def _(act):
            act.sem_inc(f["hT_done"], 2)
            act.sem_inc(seq_done, 2)

            def front(i, u):
                f["act_std"](act, i, u)
                f["act_hT"](act, i, u, proj_done)

            def copy_out(i, u):
                t = 2 * i + u
                act.wait_ge(proj_done, t + 3)
                act.wait_ge(scored, t + 1)
                act.wait_ge(stored[u], 16 * i)
                nc.scalar.copy(seq[u][:], proj[u][:]).then_inc(seq_done, 1)

            one_ahead(act, front, copy_out)


STEEP = 2.0 ** 60


def heads_factors(pr, c, scores, fac, arow_dram, H):
    nc = pr.nc
    with pr.stage():
        top = pr.sb("top", [P, H])
        top_all = pr.sb("top_all", [P, H])
        work = [pr.sb(f"work{v}", [P, NT, H]) for v in range(3)]
        rows = pr.sb("rows", [H, N])
        turned = pr.ps("turned", [H, NT, P])
        order, top_done, all_done = pr.sem("order"), pr.sem("top_done"), pr.sem("all_done")
        turn_done, rows_done, stored = pr.sem("turn_done"), pr.sem("rows_done"), pr.sem("stored")
        a, b = scores[:, 0], scores[:, 1]
        wide = top_all[:].unsqueeze(1).broadcast_to([P, NT, H])
        block = pr.block()

        @block.vector
        def _(dve):
            link = Link(dve, order)
            nc.vector.tensor_reduce(top[:], b.rearrange("p t h -> p h t"), AX.X, ALU.max).then_inc(top_done, 1)
            nc.vector.tensor_scalar(fac[:, 4], b, -1.0, None, ALU.mult)
            nc.vector.tensor_scalar(fac[:, 5], b, STEEP, None, ALU.mult)
            dve.wait_ge(all_done, 1)
            nc.vector.tensor_tensor(work[0][:], b, wide, ALU.subtract).then_inc(order, 1)
            link.k += 1
            link(nc.vector.tensor_tensor(work[1][:], a, wide, ALU.add))
            link(nc.vector.tensor_scalar(work[2][:], work[1][:], 0.0, None, ALU.min))
            link(nc.vector.tensor_scalar(work[1][:], work[1][:], 0.0, None, ALU.max))

        @block.gpsimd
        def _(pool):
            pool.wait_ge(top_done, 1)
            nc.gpsimd.partition_all_reduce(top_all[:], top[:], P, bass.bass_isa.ReduceOp.max).then_inc(all_done, 1)

        @block.tensor
        def _(pe):
            for t in range(NT):
                ins = nc.tensor.transpose(turned[:, t, :], scores[:, 0, t, :], c["id32"][:])
            ins.then_inc(turn_done, 1)

        @block.scalar
        def _(act):
            act.wait_ge(order, 4)
            nc.scalar.activation(fac[:, 0], work[0][:], ACT.Exp)
            nc.scalar.activation(fac[:, 1], work[0][:], ACT.Exp, scale=0.2)
            nc.scalar.activation(fac[:, 2], work[2][:], ACT.Exp, scale=0.8)
            nc.scalar.activation(fac[:, 3], work[1][:], ACT.Exp, scale=-0.8)
            act.wait_ge(turn_done, 1)
            nc.scalar.copy(rows[:], turned[:].rearrange("h t p -> h (t p)")).then_inc(rows_done, 1)

        @block.sync
        def _(sp):
            sp.wait_ge(rows_done, 1)
            sp.dma_start(arow_dram[0:H, :], rows[:]).then_inc(stored, 16)
            sp.wait_ge(stored, 16)


def heads_attend(pr, c, fac, seq_dram, arow_dram, hid_dram, H, DH, g, HG):
    nc = pr.nc
    adjT = c["adjT"]
    W = DH + 1
    CG = HG * DH
    per = 512 // (2 * W)
    banks = -(-NT // per)
    h0 = g * HG
    with pr.stage():
        R = pr.sb("R", [P, NT, PARTS, HG * 2 * W], BF16)
        T = pr.sb("T", [P, NT, HG, W])

        with ExitStack() as split:
            rest = [split.enter_context(nc.sbuf_tensor(f"split{b}_{pr.n}", [P, HG, 2, W], F32)) for b in range(4)]
            seq = [split.enter_context(nc.sbuf_tensor(f"seq{b}_{pr.n}", [P, HG, DH], F32)) for b in range(4)]
            loaded, rest_done, hi_done = ([pr.sem(f"{n}{b}") for b in range(4)] for n in ("loaded", "rest_done", "hi_done"))
            STEPS = 1 + PARTS
            with nc.Block() as block:
                @block.sync
                def _(sp):
                    def load(i, b):
                        sp.dma_start(seq[b][:], seq_dram[cols(4 * i + b, P), g * CG:(g + 1) * CG]
                                     .rearrange("p (h d) -> p h d", d=DH)).then_inc(loaded[b], 16)

                    for b in range(4):
                        load(0, b)
                    with sp.Fori(1, NT // 4) as i:
                        for b in range(4):
                            sp.wait_ge(rest_done[b], (i - 1) * STEPS + 2)
                            load(i, b)

                @block.vector
                def _(dve):
                    with dve.Fori(0, NT // 4) as i:
                        for pair in ((0, 1), (2, 3)):
                            for b in pair:
                                t = 4 * i + b
                                dve.wait_ge(loaded[b], 16 * i + 16)
                                dve.wait_ge(hi_done[b], i * PARTS)
                                factor = fac[:, 0:2, t, h0:h0 + HG].rearrange("p v h -> p h v").unsqueeze(3)
                                nc.vector.tensor_tensor(rest[b][:, :, :, 0:DH],
                                                        seq[b][:].unsqueeze(2).broadcast_to([P, HG, 2, DH]),
                                                        factor.broadcast_to([P, HG, 2, DH]), ALU.mult).then_inc(rest_done[b], 1)
                                nc.vector.tensor_copy(rest[b][:, :, :, DH:W], factor).then_inc(rest_done[b], 1)
                            for p in range(1, PARTS):
                                for b in pair:
                                    dve.wait_ge(hi_done[b], i * PARTS + p)
                                    nc.vector.tensor_tensor(rest[b][:].rearrange("p h v w -> p (h v w)"),
                                                            rest[b][:].rearrange("p h v w -> p (h v w)"),
                                                            R[:, 4 * i + b, p - 1, :], ALU.subtract).then_inc(rest_done[b], 1)

                @block.scalar
                def _(act):
                    with act.Fori(0, NT // 4) as i:
                        for pair in ((0, 1), (2, 3)):
                            for p in range(PARTS):
                                for b in pair:
                                    act.wait_ge(rest_done[b], i * STEPS + 2 + p)
                                    nc.scalar.copy(R[:, 4 * i + b, p, :], rest[b][:].rearrange("p h v w -> p (h v w)")) \
                                        .then_inc(hi_done[b], 1)

        R5 = R[:].rearrange("p t s (h v w) -> p t s h v w", v=2, w=W)
        with nc.psum_tensor(f"total0_{pr.n}", [P, HG * W], F32) as t0, \
                nc.psum_tensor(f"total1_{pr.n}", [P, HG * W], F32) as t1:
            total = [t0, t1]
            total_done, T_done = pr.sem("total_done"), pr.sem("T_done")
            with nc.Block() as block:
                @block.tensor
                def _(pe):
                    with pe.Fori(0, NT // 2) as i:
                        for u in range(2):
                            t = 2 * i + u
                            pe.wait_ge(T_done, t + 1)
                            for j in range(NT):
                                for p in range(PARTS):
                                    ins = nc.tensor.matmul(total[u][:].rearrange("p (h w) -> p h w", w=W),
                                                           adjT[:, j, cols(t, P)], R5[:, j, p, :, 1, :],
                                                           start=(j + p == 0), stop=(j == NT - 1 and p == PARTS - 1))
                            ins.then_inc(total_done, 1)

                @block.scalar
                def _(act):
                    act.sem_inc(T_done, 2)
                    with act.Fori(0, NT // 2) as i:
                        for u in range(2):
                            act.wait_ge(total_done, 2 * i + u + 1)
                            nc.scalar.copy(T[:, 2 * i + u].rearrange("p h w -> p (h w)"), total[u][:]).then_inc(T_done, 1)

        NM = 8
        BY_ACT = [j for j in range(NT) if j % 4 != 3]
        LEAD = 4
        arow = [pr.sb(f"arow{u}", [P, N]) for u in range(2)]
        M = [pr.sb(f"M{m}", [P, N], BF16) for m in range(NM)]
        S = pr.sb("S", [P, NT, 2, W])
        q = pr.sb("q", [P, NT, W])
        den = pr.sb("den", [P, NT, 1])
        acc = [pr.ps(f"acc{k}", [P, per, 2, W]) for k in range(banks)]
        a_loaded = [pr.sem(f"a_loaded{u}") for u in range(2)]
        raw_done, mask_done, mask_used = pr.sem("raw_done"), pr.sem("mask_done"), pr.sem("mask_used")
        sums_done, sums_read, mixed = pr.sem("sums_done"), pr.sem("sums_read"), pr.sem("mixed")
        order = pr.sem("order_mix")
        block = pr.block()
        hid_stored = pr.sem("hid_stored")

        def in_heads(eng, start, rest, end):
            start(0, 0)
            with eng.Fori(0, HG // 2 - 1) as i:
                rest(2 * i, 0)
                start(2 * i + 1, 1)
                end(2 * i)
                rest(2 * i + 1, 1)
                start(2 * i + 2, 0)
                end(2 * i + 1)
            rest(HG - 2, 0)
            start(HG - 1, 1)
            end(HG - 2)
            rest(HG - 1, 1)
            end(HG - 1)

        def loads_of(h, u):
            return 8 * h + 16 - 8 * u

        @block.sync
        def _(sp):
            for u in range(2):
                sp.dma_start(arow[u][:], arow_dram[h0 + u:h0 + u + 1, :].broadcast_to([P, N])).then_inc(a_loaded[u], 16)

            def store(h):
                sp.wait_ge(mixed, h + 1)
                sp.dma_start(hid_dram.rearrange("(t p) n -> p t n", p=P)[:, :, cols(h + h0, DH)],
                             T[:, :, bass.ds(h, 1), 0:DH].rearrange("p t h w -> p t (h w)")).then_inc(hid_stored, 16)

            with sp.Fori(0, HG // 2 - 1) as i:
                for u in range(2):
                    h = 2 * i + u
                    sp.wait_ge(mask_done, (h + 1) * NT)
                    sp.dma_start(arow[u][:], arow_dram[bass.ds(h + h0 + 2, 1), :].broadcast_to([P, N])) \
                        .then_inc(a_loaded[u], 16)
                    store(h)
            store(HG - 2)
            store(HG - 1)
            sp.wait_ge(hid_stored, 16 * HG)

        @block.vector
        def _(dve):
            def masks(h, u, js):
                for j in js:
                    if j in BY_ACT:
                        dve.wait_ge(raw_done, h * len(BY_ACT) + BY_ACT.index(j) + 1)
                        ins = nc.vector.tensor_tensor(M[j % NM][:], M[j % NM][:], adjT[:, j, :], ALU.min)
                    else:
                        dve.wait_ge(mask_used, h * NT + j + 1)
                        ins = nc.vector.scalar_tensor_tensor(out=M[j % NM][:], in0=arow[u][:],
                                                             scalar=fac[:, 4, j, bass.ds(h0 + h, 1)],
                                                             in1=adjT[:, j, :], op0=ALU.is_gt, op1=ALU.mult)
                    ins.then_inc(mask_done, 1)

            def start(h, u):
                dve.wait_ge(a_loaded[u], loads_of(h, u))
                masks(h, u, range(LEAD))

            def rest(h, u):
                masks(h, u, range(LEAD, NT))

            def mix(h):
                dve.wait_ge(sums_read, (h + 2) * banks)
                link = Link(dve, order, h * 5)
                Th = T[:, :, bass.ds(h, 1), :].rearrange("p t h w -> p t (h w)")
                link(nc.vector.tensor_tensor(q[:], Th, S[:, :, 1, :], ALU.subtract))
                nc.vector.tensor_tensor(q[:], q[:], fac[:, 3, :, bass.ds(h0 + h, 1)].broadcast_to([P, NT, W]),
                                        ALU.mult).then_inc(order, 1)
                link.k += 1
                link(nc.vector.tensor_tensor(S[:, :, 0, :], S[:, :, 0, :],
                                             fac[:, 2, :, bass.ds(h0 + h, 1)].broadcast_to([P, NT, W]), ALU.mult))
                link(nc.vector.tensor_tensor(q[:], q[:], S[:, :, 0, :], ALU.add))
                link(nc.vector.reciprocal(den[:], q[:, :, DH:W]))
                nc.vector.tensor_tensor(Th[:, :, 0:DH], q[:, :, 0:DH], den[:].broadcast_to([P, NT, DH]), ALU.mult) \
                    .then_inc(mixed, 1)
                dve.wait_ge(mixed, h + 1)

            in_heads(dve, start, rest, mix)

        @block.tensor
        def _(pe):
            pe.sem_inc(mask_used, NM)
            with pe.Fori(0, HG) as h:
                for k in range(banks):
                    pe.wait_ge(sums_read, h * banks + k + 1)
                    nc.tensor.matmul(acc[k][:].rearrange("p i v w -> p (i v w)"), c["zero16"][:, 0:P],
                                     c["zero16"][:, 0:per * 2 * W], start=True, stop=False, skip_group_check=True)
                with pe.Fori(0, NT // NM) as jq:
                    for m in range(NM):
                        j = NM * jq + m
                        pe.wait_ge(mask_done, h * NT + j + 1)
                        for t in range(NT):
                            for p in range(PARTS):
                                ins = nc.tensor.matmul(acc[t // per][:, t % per].rearrange("p v w -> p (v w)"),
                                                       M[m][:, t * P:(t + 1) * P],
                                                       R[:, bass.ds(j, 1), p, cols(h, 2 * W)].rearrange("p t w -> p (t w)"),
                                                       start=False, stop=False, skip_group_check=True)
                        ins.then_inc(mask_used, 1)
                for k in range(banks):
                    nc.tensor.matmul(acc[k][:].rearrange("p i v w -> p (i v w)"), c["zero16"][:, 0:P],
                                     c["zero16"][:, 0:per * 2 * W], start=False, stop=True,
                                     skip_group_check=True).then_inc(sums_done, 1)

        @block.scalar
        def _(act):
            def raw(h, u, js):
                for j in js:
                    if j in BY_ACT:
                        act.wait_ge(mask_used, h * NT + j + 1)
                        nc.scalar.activation(M[j % NM][:], arow[u][:], ACT.Relu,
                                             bias=fac[:, 5, j, bass.ds(h0 + h, 1)], scale=STEEP).then_inc(raw_done, 1)

            def start(h, u):
                act.wait_ge(a_loaded[u], loads_of(h, u))
                raw(h, u, range(LEAD))

            def rest(h, u):
                raw(h, u, range(LEAD, NT))

            def copy_sums(h):
                act.wait_ge(mixed, h)
                for k in range(banks):
                    n = min(per, NT - k * per)
                    act.wait_ge(sums_done, h * banks + k + 1)
                    nc.scalar.copy(S[:, k * per:k * per + n], acc[k][:, 0:n]).then_inc(sums_read, 1)

            act.sem_inc(sums_read, banks)
            in_heads(act, start, rest, copy_sums)


def tile_loads(pr, sp_loads):
    def run(eng, freed):
        for u in range(2):
            for buf, src, sem in sp_loads:
                eng.dma_start(buf[u][:], src(u)).then_inc(sem[u], 16)
        with eng.Fori(1, NT // 2) as i:
            for u in range(2):
                for s in freed:
                    eng.wait_ge(s, 2 * i + u + 1)
                for buf, src, sem in sp_loads:
                    eng.dma_start(buf[u][:], src(2 * i + u)).then_inc(sem[u], 16)
    return run


def heads_out(pr, c, hid_dram, x_dram, out_dram, w, brow):
    nc = pr.nc
    with pr.stage():
        wsb, bsb = pr.sb("w", [P, KC, D]), pr.sb("b", [P, D])
        hid, x, y, low, e = ([pr.sb(f"{n}{u}", [P, D]) for u in range(2)] for n in ("hid", "x", "y", "low", "e"))
        hT = [pr.sb(f"hT{u}", [P, KC, P]) for u in range(2)]
        turned = pr.ps("turned", [P, KC, P])
        prod = [pr.ps(f"prod{u}", [P, D]) for u in range(2)]
        w_loaded = pr.sem("w_loaded")
        hid_loaded, x_loaded, stored = ([pr.sem(f"{n}{u}") for u in range(2)] for n in ("hid_loaded", "x_loaded", "stored"))
        turn_done, hT_done, prod_done, low_done, e_done, out_done, order, order2 = (
            pr.sem(n) for n in ("turn_done", "hT_done", "prod_done", "low_done", "e_done", "out_done", "order", "order_sum"))
        block = pr.block()

        @block.sync
        def _(sp):
            sp.dma_start(wsb[:], w.rearrange("(k p) n -> p k n", p=P)).then_inc(w_loaded, 16)
            sp.dma_start(bsb[:], brow.broadcast_to([P, D])).then_inc(w_loaded, 16)
            tile_loads(pr, [(hid, lambda t: hid_dram[cols(t, P), :], hid_loaded),
                            (x, lambda t: x_dram[cols(t, P), :], x_loaded)])(sp, [out_done])

        @block.gpsimd
        def _(pool):
            with pool.Fori(0, NT // 2) as i:
                for u in range(2):
                    pool.wait_ge(out_done, 2 * i + u + 3)
                    pool.dma_start(out_dram[cols(2 * i + u, P), :], y[u][:]).then_inc(stored[u], 16)
            for u in range(2):
                pool.wait_ge(stored[u], 16 * (NT // 2))

        @block.tensor
        def _(pe):
            pe.sem_inc(turn_done, 2)
            pe.sem_inc(prod_done, 2)
            pe.wait_ge(w_loaded, 32)

            def turn(i, u):
                pe.wait_ge(hid_loaded[u], 16 * i + 16)
                pe.wait_ge(hT_done, 2 * i + u + 2)
                for k in range(KC):
                    ins = nc.tensor.transpose(turned[:, k, :], hid[u][:, k * P:(k + 1) * P], c["id32"][:])
                ins.then_inc(turn_done, 1)

            def product(i, u):
                t = 2 * i + u
                pe.wait_ge(hT_done, t + 3)
                pe.wait_ge(low_done, t + 1)
                for k in range(KC):
                    ins = nc.tensor.matmul(prod[u][:], hT[u][:, k, :], wsb[:, k, :], start=(k == 0), stop=(k == KC - 1))
                ins.then_inc(prod_done, 1)

            one_ahead(pe, turn, product)

        @block.scalar
        def _(act):
            act.sem_inc(hT_done, 2)
            act.sem_inc(e_done, 2)

            def copy_out(i, u):
                act.wait_ge(turn_done, 2 * i + u + 3)
                act.wait_ge(prod_done, 2 * i + u + 1)
                nc.scalar.copy(hT[u][:], turned[:]).then_inc(hT_done, 1)

            def exps(i, u):
                act.wait_ge(low_done, 2 * i + u + 3)
                act.wait_ge(out_done, 2 * i + u + 1)
                nc.scalar.activation(e[u][:], low[u][:], ACT.Exp).then_inc(e_done, 1)

            one_ahead(act, copy_out, exps)

        @block.vector
        def _(dve):
            dve.sem_inc(low_done, 2)
            dve.sem_inc(out_done, 2)
            dve.wait_ge(w_loaded, 32)

            def parts(i, u):
                t = 2 * i + u
                link = Link(dve, order, t * 2)
                dve.wait_ge(prod_done, t + 3)
                dve.wait_ge(stored[u], 16 * i)
                dve.wait_ge(e_done, t + 1)
                link(nc.vector.tensor_tensor(y[u][:], prod[u][:], bsb[:], ALU.add))
                nc.vector.tensor_scalar(low[u][:], y[u][:], 0.0, None, ALU.min).then_inc(low_done, 1)
                link(nc.vector.tensor_scalar(y[u][:], y[u][:], 0.0, None, ALU.max))

            def result(i, u):
                t = 2 * i + u
                link = Link(dve, order2, t)
                dve.wait_ge(e_done, t + 3)
                link(nc.vector.scalar_tensor_tensor(out=y[u][:], in0=e[u][:], scalar=-1.0, in1=y[u][:],
                                                    op0=ALU.add, op1=ALU.add))
                dve.wait_ge(x_loaded[u], 16 * i + 16)
                nc.vector.tensor_tensor(y[u][:], y[u][:], x[u][:], ALU.add).then_inc(out_done, 1)

            with dve.Fori(0, NT // 2) as i:
                for u in range(2):
                    parts(i, u)
                    result(i, u)


def features_keys(pr, c, x_dram, h_dram, w1, w2, w3, QW, K):
    nc = pr.nc
    with pr.stage():
        f = norm_and_turn(pr, c, x_dram)
        w1s, w3s, w2s = pr.sb("w1", [P, KC, 64]), pr.sb("w3", [P, KC, 64]), pr.sb("w2", [64, 64])
        qT = pr.sb("qT", [64, P])
        kq = pr.ps("kq", [64, 2, P])
        qw = pr.ps("qw", [64, P])
        w_loaded = pr.sem("w_loaded")
        stored = [pr.sem(f"stored{u}") for u in range(2)]
        kq_done, q_done, qw_done, copied = (pr.sem(n) for n in ("kq_done", "q_done", "qw_done", "copied"))
        block = pr.block()

        @block.sync
        def _(sp):
            sp.dma_start(w1s[:], w1.rearrange("(k p) n -> p k n", p=P)).then_inc(w_loaded, 16)
            sp.dma_start(w3s[:], w3.rearrange("(k p) n -> p k n", p=P)).then_inc(w_loaded, 16)
            sp.dma_start(w2s[:], w2).then_inc(w_loaded, 16)
            f["load"](sp)

        @block.gpsimd
        def _(pool):
            with pool.Fori(0, NT // 2) as i:
                for u in range(2):
                    pool.wait_ge(f["h_done"], 2 * i + u + 3)
                    pool.dma_start(h_dram[cols(2 * i + u, P), :], f["h"][u][:]).then_inc(stored[u], 16)
            for u in range(2):
                pool.wait_ge(stored[u], 16 * (NT // 2))

        @block.vector
        def _(dve):
            dve.sem_inc(f["h_done"], 2)
            with dve.Fori(0, NT // 2) as i:
                for u in range(2):
                    f["dve_step"](dve, i, u, [f["turn_done"]], stored)

        @block.tensor
        def _(pe):
            pe.sem_inc(f["turn_done"], 2)
            pe.sem_inc(kq_done, 2)
            pe.wait_ge(w_loaded, 48)

            def product(i, u):
                t = 2 * i + u
                pe.wait_ge(f["hT_done"], t + 3)
                pe.wait_ge(copied, t)
                for v, ws in enumerate((w3s, w1s)):
                    for k in range(KC):
                        ins = nc.tensor.matmul(kq[:, v, :], ws[:, k, :], f["hT"][u][:, k, :],
                                               start=(k == 0), stop=(k == KC - 1))
                ins.then_inc(kq_done, 1)
                pe.wait_ge(q_done, t + 1)
                pr.passed(pe)
                nc.tensor.matmul(qw[:], w2s[:], qT[:], start=True, stop=True).then_inc(qw_done, 1)

            one_ahead(pe, lambda i, u: f["pe_turn"](pe, i, u), product)

        @block.scalar
        def _(act):
            act.sem_inc(f["hT_done"], 2)

            def front(i, u):
                f["act_std"](act, i, u)
                f["act_hT"](act, i, u, kq_done)

            def copy_out(i, u):
                t = 2 * i + u
                act.wait_ge(kq_done, t + 3)
                nc.scalar.copy(qT[:], kq[:, 1, :]).then_inc(q_done, 1)
                nc.scalar.copy(K[:, cols(t, P)], kq[:, 0, :])
                act.wait_ge(qw_done, t + 1)
                nc.scalar.copy(QW[:, cols(t, P)], qw[:]).then_inc(copied, 1)

            one_ahead(act, front, copy_out)


def walk(pr, c, s, xf_dram, xf_new, z_dram, z_new, u1):
    nc = pr.nc
    adjT = c["adjT"]
    with pr.stage():
        XP = pr.sb("XP", [P, NT, PARTS, D], BF16)

        with ExitStack() as split:
            rest = [split.enter_context(nc.sbuf_tensor(f"rest{b}_{pr.n}", [P, D], F32)) for b in range(4)]
            loaded, rest_done, cast_done = ([pr.sem(f"{n}{b}") for b in range(4)] for n in ("loaded", "rest_done", "cast_done"))
            with nc.Block() as block:
                @block.sync
                def _(sp):
                    for b in range(4):
                        sp.dma_start(rest[b][:], xf_dram[cols(b, P), :]).then_inc(loaded[b], 16)
                    with sp.Fori(1, NT // 4) as i:
                        for b in range(4):
                            sp.wait_ge(cast_done[b], i * PARTS)
                            sp.dma_start(rest[b][:], xf_dram[cols(4 * i + b, P), :]).then_inc(loaded[b], 16)

                @block.vector
                def _(dve):
                    with dve.Fori(0, NT // 4) as i:
                        for pair in ((0, 1), (2, 3)):
                            for p in range(1, PARTS):
                                for b in pair:
                                    dve.wait_ge(cast_done[b], i * PARTS + p)
                                    nc.vector.tensor_tensor(rest[b][:], rest[b][:], XP[:, 4 * i + b, p - 1, :],
                                                            ALU.subtract).then_inc(rest_done[b], 1)

                @block.scalar
                def _(act):
                    with act.Fori(0, NT // 4) as i:
                        for pair in ((0, 1), (2, 3)):
                            for p in range(PARTS):
                                for b in pair:
                                    if p:
                                        act.wait_ge(rest_done[b], i * (PARTS - 1) + p)
                                    else:
                                        act.wait_ge(loaded[b], 16 * i + 16)
                                    nc.scalar.copy(XP[:, 4 * i + b, p, :], rest[b][:]).then_inc(cast_done[b], 1)

        usb = pr.sb("u1", [P, KC, D])
        xf, z, new, zo = ([pr.sb(f"{n}{u}", [P, D]) for u in range(2)] for n in ("xf", "z", "new", "zo"))
        nT = [pr.sb(f"nT{u}", [P, KC, P]) for u in range(2)]
        inv = [pr.sb(f"inv{u}", [P, 1]) for u in range(2)]
        acc = [pr.ps(f"acc{u}", [P, D]) for u in range(2)]
        deg = [pr.ps(f"deg{u}", [P, 2]) for u in range(2)]
        turned = pr.ps("turned", [P, KC, P])
        prod = pr.ps("prod", [P, D])
        u_loaded = pr.sem("u_loaded")
        xf_loaded, z_loaded, n_stored, z_stored = ([pr.sem(f"{n}{u}") for u in range(2)]
                                                   for n in ("xf_loaded", "z_loaded", "n_stored", "z_stored"))
        acc_done, new_done, turn_done, nT_done, prod_done, z_done, order = (
            pr.sem(n) for n in ("acc_done", "new_done", "turn_done", "nT_done", "prod_done", "z_done", "order_walk"))
        block = pr.block()

        @block.sync
        def _(sp):
            sp.dma_start(usb[:], u1.rearrange("(k p) n -> p k n", p=P)).then_inc(u_loaded, 16)
            tile_loads(pr, [(xf, lambda t: xf_dram[cols(t, P), :], xf_loaded),
                            (z, lambda t: z_dram[cols(t, P), :], z_loaded)])(sp, [new_done, z_done])

        @block.gpsimd
        def _(pool):
            with pool.Fori(0, NT // 2) as i:
                for u in range(2):
                    t = 2 * i + u
                    pool.wait_ge(new_done, t + 3)
                    pool.dma_start(xf_new[cols(t, P), :], new[u][:]).then_inc(n_stored[u], 16)
                    pool.wait_ge(z_done, t + 3)
                    pr.passed(pool)
                    pool.dma_start(z_new[cols(t, P), :], zo[u][:]).then_inc(z_stored[u], 16)
            for u in range(2):
                pool.wait_ge(n_stored[u], 16 * (NT // 2))
                pool.wait_ge(z_stored[u], 16 * (NT // 2))

        @block.tensor
        def _(pe):
            def product(t, u):
                pe.wait_ge(new_done, t + 1)
                for j in range(NT):
                    lhs = adjT[:, j, cols(t, P)]
                    nc.tensor.matmul(deg[u][:], lhs, c["ones16"][:], start=(j == 0), stop=(j == NT - 1))
                    for p in range(PARTS):
                        ins = nc.tensor.matmul(acc[u][:], lhs, XP[:, j, p, :], start=(j + p == 0),
                                               stop=(j == NT - 1 and p == PARTS - 1))
                ins.then_inc(acc_done, 1)

            def project(t, u):
                pe.wait_ge(new_done, t + 3)
                pe.wait_ge(nT_done, t + 2)
                for k in range(KC):
                    ins = nc.tensor.transpose(turned[:, k, :], new[u][:, k * P:(k + 1) * P], c["id32"][:])
                ins.then_inc(turn_done, 1)
                pe.wait_ge(nT_done, t + 3)
                pe.wait_ge(z_done, t + 2)
                for k in range(KC):
                    ins = nc.tensor.matmul(prod[:], nT[u][:, k, :], usb[:, k, :], start=(k == 0), stop=(k == KC - 1))
                ins.then_inc(prod_done, 1)

            pe.sem_inc(turn_done, 2)
            pe.sem_inc(prod_done, 2)
            pe.wait_ge(u_loaded, 16)
            product(0, 0)
            with pe.Fori(0, NT // 2 - 1) as i:
                for u in range(2):
                    product(2 * i + u + 1, 1 - u)
                    project(2 * i + u, u)
            product(NT - 1, 1)
            project(NT - 2, 0)
            project(NT - 1, 1)

        @block.scalar
        def _(act):
            act.sem_inc(nT_done, 2)
            with act.Fori(0, NT // 2) as i:
                for u in range(2):
                    t = 2 * i + u
                    act.wait_ge(turn_done, t + 3)
                    act.wait_ge(prod_done, t + 1)
                    nc.scalar.copy(nT[u][:], turned[:]).then_inc(nT_done, 1)

        @block.vector
        def _(dve):
            dve.sem_inc(new_done, 2)
            dve.sem_inc(z_done, 2)
            with dve.Fori(0, NT // 2) as i:
                for u in range(2):
                    t = 2 * i + u
                    link = Link(dve, order, t * 3)
                    dve.wait_ge(acc_done, t + 1)
                    link(nc.vector.tensor_scalar(inv[u][:], deg[u][:, 0:1], 1.0, 1e-12, ALU.add, ALU.max))
                    link(nc.vector.reciprocal(inv[u][:], inv[u][:]))
                    dve.wait_ge(xf_loaded[u], 16 * i + 16)
                    dve.wait_ge(n_stored[u], 16 * i)
                    dve.wait_ge(turn_done, t + 1)
                    link(nc.vector.tensor_tensor(new[u][:], acc[u][:], xf[u][:], ALU.add))
                    nc.vector.tensor_scalar(new[u][:], new[u][:], inv[u][:, 0:1], None, ALU.mult).then_inc(new_done, 1)
                    dve.wait_ge(prod_done, t + 3)
                    dve.wait_ge(z_loaded[u], 16 * i + 16)
                    dve.wait_ge(z_stored[u], 16 * i)
                    nc.vector.tensor_tensor(zo[u][:], prod[:], z[u][:], ALU.add).then_inc(z_done, 1)


P_TOP = 0.9
ALL = 24
WIDTH = 9.94


def top_attention(pr, c, first, last, xa_dram, xa_new, z_dram, z_new, u2, QW, K, w1, w2, w3, QWn, Kn):
    nc = pr.nc
    G = 4
    NG = NT // G
    with pr.stage():
        Xa = pr.sb("Xa", [P, NT, D])
        E = [pr.sb(f"E{u}", [P, G, N]) for u in range(2)]
        below = [pr.sb(f"below{u}", [P, N]) for u in range(2)]
        junk = [below[k // 2][:].bitcast(BF16)[:, (k % 2) * N:(k % 2 + 1) * N] for k in range(4)]
        WT = [pr.sb(f"WT{u}", [P, NT, P]) for u in range(2)]
        usb = pr.sb("u2", [P, KC, D])
        w1s, w3s, w2s = pr.sb("w1", [P, KC, 64]), pr.sb("w3", [P, KC, 64]), pr.sb("w2", [64, 64])
        qs = [pr.sb(f"qs{u}", [64, P]) for u in range(G)]
        qT = pr.sb("qT", [64, P])
        ratio = pr.sb("ratio", [P, ALL])
        mx, nmx, S, goal, lo, th, F, hit, kept, low_sum, unres, thr = (
            pr.sb(n, [P, G]) for n in ("mx", "nmx", "S", "goal", "lo", "th", "F", "hit", "kept", "low_sum", "unres", "thr"))
        inv = [pr.sb(f"inv{u}", [P, G]) for u in range(2)]
        top8, sum8a, sum8b, in8 = (pr.sb(n, [P, G, 8]) for n in ("top8", "sum8a", "sum8b", "in8"))
        flag, flagT = pr.sb("flag", [P, 32]), pr.sb("flagT", [P, 32])
        flag1, flag4 = pr.sb("flag1", [P, 1]), pr.sb("flag4", [1, 4])
        flagi = pr.sb("flagi", [1, 1], mybir.dt.int32)
        z, zo, new, ys = ([pr.sb(f"{n}{u}", [P, D]) for u in range(2)] for n in ("z", "zo", "new", "ys"))
        nT = pr.sb("nT", [P, KC, P])
        zps = pr.ps("zps", [P, N])
        tw = [pr.ps(f"tw{u}", [P, 4, P]) for u in range(2)]
        o = pr.ps("o", [P, D])
        y = pr.ps("y", [P, D])
        w_loaded, x_loaded, steps_set = pr.sem("w_loaded"), pr.sem("x_loaded"), pr.sem("steps_set")
        z_loaded, n_stored, z_stored = ([pr.sem(f"{n}{u}") for u in range(2)] for n in ("z_loaded", "n_stored", "z_stored"))
        (qs_done, logits_done, logits_kept, max_done, exp_done, masked, inv_done, order, order2, order3, order4, turn_done, quad_done,
         pv_done, new_done, y_done, ys_done, z_done, kq_done, q_done, qw_done, copied) = (pr.sem(n) for n in (
             "qs_done", "logits_done", "logits_kept", "max_done", "exp_done", "masked", "inv_done", "order_group",
             "order_rounds", "order_next8", "order_rest", "turn_done", "quad_done", "pv_done", "new_done", "y_done", "ys_done", "z_done",
             "kq_done", "q_done", "qw_done", "copied"))
        QUADS = NT // 4 + 1
        block = pr.block()

        def in_groups(eng, ahead, behind):
            ahead(0, 0)
            with eng.Fori(0, NG // 2 - 1) as i:
                ahead(2 * i + 1, 1)
                behind(2 * i, 0)
                ahead(2 * i + 2, 0)
                behind(2 * i + 1, 1)
            ahead(NG - 1, 1)
            behind(NG - 2, 0)
            behind(NG - 1, 1)

        @block.sync
        def _(sp):
            sp.dma_start(w1s[:], w1.rearrange("(k p) n -> p k n", p=P)).then_inc(w_loaded, 16)
            sp.dma_start(w3s[:], w3.rearrange("(k p) n -> p k n", p=P)).then_inc(w_loaded, 16)
            sp.dma_start(w2s[:], w2).then_inc(w_loaded, 16)
            sp.dma_start(usb[:], u2.rearrange("(k p) n -> p k n", p=P)).then_inc(w_loaded, 16)
            sp.dma_start(Xa[:], xa_dram.rearrange("(t p) n -> p t n", p=P)).then_inc(x_loaded, 16)
            tile_loads(pr, [(z, lambda t: z_dram[cols(t, P), :], z_loaded)])(sp, [z_done])

        @block.gpsimd
        def _(pool):
            for k in range(ALL):
                ins = nc.gpsimd.memset(ratio[:, k:k + 1], float(np.exp(WIDTH / 2 ** (k + 1))))
            nc.gpsimd.memset(flag[:], 0.0).then_inc(steps_set, 1)
            pool.sem_inc(z_done, 2)
            with pool.Fori(0, NT // 2) as i:
                for u in range(2):
                    t = 2 * i + u
                    pool.wait_ge(new_done, t + 3)
                    pool.dma_start(xa_new[cols(t, P), :], new[u][:]).then_inc(n_stored[u], 16)
                    pool.wait_ge(ys_done, t + 3)
                    pool.wait_ge(z_loaded[u], 16 * i + 16)
                    pool.wait_ge(z_stored[u], 16 * i)
                    nc.gpsimd.tensor_tensor(zo[u][:], ys[u][:], z[u][:], ALU.add).then_inc(z_done, 1)
                    pool.wait_ge(z_done, t + 3)
                    pr.passed(pool)
                    pool.dma_start(z_new[cols(t, P), :], zo[u][:]).then_inc(z_stored[u], 16)
            for u in range(2):
                pool.wait_ge(n_stored[u], 16 * (NT // 2))
                pool.wait_ge(z_stored[u], 16 * (NT // 2))

        @block.tensor
        def _(pe):
            def logits(g, v):
                for u in range(G):
                    t = G * g + u
                    pe.wait_ge(qs_done, t + 1)
                    pe.wait_ge(logits_kept, t)
                    for n in range(4):
                        ins = nc.tensor.matmul(zps[:, n * 512:(n + 1) * 512], qs[u][:], K[:, n * 512:(n + 1) * 512],
                                               start=True, stop=True)
                    ins.then_inc(logits_done, 1)

            def values(g, v):
                for u in range(G):
                    t = G * g + u
                    pe.wait_ge(masked, t + 1)
                    for q in range(4):
                        pe.wait_ge(quad_done, t * QUADS + q + 1)
                        for k in range(4):
                            b = 4 * q + k
                            ins = nc.tensor.transpose(tw[(u * QUADS + q) % 2][:, k, :], E[v][:, u, b * P:(b + 1) * P], c["id32"][:])
                        ins.then_inc(turn_done, 1)
                    pe.wait_ge(copied, t)
                    for q in range(4):
                        pe.wait_ge(quad_done, t * QUADS + q + 3)
                        for j in range(4 * q, 4 * q + 4):
                            ins = nc.tensor.matmul(o[:], WT[u % 2][:, j, :], Xa[:, j, :], start=(j == 0), stop=(j == NT - 1))
                    ins.then_inc(pv_done, 1)
                    pe.wait_ge(new_done, t + 3)
                    for k in range(KC):
                        ins = nc.tensor.transpose(tw[(u * QUADS + 4) % 2][:, k, :], new[u % 2][:, k * P:(k + 1) * P], c["id32"][:])
                    ins.then_inc(turn_done, 1)
                    pe.wait_ge(quad_done, (t + 1) * QUADS + 2)
                    pe.wait_ge(ys_done, t + 2)
                    for k in range(KC):
                        ins = nc.tensor.matmul(y[:], nT[:, k, :], usb[:, k, :], start=(k == 0), stop=(k == KC - 1))
                    ins.then_inc(y_done, 1)
                    if not last:
                        for w, ws in enumerate((w3s, w1s)):
                            for k in range(KC):
                                ins = nc.tensor.matmul(o[0:64, w * P:(w + 1) * P], ws[:, k, :], nT[:, k, :],
                                                       start=(k == 0), stop=(k == KC - 1))
                        ins.then_inc(kq_done, 1)
                        pe.wait_ge(q_done, t + 1)
                        pr.passed(pe)
                        nc.tensor.matmul(o[0:64, 2 * P:3 * P], w2s[:], qT[:], start=True, stop=True).then_inc(qw_done, 1)

            pe.wait_ge(w_loaded, 64)
            pe.wait_ge(x_loaded, 16)
            in_groups(pe, logits, values)

        @block.scalar
        def _(act):
            def keep_logits(g, v):
                for u in range(G):
                    nc.scalar.copy(qs[u][:], QW[:, cols(G * g + u, P)]).then_inc(qs_done, 1)
                for u in range(G):
                    t = G * g + u
                    act.wait_ge(logits_done, t + 1)
                    nc.scalar.copy(E[v][:, u, :], zps[:]).then_inc(logits_kept, 1)

            def exps(g, v):
                for u in range(G):
                    t = G * g + u
                    act.wait_ge(max_done, t + 1)
                    nc.scalar.activation(E[v][:, u, :], E[v][:, u, :], ACT.Exp, bias=nmx[:, u:u + 1],
                                         accum_out=S[:, u:u + 1]).then_inc(exp_done, 1)

            def serve(g, v):
                act.wait_ge(inv_done, g + 1)
                for u in range(G):
                    t = G * g + u
                    for q in range(4):
                        act.wait_ge(turn_done, t * QUADS + q + 1)
                        nc.scalar.copy(WT[u % 2][:, 4 * q:4 * q + 4, :], tw[(u * QUADS + q) % 2][:]).then_inc(quad_done, 1)
                    act.wait_ge(pv_done, t + 1)
                    act.wait_ge(n_stored[u % 2], (2 * g + u // 2) * 16)
                    ins = nc.scalar.activation(new[u % 2][:], o[:], ACT.Copy, scale=inv[v][:, u:u + 1]).then_inc(new_done, 1)
                    act.wait_ge(turn_done, (t + 1) * QUADS)
                    nc.scalar.copy(nT[:], tw[(u * QUADS + 4) % 2][:]).then_inc(quad_done, 1)
                    act.wait_ge(y_done, t + 1)
                    act.wait_ge(z_done, t + 1)
                    nc.scalar.copy(ys[u % 2][:], y[:]).then_inc(ys_done, 1)
                    if last:
                        act.wait_ge(new_done, t + 3)
                        act.sem_inc(copied, 1)
                    else:
                        act.wait_ge(kq_done, t + 1)
                        nc.scalar.copy(Kn[:, cols(t, P)], o[0:64, 0:P])
                        nc.scalar.copy(qT[:], o[0:64, P:2 * P]).then_inc(q_done, 1)
                        act.wait_ge(qw_done, t + 1)
                        nc.scalar.copy(QWn[:, cols(t, P)], o[0:64, 2 * P:3 * P]).then_inc(copied, 1)

            act.sem_inc(quad_done, 2)
            act.sem_inc(new_done, 2)
            act.sem_inc(ys_done, 2)
            keep_logits(0, 0)
            exps(0, 0)
            with act.Fori(0, NG // 2 - 1) as i:
                keep_logits(2 * i + 1, 1)
                exps(2 * i + 1, 1)
                serve(2 * i, 0)
                keep_logits(2 * i + 2, 0)
                exps(2 * i + 2, 0)
                serve(2 * i + 1, 1)
            keep_logits(NG - 1, 1)
            exps(NG - 1, 1)
            serve(NG - 2, 0)
            serve(NG - 1, 1)

        @block.vector
        def _(dve):
            def halve(Ev, k, link):
                link(nc.vector.tensor_scalar(th[:], lo[:], ratio[:, bass.ds(k, 1)], None, ALU.mult))
                for u in range(G):
                    ins = nc.vector.scalar_tensor_tensor(out=junk[u], in0=Ev[:, u, :], scalar=th[:, u:u + 1],
                                                         in1=Ev[:, u, :], op0=ALU.is_ge, op1=ALU.mult,
                                                         accum_out=F[:, u:u + 1])
                link(ins)
                link(nc.vector.tensor_tensor(hit[:], F[:], goal[:], ALU.is_ge))
                link(nc.vector.tensor_tensor(hit[:], hit[:], th[:], ALU.mult))
                link(nc.vector.tensor_tensor(lo[:], lo[:], hit[:], ALU.max))

            def bracket_end(halvings):
                return nc.vector.tensor_scalar(th[:], lo[:], float(np.exp(WIDTH / 2 ** halvings)) * (1 + 1e-6), None, ALU.mult)

            def single_out(Ev, link):
                for u in range(G):
                    link(nc.vector.scalar_tensor_tensor(out=below[u % 2][:], in0=Ev[:, u, :], scalar=th[:, u:u + 1],
                                                        in1=Ev[:, u, :], op0=ALU.is_lt, op1=ALU.mult,
                                                        accum_out=low_sum[:, u:u + 1]))
                    pr.passed(dve)
                    link(nc.vector.max(top8[:, u, :], below[u % 2][:]))
                link(nc.vector.tensor_copy(sum8a[:, :, 0:1], top8[:, :, 0:1]))
                link(nc.vector.tensor_tensor(sum8a[:, :, 1:8], top8[:, :, 1:8], top8[:, :, 0:7], ALU.add))
                link(nc.vector.tensor_copy(sum8b[:, :, 0:2], sum8a[:, :, 0:2]))
                link(nc.vector.tensor_tensor(sum8b[:, :, 2:8], sum8a[:, :, 2:8], sum8a[:, :, 0:6], ALU.add))
                link(nc.vector.tensor_copy(sum8a[:, :, 0:4], sum8b[:, :, 0:4]))
                link(nc.vector.tensor_tensor(sum8a[:, :, 4:8], sum8b[:, :, 4:8], sum8b[:, :, 0:4], ALU.add))
                link(nc.vector.tensor_tensor(F[:], goal[:], S[:], ALU.subtract))
                link(nc.vector.tensor_tensor(F[:], F[:], low_sum[:], ALU.add))
                link(nc.vector.tensor_tensor(in8[:], sum8a[:], F[:].unsqueeze(2).broadcast_to([P, G, 8]), ALU.is_lt))
                link(nc.vector.tensor_copy(unres[:].unsqueeze(2), in8[:, :, 7:8]))
                link(nc.vector.tensor_scalar(in8[:, :, 0:7], in8[:, :, 0:7], -4.0, 4.0, ALU.mult, ALU.add))
                link(nc.vector.tensor_tensor(sum8b[:, :, 1:8], in8[:, :, 0:7], top8[:, :, 1:8], ALU.max))
                link(nc.vector.tensor_copy(sum8b[:, :, 0:1], top8[:, :, 0:1]))
                link(nc.vector.tensor_reduce(thr[:], sum8b[:], AX.X, ALU.min))
                link(nc.vector.tensor_scalar(F[:], F[:], 0.0, None, ALU.is_le))
                link(nc.vector.tensor_tensor(F[:], F[:], th[:], ALU.mult))
                link(nc.vector.tensor_tensor(thr[:], thr[:], F[:], ALU.max))

            def any_unresolved(link):
                link(nc.vector.tensor_reduce(flag[:, 0:1], unres[:], AX.X, ALU.max))
                link(nc.vector.transpose(flagT[:], flag[:]))
                link(nc.vector.tensor_reduce(flag1[:], flagT[:], AX.X, ALU.max))
                for q in range(4):
                    link(nc.vector.tensor_copy(flag4[0:1, q:q + 1], flag1[32 * q:32 * q + 1, :]))
                link(nc.vector.tensor_reduce(flagi[:], flag4[:], AX.X, ALU.max))
                pr.passed(dve)
                return dve.value_load(flagi[0:1, 0:1], min_val=0, max_val=1) > 0

            HALVE, SINGLE, ANY = 5, 25, 8
            BODY = G + 3 + SINGLE + ANY + 1

            def search(g, v):
                Ev = E[v]
                link = Link(dve, order, g * BODY)
                for u in range(G):
                    t = G * g + u
                    dve.wait_ge(logits_kept, t + 1)
                    link(nc.vector.tensor_reduce(mx[:, u:u + 1], Ev[:, u, :], AX.X, ALU.max))
                    nc.vector.tensor_scalar(nmx[:, u:u + 1], mx[:, u:u + 1], -1.0, None, ALU.mult).then_inc(max_done, 1)
                dve.wait_ge(exp_done, G * (g + 1))
                link(nc.vector.memset(lo[:], float(np.exp(-WIDTH))))
                link(nc.vector.tensor_scalar(goal[:], S[:], P_TOP, None, ALU.mult))
                pr.passed(dve)
                with dve.Fori(0, first) as k:
                    inner = Link(dve, order2, (g * first + k) * HALVE)
                    halve(Ev, k, inner)
                    assert inner.k == HALVE
                link(bracket_end(first))
                n = link.k
                single_out(Ev, link)
                assert link.k - n == SINGLE, link.k - n
                with dve.If(any_unresolved(link)):
                    inner = Link(dve, order3)
                    inner(nc.vector.tensor_tensor(hit[:].unsqueeze(2), top8[:, :, 7:8], unres[:].unsqueeze(2), ALU.mult))
                    inner(nc.vector.tensor_scalar(unres[:], unres[:], -1.0, 1.0, ALU.mult, ALU.add))
                    inner(nc.vector.tensor_tensor(th[:], th[:], unres[:], ALU.mult))
                    inner(nc.vector.tensor_tensor(th[:], th[:], hit[:], ALU.max))
                    single_out(Ev, inner)
                    with dve.If(any_unresolved(inner)):
                        with dve.Fori(first, ALL) as k:
                            halve(Ev, k, Link(dve, order4, (k - first) * HALVE))
                        rest = Link(dve, order4, (ALL - first) * HALVE)
                        rest(bracket_end(ALL))
                        single_out(Ev, rest)
                        rest(nc.vector.tensor_tensor(hit[:], lo[:], unres[:], ALU.mult))
                        rest(nc.vector.tensor_scalar(unres[:], unres[:], -1.0, 1.0, ALU.mult, ALU.add))
                        rest(nc.vector.tensor_tensor(thr[:], thr[:], unres[:], ALU.mult))
                        rest(nc.vector.tensor_tensor(thr[:], thr[:], hit[:], ALU.max))
                        dve.sem_clear(order4)
                    dve.sem_clear(order3)
                for u in range(G):
                    ins = nc.vector.scalar_tensor_tensor(out=Ev[:, u, :], in0=Ev[:, u, :], scalar=thr[:, u:u + 1],
                                                         in1=Ev[:, u, :], op0=ALU.is_ge, op1=ALU.mult,
                                                         accum_out=kept[:, u:u + 1]).then_inc(masked, 1)
                dve.wait_ge(masked, G * (g + 1))
                nc.vector.reciprocal(inv[v][:], kept[:]).then_inc(inv_done, 1)
                dve.wait_ge(inv_done, g + 1)
                link.k += 1
                dve.sem_inc(order, 1)
                assert link.k == BODY, (link.k, BODY)

            dve.wait_ge(steps_set, 1)
            with dve.Fori(0, NG // 2) as i:
                search(2 * i, 0)
                search(2 * i + 1, 1)


def norm_add(pr, c, z_dram, x_dram, out_dram, gamma, beta):
    nc = pr.nc
    with pr.stage():
        rows = pr.sb("rows", [P, 2, D])
        z, x, y = ([pr.sb(f"{n}{u}", [P, D]) for u in range(2)] for n in ("z", "x", "y"))
        stats = [pr.sb(f"stats{u}", [P, 6]) for u in range(2)]
        mv = [pr.sb(f"mv{u}", [P, 2]) for u in range(2)]
        std, rstd = ([pr.sb(f"{n}{u}", [P, 1]) for u in range(2)] for n in ("std", "rstd"))
        z_loaded, x_loaded, stored = ([pr.sem(f"{n}{u}") for u in range(2)] for n in ("z_loaded", "x_loaded", "stored"))
        r_loaded, mv_done, std_done, out_done, order, order2 = (
            pr.sem(n) for n in ("r_loaded", "mv_done", "std_done", "out_done", "order", "order_stats"))
        block = pr.block()

        @block.sync
        def _(sp):
            sp.dma_start(rows[:, 0, :], gamma.broadcast_to([P, D])).then_inc(r_loaded, 16)
            sp.dma_start(rows[:, 1, :], beta.broadcast_to([P, D])).then_inc(r_loaded, 16)
            tile_loads(pr, [(z, lambda t: z_dram[cols(t, P), :], z_loaded),
                            (x, lambda t: x_dram[cols(t, P), :], x_loaded)])(sp, [out_done])

        @block.gpsimd
        def _(pool):
            with pool.Fori(0, NT // 2) as i:
                for u in range(2):
                    pool.wait_ge(out_done, 2 * i + u + 3)
                    pool.dma_start(out_dram[cols(2 * i + u, P), :], y[u][:]).then_inc(stored[u], 16)
            for u in range(2):
                pool.wait_ge(stored[u], 16 * (NT // 2))

        @block.scalar
        def _(act):
            with act.Fori(0, NT // 2) as i:
                for u in range(2):
                    act.wait_ge(mv_done, 2 * i + u + 1)
                    nc.scalar.activation(std[u][:], mv[u][:, 1:2], ACT.Sqrt, bias=c["eps"][:, 0:1]).then_inc(std_done, 1)

        @block.vector
        def _(dve):
            dve.sem_inc(out_done, 2)
            dve.wait_ge(r_loaded, 32)

            def stat(i, u):
                dve.wait_ge(z_loaded[u], 16 * i + 16)
                Link(dve, order2, 2 * i + u)(nc.vector.bn_stats(stats[u][:], z[u][:]))
                pr.passed(dve)
                nc.vector.bn_aggr(mv[u][:], stats[u][:]).then_inc(mv_done, 1)

            def norm(i, u):
                t = 2 * i + u
                link = Link(dve, order, t * 4)
                dve.wait_ge(mv_done, t + 1)
                dve.wait_ge(std_done, t + 1)
                link(nc.vector.reciprocal(rstd[u][:], std[u][:]))
                dve.wait_ge(stored[u], 16 * i)
                link(nc.vector.tensor_scalar(y[u][:], z[u][:], mv[u][:, 0:1], rstd[u][:, 0:1], ALU.subtract, ALU.mult))
                link(nc.vector.tensor_tensor(y[u][:], y[u][:], rows[:, 0, :], ALU.mult))
                link(nc.vector.tensor_tensor(y[u][:], y[u][:], rows[:, 1, :], ALU.add))
                dve.wait_ge(x_loaded[u], 16 * i + 16)
                nc.vector.tensor_tensor(y[u][:], y[u][:], x[u][:], ALU.add).then_inc(out_done, 1)

            one_ahead(dve, stat, norm)


def heads_mlp(pr, c, hid_dram, x_dram, out_dram, w1, w2, w3, w4, b1, b2, b3, b4):
    nc = pr.nc
    with pr.stage():
        w1s, w2s, w3s, w4s = (pr.sb("w1", [P, KC, 256]), pr.sb("w2", [P, 2, 128]), pr.sb("w3", [P, 256]),
                              pr.sb("w4", [P, 2, D]))
        b1s, b2s, b3s, b4s = pr.sb("b1", [P, 2]), pr.sb("b2", [P, 1]), pr.sb("b3", [P, 2]), pr.sb("b4", [P, D])
        hid, x, low, e, y = ([pr.sb(f"{n}{u}", [P, D]) for u in range(2)] for n in ("hid", "x", "low", "e", "y"))
        hT = [pr.sb(f"hT{u}", [P, KC, P]) for u in range(2)]
        o1s, o2s, o3s = pr.sb("o1s", [P, 2, P]), pr.sb("o2s", [P, P]), pr.sb("o3s", [P, 2, P])
        turned, o1, o2, o3, o4 = (pr.ps("turned", [P, KC, P]), pr.ps("o1", [P, 2, P]), pr.ps("o2", [P, P]),
                                  pr.ps("o3", [P, 2, P]), pr.ps("o4", [P, D]))
        w_loaded = pr.sem("w_loaded")
        hid_loaded, x_loaded, stored = ([pr.sem(f"{n}{u}") for u in range(2)] for n in ("hid_loaded", "x_loaded", "stored"))
        low_done, e_done, elu_done, turn_done, hT_done, out_done, order, order2 = (
            pr.sem(n) for n in ("low_done", "e_done", "elu_done", "turn_done", "hT_done", "out_done", "order", "order_sum"))
        l_done = [pr.sem(f"l{k}_done") for k in range(1, 5)]
        r_done = [pr.sem(f"r{k}_done") for k in range(1, 4)]
        block = pr.block()

        @block.sync
        def _(sp):
            for dst, src in ((w1s, w1.rearrange("(k p) n -> p k n", p=P)), (w2s, w2.rearrange("(k p) n -> p k n", p=P)),
                             (w3s, w3), (w4s, w4.rearrange("(k p) n -> p k n", p=P)), (b1s, b1), (b2s, b2), (b3s, b3),
                             (b4s, b4.broadcast_to([P, D]))):
                sp.dma_start(dst[:], src).then_inc(w_loaded, 16)
            tile_loads(pr, [(hid, lambda t: hid_dram[cols(t, P), :], hid_loaded),
                            (x, lambda t: x_dram[cols(t, P), :], x_loaded)])(sp, [out_done])

        @block.gpsimd
        def _(pool):
            with pool.Fori(0, NT // 2) as i:
                for u in range(2):
                    pool.wait_ge(out_done, 2 * i + u + 3)
                    pool.dma_start(out_dram[cols(2 * i + u, P), :], y[u][:]).then_inc(stored[u], 16)
            for u in range(2):
                pool.wait_ge(stored[u], 16 * (NT // 2))

        @block.tensor
        def _(pe):
            pe.wait_ge(w_loaded, 128)

            def turn(i, u):
                pe.wait_ge(elu_done, 2 * i + u + 1)
                pe.wait_ge(hT_done, 2 * i + u)
                for k in range(KC):
                    ins = nc.tensor.transpose(turned[:, k, :], hid[u][:, k * P:(k + 1) * P], c["id32"][:])
                ins.then_inc(turn_done, 1)

            def layers(i, u):
                    t = 2 * i + u
                    pe.wait_ge(hT_done, t + 1)
                    for m in range(2):
                        for k in range(KC):
                            ins = nc.tensor.matmul(o1[:, m, :], w1s[:, k, m * P:(m + 1) * P], hT[u][:, k, :],
                                                   start=(k == 0), stop=(k == KC - 1))
                    ins.then_inc(l_done[0], 1)
                    pe.wait_ge(r_done[0], t + 1)
                    for k in range(2):
                        ins = nc.tensor.matmul(o2[:], w2s[:, k, :], o1s[:, k, :], start=(k == 0), stop=(k == 1))
                    ins.then_inc(l_done[1], 1)
                    pe.wait_ge(r_done[1], t + 1)
                    for m in range(2):
                        ins = nc.tensor.matmul(o3[:, m, :], w3s[:, m * P:(m + 1) * P], o2s[:], start=True, stop=True)
                    ins.then_inc(l_done[2], 1)
                    pe.wait_ge(r_done[2], t + 1)
                    pe.wait_ge(out_done, t + 2)
                    for k in range(2):
                        ins = nc.tensor.matmul(o4[:], o3s[:, k, :], w4s[:, k, :], start=(k == 0), stop=(k == 1))
                    ins.then_inc(l_done[3], 1)

            one_ahead(pe, turn, layers)

        @block.scalar
        def _(act):
            act.wait_ge(w_loaded, 128)

            def front(i, u):
                t = 2 * i + u
                act.wait_ge(low_done, t + 1)
                nc.scalar.activation(e[u][:], low[u][:], ACT.Exp).then_inc(e_done, 1)
                act.wait_ge(turn_done, t + 1)
                nc.scalar.copy(hT[u][:], turned[:]).then_inc(hT_done, 1)

            def relus(i, u):
                    t = 2 * i + u
                    act.wait_ge(l_done[0], t + 1)
                    for m in range(2):
                        ins = nc.scalar.activation(o1s[:, m, :], o1[:, m, :], ACT.Relu, bias=b1s[:, m:m + 1])
                    ins.then_inc(r_done[0], 1)
                    act.wait_ge(l_done[1], t + 1)
                    nc.scalar.activation(o2s[:], o2[:], ACT.Relu, bias=b2s[:, 0:1]).then_inc(r_done[1], 1)
                    act.wait_ge(l_done[2], t + 1)
                    for m in range(2):
                        ins = nc.scalar.activation(o3s[:, m, :], o3[:, m, :], ACT.Relu, bias=b3s[:, m:m + 1])
                    ins.then_inc(r_done[2], 1)

            one_ahead(act, front, relus)

        @block.vector
        def _(dve):
            dve.sem_inc(out_done, 2)
            dve.wait_ge(w_loaded, 128)

            def elu(i, u):
                t = 2 * i + u
                dve.wait_ge(hid_loaded[u], 16 * i + 16)
                nc.vector.tensor_scalar(low[u][:], hid[u][:], 0.0, None, ALU.min).then_inc(low_done, 1)
                dve.wait_ge(e_done, t + 1)
                Link(dve, order, t)(nc.vector.tensor_scalar(hid[u][:], hid[u][:], 0.0, None, ALU.max))
                nc.vector.scalar_tensor_tensor(out=hid[u][:], in0=e[u][:], scalar=-1.0, in1=hid[u][:],
                                               op0=ALU.add, op1=ALU.add).then_inc(elu_done, 1)

            def result(i, u):
                t = 2 * i + u
                dve.wait_ge(l_done[3], t + 1)
                dve.wait_ge(stored[u], 16 * i)
                Link(dve, order2, t)(nc.vector.tensor_tensor(y[u][:], o4[:], b4s[:], ALU.add))
                dve.wait_ge(x_loaded[u], 16 * i + 16)
                nc.vector.tensor_tensor(y[u][:], y[u][:], x[u][:], ALU.add).then_inc(out_done, 1)

            one_ahead(dve, elu, result)


def project_qkv(pr, c, x_dram, wq, wk, wv, bq, bk, bv, q_dram, kT, V):
    nc = pr.nc
    with pr.stage():
        f = norm_and_turn(pr, c, x_dram)
        w = [pr.sb(f"w{n}", [P, KC, D]) for n in "qkv"]
        bqs, bks, bvs = pr.sb("bq", [P, KC]), pr.sb("bk", [P, KC]), pr.sb("bv", [P, D])
        qT = [pr.sb(f"qT{u}", [P, KC, P]) for u in range(2)]
        qp, kp, vp = pr.ps("qp", [P, KC, P]), pr.ps("kp", [P, KC, P]), pr.ps("vp", [P, D])
        w_loaded = pr.sem("w_loaded")
        stored = [pr.sem(f"stored{u}") for u in range(2)]
        q_done, k_done, v_done, q_out, k_out, v_out = (pr.sem(n) for n in ("q_done", "k_done", "v_done", "q_out", "k_out", "v_out"))
        block = pr.block()

        @block.sync
        def _(sp):
            for dst, src in zip(w, (wq, wk, wv)):
                sp.dma_start(dst[:], src.rearrange("(k p) n -> p k n", p=P)).then_inc(w_loaded, 16)
            sp.dma_start(bqs[:], bq).then_inc(w_loaded, 16)
            sp.dma_start(bks[:], bk).then_inc(w_loaded, 16)
            sp.dma_start(bvs[:], bv.broadcast_to([P, D])).then_inc(w_loaded, 16)
            f["load"](sp)

        @block.gpsimd
        def _(pool):
            with pool.Fori(0, NT // 2) as i:
                for u in range(2):
                    t = 2 * i + u
                    pool.wait_ge(q_out, t + 1)
                    pool.dma_start(q_dram[cols(t, P), :], qT[u][:].rearrange("p k n -> p (k n)")).then_inc(stored[u], 16)
            for u in range(2):
                pool.wait_ge(stored[u], 16 * (NT // 2))

        @block.vector
        def _(dve):
            dve.sem_inc(f["h_done"], 2)
            dve.wait_ge(w_loaded, 96)

            def values(i, u):
                dve.wait_ge(v_done, 2 * i + u + 3)
                nc.vector.tensor_tensor(V[:, 2 * i + u, :], vp[:], bvs[:], ALU.add).then_inc(v_out, 1)

            one_ahead(dve, lambda i, u: f["dve_step"](dve, i, u, [f["turn_done"]]), values)

        @block.tensor
        def _(pe):
            pe.sem_inc(f["turn_done"], 2)
            pe.sem_inc(v_done, 2)
            pe.wait_ge(w_loaded, 96)

            def products(i, u):
                    t = 2 * i + u
                    pe.wait_ge(f["hT_done"], t + 3)
                    for ws, dst, done, out in ((w[0], qp, q_done, q_out), (w[1], kp, k_done, k_out)):
                        pe.wait_ge(out, t)
                        for m in range(KC):
                            for k in range(KC):
                                ins = nc.tensor.matmul(dst[:, m, :], ws[:, k, m * P:(m + 1) * P], f["hT"][u][:, k, :],
                                                       start=(k == 0), stop=(k == KC - 1))
                        ins.then_inc(done, 1)
                    pe.wait_ge(v_out, t)
                    for k in range(KC):
                        ins = nc.tensor.matmul(vp[:], f["hT"][u][:, k, :], w[2][:, k, :], start=(k == 0), stop=(k == KC - 1))
                    ins.then_inc(v_done, 1)

            one_ahead(pe, lambda i, u: f["pe_turn"](pe, i, u), products)

        @block.scalar
        def _(act):
            act.sem_inc(f["hT_done"], 2)
            act.wait_ge(w_loaded, 96)

            def front(i, u):
                f["act_std"](act, i, u)
                f["act_hT"](act, i, u, v_done)

            def copies(i, u):
                    t = 2 * i + u
                    act.wait_ge(q_done, t + 1)
                    act.wait_ge(stored[u], 16 * i)
                    for m in range(KC):
                        ins = nc.scalar.activation(qT[u][:, m, :], qp[:, m, :], ACT.Identity, bias=bqs[:, m:m + 1])
                    ins.then_inc(q_out, 1)
                    act.wait_ge(k_done, t + 1)
                    for m in range(KC):
                        ins = nc.scalar.activation(kT[:, m, cols(t, P)], kp[:, m, :], ACT.Identity, bias=bks[:, m:m + 1])
                    ins.then_inc(k_out, 1)

            one_ahead(act, front, copies)


def masked_attention(pr, c, q_dram, kT, V, adj, x_dram, out_dram):
    nc = pr.nc
    SCALE = float(D) ** -0.5
    with pr.stage():
        qT = [pr.sb(f"qT{u}", [P, KC, P]) for u in range(2)]
        a = [pr.sb(f"a{u}", [P, N]) for u in range(2)]
        z, zero, e = pr.sb("z", [P, N]), pr.sb("zero", [P, N]), [pr.sb(f"e{u}", [P, N]) for u in range(2)]
        eT = pr.sb("eT", [P, NT, P])
        x, y = ([pr.sb(f"{n}{u}", [P, D]) for u in range(2)] for n in ("x", "y"))
        mx, nmx, S, inv = ([pr.sb(f"{n}{u}", [P, 1]) for u in range(2)] for n in ("mx", "nmx", "S", "inv"))
        zps = pr.ps("zps", [P, N])
        tw = [pr.ps(f"tw{u}", [P, 4, P]) for u in range(2)]
        o = pr.ps("o", [P, D])
        q_loaded, a_loaded, x_loaded, stored = ([pr.sem(f"{n}{u}") for u in range(2)]
                                                for n in ("q_loaded", "a_loaded", "x_loaded", "stored"))
        z_done, z_read, max_done, exp_done, turn_done, quad_done, pv_done, out_done, order, order2 = (
            pr.sem(n) for n in ("z_done", "z_read", "max_done", "exp_done", "turn_done", "quad_done", "pv_done",
                                "out_done", "order", "order_result"))
        block = pr.block()

        @block.sync
        def _(sp):
            tile_loads(pr, [(qT, lambda t: q_dram[cols(t, P), :].rearrange("p (k n) -> p k n", n=P), q_loaded),
                            (a, lambda t: adj[cols(t, P), :], a_loaded),
                            (x, lambda t: x_dram[cols(t, P), :], x_loaded)])(sp, [z_done, out_done])

        @block.gpsimd
        def _(pool):
            with pool.Fori(0, NT // 2) as i:
                for u in range(2):
                    pool.wait_ge(out_done, 2 * i + u + 3)
                    pool.dma_start(out_dram[cols(2 * i + u, P), :], y[u][:]).then_inc(stored[u], 16)
            for u in range(2):
                pool.wait_ge(stored[u], 16 * (NT // 2))

        @block.tensor
        def _(pe):
            def logits(i, u):
                t = 2 * i + u
                pe.wait_ge(q_loaded[u], 16 * i + 16)
                pe.wait_ge(z_read, t)
                for n in range(4):
                    for k in range(KC):
                        ins = nc.tensor.matmul(zps[:, n * 512:(n + 1) * 512], qT[u][:, k, :], kT[:, k, n * 512:(n + 1) * 512],
                                               start=(k == 0), stop=(k == KC - 1))
                ins.then_inc(z_done, 1)

            def values(i, u):
                t = 2 * i + u
                pe.wait_ge(exp_done, t + 3)
                for q in range(4):
                    pe.wait_ge(quad_done, 4 * t + q + 1)
                    for k in range(4):
                        b = 4 * q + k
                        ins = nc.tensor.transpose(tw[q % 2][:, k, :], e[u][:, b * P:(b + 1) * P], c["id32"][:])
                    ins.then_inc(turn_done, 1)
                pe.wait_ge(out_done, t + 2)
                for q in range(4):
                    pe.wait_ge(quad_done, 4 * t + q + 3)
                    for j in range(4 * q, 4 * q + 4):
                        ins = nc.tensor.matmul(o[:], eT[:, j, :], V[:, j, :], start=(j == 0), stop=(j == NT - 1))
                ins.then_inc(pv_done, 1)

            pe.sem_inc(z_done, 2)
            pe.sem_inc(pv_done, 2)
            logits(0, 0)
            with pe.Fori(0, NT // 2 - 1) as i:
                logits(i, 1)
                values(i, 0)
                logits(i + 1, 0)
                values(i, 1)
            logits(NT // 2 - 1, 1)
            values(NT // 2 - 1, 0)
            values(NT // 2 - 1, 1)

        @block.scalar
        def _(act):
            def exps(i, u):
                t = 2 * i + u
                act.wait_ge(max_done, t + 1)
                act.wait_ge(pv_done, t + 1)
                act.wait_ge(out_done, t + 1)
                nc.scalar.activation(e[u][:], z[:], ACT.Exp, bias=nmx[u][:, 0:1], accum_out=S[u][:, 0:1]).then_inc(exp_done, 1)

            def copies(i, u):
                t = 2 * i + u
                act.wait_ge(pv_done, t + 2)
                for q in range(4):
                    act.wait_ge(turn_done, 4 * t + q + 1)
                    nc.scalar.copy(eT[:, 4 * q:4 * q + 4, :], tw[q % 2][:]).then_inc(quad_done, 1)

            act.sem_inc(exp_done, 2)
            act.sem_inc(quad_done, 2)
            exps(0, 0)
            with act.Fori(0, NT // 2 - 1) as i:
                copies(i, 0)
                exps(i, 1)
                copies(i, 1)
                exps(i + 1, 0)
            copies(NT // 2 - 1, 0)
            exps(NT // 2 - 1, 1)
            copies(NT // 2 - 1, 1)

        @block.vector
        def _(dve):
            def scores(i, u):
                t = 2 * i + u
                link = Link(dve, order, t * 3)
                dve.wait_ge(z_done, t + 3)
                dve.wait_ge(a_loaded[u], 16 * i + 16)
                dve.wait_ge(exp_done, t + 2)
                nc.vector.scalar_tensor_tensor(out=z[:], in0=zps[:], scalar=SCALE, in1=a[u][:], op0=ALU.mult,
                                               op1=ALU.mult).then_inc(z_read, 1)
                dve.wait_ge(z_read, t + 1)
                link(nc.vector.tensor_scalar(zero[:], z[:], 0.0, -10000.0, ALU.is_equal, ALU.mult))
                link(nc.vector.tensor_tensor(z[:], z[:], zero[:], ALU.add))
                link(nc.vector.tensor_reduce(mx[u][:], z[:], AX.X, ALU.max))
                nc.vector.tensor_scalar(nmx[u][:], mx[u][:], -1.0, None, ALU.mult).then_inc(max_done, 1)

            def result(i, u):
                t = 2 * i + u
                link = Link(dve, order2, t * 2)
                dve.wait_ge(pv_done, t + 3)
                link(nc.vector.reciprocal(inv[u][:], S[u][:]))
                dve.wait_ge(stored[u], 16 * i)
                link(nc.vector.tensor_scalar(y[u][:], o[:], inv[u][:, 0:1], 0.0, ALU.mult, ALU.max))
                dve.wait_ge(x_loaded[u], 16 * i + 16)
                nc.vector.tensor_tensor(y[u][:], y[u][:], x[u][:], ALU.add).then_inc(out_done, 1)

            dve.sem_inc(out_done, 2)
            one_ahead(dve, scores, result)


def layout(inputs):
    a = {k: np.asarray(v) for k, v in inputs.items()}
    ins = {"x": a["x"], "adj": a["adj"]}
    ins["w0"] = a["L0_gnn_W_seq"]
    ins["a01"] = np.tile(a["L0_gnn_a1"], 16).reshape(1, D)
    ins["a02"] = np.tile(a["L0_gnn_a2"], 16).reshape(1, D)
    ins["w0o"] = a["L0_gnn_W_out"]
    ins["b0o"] = a["L0_gnn_b_out"].reshape(1, D)
    for n in ("W1", "W2", "W3", "U1_0", "U1_1", "U2_0", "U2_1"):
        ins[f"l1_{n}"] = a[f"L1_gnn_{n}"]
    ins["gamma"] = a["L1_gnn_gamma"].reshape(1, D)
    ins["beta"] = a["L1_gnn_beta"].reshape(1, D)
    ins["w2h"] = np.transpose(a["L2_gnn_W"], (1, 0, 2)).reshape(D, D)
    ins["a21"] = a["L2_gnn_a1"].reshape(1, D)
    ins["a22"] = a["L2_gnn_a2"].reshape(1, D)
    for n in ("W1", "W2", "W3", "W4"):
        ins[f"l2_{n}"] = a[f"L2_gnn_{n}"].T
    for n in ("b1", "b2", "b3"):
        ins[f"l2_{n}"] = a[f"L2_gnn_{n}"].reshape(-1, P).T
    ins["l2_b4"] = a["L2_gnn_b4"].reshape(1, D)
    for n in "qkv":
        ins[f"l3_W{n}"] = a[f"L3_gnn_W_{n}"].T
    for n in "qk":
        ins[f"l3_b{n}"] = a[f"L3_gnn_b_{n}"].reshape(KC, P).T
    ins["l3_bv"] = a["L3_gnn_b_v"].reshape(1, D)
    return {k: np.ascontiguousarray(v) for k, v in ins.items()}


def build(nc, ins, out, stop=99):
    pr = Program(nc)
    root = ExitStack()
    with root:
        def sb(name, shape, dt=F32):
            return root.enter_context(nc.sbuf_tensor(name, shape, dt))

        def dram(name, shape=(N, D), dt=F32):
            return nc.dram_tensor(name, list(shape), dt, kind="Internal").ap()
        c = dict(id32=sb("id32", [P, P]), id16=sb("id16", [P, P], BF16), ones16=sb("ones16", [P, 2], BF16),
                 zero16=sb("zero16", [P, 512], BF16), eps=sb("eps", [P, 1]))
        adjT_dram = dram("adjT_dram", [N, N], BF16)
        seq_dram, hid_dram = dram("seq_dram"), dram("hid_dram")
        arow_dram = dram("arow_dram", [16, N])
        x1, x2, x3 = dram("x1"), dram("x2"), dram("x3")
        h_dram, xf1, xf2, xa1, xa2 = (dram(n) for n in ("h_dram", "xf1", "xf2", "xa1", "xa2"))
        z1, z2, z3, z4 = (dram(n) for n in ("z1", "z2", "z3", "z4"))
        q_dram, keys_dram = dram("q_dram"), dram("keys_dram", [64, 2 * N])
        constants(pr, c)

        def heads_layer(x, w, a1, a2, H, DH, groups):
            with nc.sbuf_tensor(f"scores_{pr.n}", [P, 2, NT, H], F32) as scores, \
                    nc.sbuf_tensor(f"fac_{pr.n}", [P, 6, NT, H], F32) as fac:
                heads_project(pr, c, x, w, a1, a2, seq_dram, scores, H, DH)
                heads_factors(pr, c, scores, fac, arow_dram, H)
                for g in range(groups):
                    heads_attend(pr, c, fac, seq_dram, arow_dram, hid_dram, H, DH, g, H // groups)

        with nc.sbuf_tensor("adjT", [P, NT, N], BF16) as adjT:
            c["adjT"] = adjT
            transpose_adjacency(pr, c, ins["adj"], adjT_dram)
            heads_layer(ins["x"], ins["w0"], ins["a01"], ins["a02"], 16, 32, 2)
            heads_out(pr, c, hid_dram, ins["x"], x1, ins["w0o"], ins["b0o"])
            if stop == 0:
                return
            w = [ins[f"l1_{n}"] for n in ("W1", "W2", "W3")]
            with nc.sbuf_tensor("keys", [64, 2, N], F32) as ks:
                features_keys(pr, c, x1, h_dram, *w, ks[:, 0], ks[:, 1])
                carry(pr, keys_dram, ks[:].rearrange("p v n -> p (v n)"))
            walk(pr, c, 0, h_dram, xf1, h_dram, z1, ins["l1_U1_0"])
            walk(pr, c, 1, xf1, xf2, z1, z2, ins["l1_U1_1"])
            if stop == 1:
                return
        with nc.sbuf_tensor("keys2", [64, 4, N], F32) as ks:
            carry(pr, ks[:, 0:2, :].rearrange("p v n -> p (v n)"), keys_dram)
            top_attention(pr, c, 8, False, h_dram, xa1, z2, z3, ins["l1_U2_0"], ks[:, 0], ks[:, 1], *w, ks[:, 2], ks[:, 3])
            top_attention(pr, c, 10, True, xa1, xa2, z3, z4, ins["l1_U2_1"], ks[:, 2], ks[:, 3], *w, None, None)
        norm_add(pr, c, z4, x1, x2, ins["gamma"], ins["beta"])
        if stop == 2:
            return
        with nc.sbuf_tensor("adjT2", [P, NT, N], BF16) as adjT:
            c["adjT"] = adjT
            reload_adjacency(pr, c, adjT_dram)
            heads_layer(x2, ins["w2h"], ins["a21"], ins["a22"], 8, 64, 2)
        heads_mlp(pr, c, hid_dram, x2, x3, *(ins[f"l2_{n}"] for n in ("W1", "W2", "W3", "W4", "b1", "b2", "b3", "b4")))
        if stop == 3:
            return
        with nc.sbuf_tensor("kT", [P, KC, N], F32) as kT, nc.sbuf_tensor("V", [P, NT, D], F32) as V:
            project_qkv(pr, c, x3, *(ins[f"l3_W{n}"] for n in "qkv"), *(ins[f"l3_b{n}"] for n in "qkv"), q_dram, kT, V)
            masked_attention(pr, c, q_dram, kT, V, ins["adj"], x3, out)


def kernel(**inputs):
    import concourse.bacc as bacc
    from concourse.bass_utils import run_bass_kernel_spmd

    nc = bacc.Bacc("TRN2", target_bir_lowering=False, num_devices=1)
    arrays = {f"in_{k}": v for k, v in layout(inputs).items()}
    ins = {k[3:]: nc.dram_tensor(k, v.shape, mybir.dt.from_np(v.dtype), kind="ExternalInput").ap()
           for k, v in arrays.items()}
    out = nc.dram_tensor("out_0", (N, D), F32, kind="ExternalOutput").ap()
    build(nc, ins, out)
    r = run_bass_kernel_spmd(nc, [arrays], core_ids=[0])
    return r.results[0]["out_0"]
```

```python
from contextlib import ExitStack

import numpy as np

import concourse.bass as bass
from concourse import mybir

F32 = mybir.dt.float32
BF16 = mybir.dt.bfloat16
ALU = mybir.AluOpType
ACT = mybir.ActivationFunctionType
AX = mybir.AxisListType

N = 2048
D = 512
P = 128
NT = N // P
KC = D // P
PARTS = 3
EPS = 1e-5


class Link:

    def __init__(self, eng, sem, base=0):
        self.eng, self.sem, self.base, self.k = eng, sem, base, 0

    def signals(self, ins):
        self.k += 1
        ins.then_inc(self.sem, 1)

    def __call__(self, ins):
        self.signals(ins)
        self.eng.wait_ge(self.sem, self.base + self.k)

    def upto(self, back):
        self.eng.wait_ge(self.sem, self.base + self.k - back)


def pipelined(eng, count, *steps):
    most = max(lead for lead, _ in steps)

    def straight(first, end):
        for t in range(first, end):
            for lead, step in steps:
                if 0 <= t + lead < count:
                    step((t + lead) // 2, (t + lead) % 2)

    pairs = (count - most) // 2
    straight(-most, 0)
    with eng.Fori(0, pairs) as i:
        for u in range(2):
            for lead, step in steps:
                step(i + (u + lead) // 2, (u + lead) % 2)
    straight(2 * pairs, count)


def one_ahead(eng, ahead, behind):
    pipelined(eng, NT, (1, ahead), (0, behind))


CHUNK = 4


def in_chunks(eng, lead, stats, ahead, behind):
    def tiles(q, count):
        for v in range(count):
            ahead(2 * q + (v + lead) // 2, (v + lead) % 2)
            behind(2 * q + v // 2, v % 2)

    stats(0)
    for t in range(lead):
        ahead(t // 2, t % 2)
    with eng.Fori(0, NT // CHUNK - 1) as q:
        stats(q + 1)
        tiles(q, CHUNK)
    tiles(NT // CHUNK - 1, CHUNK - lead)
    for t in range(NT - lead, NT):
        behind(t // 2, t % 2)


def cols(t, width):
    return bass.ds(t * width, width)


class Program:

    def __init__(self, nc):
        self.nc = nc
        self.n = 0
        self.ticks = nc.alloc_semaphore("ticks")

    def stage(self):
        self.ctx = ExitStack()
        self.n += 1
        sems = self.sems = []

        def free():
            for s in sems:
                self.nc.gpsimd.sem_clear(s)
                self.nc.release_semaphore(s)
        self.ctx.callback(free)
        return self.ctx

    def sb(self, name, shape, dt=F32):
        return self.ctx.enter_context(self.nc.sbuf_tensor(f"{name}_{self.n}", shape, dt))

    def ps(self, name, shape, dt=F32):
        return self.ctx.enter_context(self.nc.psum_tensor(f"{name}_{self.n}", shape, dt))

    def sem(self, name):
        sem = self.nc.alloc_semaphore(f"{name}_{self.n}")
        if not name.rstrip("01").endswith("stored"):
            self.sems.append(sem)
        return sem

    def passed(self, eng):
        eng.sem_inc(self.ticks, 1)

    def block(self):
        return self.ctx.enter_context(self.nc.Block())


def constants(pr, c):
    nc = pr.nc
    with pr.stage():
        filled = pr.sem("filled")
        block = pr.block()

        @block.gpsimd
        def _(pool):
            nc.gpsimd.memset(c["id32"][:], 0.0).then_inc(filled, 1)
            nc.gpsimd.memset(c["id16"][:], 0.0).then_inc(filled, 1)
            nc.gpsimd.memset(c["ones16"][:], 1.0)
            nc.gpsimd.memset(c["zero16"][:], 0.0)
            nc.gpsimd.memset(c["eps"][:], EPS)
            pool.wait_ge(filled, 2)
            for m in (c["id32"], c["id16"]):
                nc.gpsimd.affine_select(out=m[:], in_=m[:], compare_op=ALU.not_equal, fill=1.0, base=0,
                                        pattern=[[-1, P]], channel_multiplier=1)


def transpose_adjacency(pr, c, adj, adjT_dram):
    nc = pr.nc
    adjT = c["adjT"]
    with pr.stage():
        raw = [pr.sb(f"raw{u}", [P, N]) for u in range(2)]
        cast = [pr.sb(f"cast{u}", [P, N], BF16) for u in range(2)]
        turned = [pr.ps(f"turned{u}", [P, NT, P], BF16) for u in range(2)]
        loaded = [pr.sem(f"loaded{u}") for u in range(2)]
        cast_done = pr.sem("cast_done")
        turn_done = pr.sem("turn_done")
        kept = pr.sem("kept")
        stored = pr.sem("stored")
        block = pr.block()

        @block.sync
        def _(sp):
            for u in range(2):
                sp.dma_start(raw[u][:], adj[cols(u, P), :]).then_inc(loaded[u], 16)
            with sp.Fori(1, NT // 2) as i:
                for u in range(2):
                    sp.wait_ge(cast_done, 2 * i + u + 1)
                    sp.dma_start(raw[u][:], adj[cols(2 * i + u, P), :]).then_inc(loaded[u], 16)
            sp.wait_ge(kept, NT + 2)
            sp.dma_start(adjT_dram.rearrange("(t p) n -> p t n", p=P), adjT[:]).then_inc(stored, 16)
            sp.wait_ge(stored, 16)

        @block.vector
        def _(dve):
            dve.sem_inc(cast_done, 2)
            with dve.Fori(0, NT // 2) as i:
                for u in range(2):
                    dve.wait_ge(loaded[u], 16 * i + 16)
                    dve.wait_ge(turn_done, 2 * i + u + 1)
                    nc.vector.tensor_copy(cast[u][:], raw[u][:]).then_inc(cast_done, 1)

        @block.tensor
        def _(pe):
            pe.sem_inc(turn_done, 2)
            with pe.Fori(0, NT // 2) as i:
                for u in range(2):
                    pe.wait_ge(cast_done, 2 * i + u + 3)
                    pe.wait_ge(kept, 2 * i + u + 1)
                    for j in range(NT):
                        ins = nc.tensor.transpose(turned[u][:, j, :], cast[u][:, j * P:(j + 1) * P], c["id16"][:])
                    ins.then_inc(turn_done, 1)

        @block.scalar
        def _(act):
            act.sem_inc(kept, 2)
            with act.Fori(0, NT // 2) as i:
                for u in range(2):
                    act.wait_ge(turn_done, 2 * i + u + 3)
                    nc.scalar.copy(adjT[:, :, cols(2 * i + u, P)], turned[u][:]).then_inc(kept, 1)


def reload_adjacency(pr, c, adjT_dram):
    with pr.stage():
        loaded = pr.sem("loaded")
        block = pr.block()

        @block.sync
        def _(sp):
            sp.dma_start(c["adjT"][:], adjT_dram.rearrange("(t p) n -> p t n", p=P)).then_inc(loaded, 16)
            sp.wait_ge(loaded, 16)


def carry(pr, dst, src):
    with pr.stage():
        carried = pr.sem("carried_stored")
        block = pr.block()

        @block.sync
        def _(sp):
            sp.dma_start(dst, src).then_inc(carried, 16)
            sp.wait_ge(carried, 16)


def norm_and_turn(pr, c, x_dram, h_dram=None):
    nc = pr.nc
    f = {}
    x = pr.sb("x_all", [P, NT, D])
    h = [pr.sb(f"h{u}", [P, D]) for u in range(2)]
    hT = [pr.sb(f"hT{u}", [P, KC, P]) for u in range(2)]
    stats, mv, std = pr.sb("stats", [P, CHUNK, 6]), pr.sb("mv", [P, CHUNK, 2]), pr.sb("std", [P, CHUNK])
    mean, rstd = pr.sb("mean", [P, NT]), pr.sb("rstd", [P, NT])
    turned = pr.ps("hturned", [P, KC, P])
    x_loaded = pr.sem("x_loaded")
    mv_done, std_done, h_done = pr.sem("mv_done"), pr.sem("std_done"), pr.sem("h_done")
    turn_done, hT_done = pr.sem("turn_done"), pr.sem("hT_done")
    order, order2 = pr.sem("order"), pr.sem("order_stats")

    def load(sp, others):
        def chunk(q):
            sp.dma_start(x[:, cols(q, CHUNK), :], x_dram[cols(q, CHUNK * P), :].rearrange("(t p) n -> p t n", p=P)) \
                .then_inc(x_loaded, 16)

        chunk(0)
        others()
        with sp.Fori(1, NT // CHUNK) as q:
            sp.wait_ge(x_loaded, 16 * q)
            chunk(q)

    def dve_stats(dve, q):
        link = Link(dve, order2, q * 2)
        dve.wait_ge(x_loaded, 16 * q + 16)
        for v in range(CHUNK):
            ins = nc.vector.bn_stats(stats[:, v, :], x[:, CHUNK * q + v, :])
        link(ins)
        pr.passed(dve)
        for v in range(CHUNK):
            ins = nc.vector.bn_aggr(mv[:, v, :], stats[:, v, :])
        ins.then_inc(mv_done, 1)
        dve.wait_ge(mv_done, q + 1)
        nc.vector.tensor_copy(mean[:, cols(q, CHUNK)].unsqueeze(2), mv[:, :, 0:1])
        dve.wait_ge(std_done, q + 1)
        link(nc.vector.reciprocal(rstd[:, cols(q, CHUNK)], std[:]))

    def dve_norm(dve, i, u, h_used, h_stored=None):
        t = 2 * i + u
        link = Link(dve, order, t)
        dve.wait_ge(h_used, t + 1)
        if h_stored:
            dve.wait_ge(h_stored[u], 16 * i)
        link(nc.vector.tensor_scalar(h[u][:], x[:, t, :], mean[:, bass.ds(t, 1)], rstd[:, bass.ds(t, 1)],
                                     ALU.subtract, ALU.mult))
        nc.vector.tensor_scalar(h[u][:], h[u][:], 0.0, None, ALU.max).then_inc(h_done, 1)

    def act_std(act, q):
        act.wait_ge(mv_done, q + 1)
        nc.scalar.activation(std[:].unsqueeze(2), mv[:, :, 1:2], ACT.Sqrt, bias=c["eps"][:, 0:1]).then_inc(std_done, 1)

    def pe_turn(pe, i, u):
        pe.wait_ge(h_done, 2 * i + u + 3)
        pe.wait_ge(hT_done, 2 * i + u + 2)
        for k in range(KC):
            ins = nc.tensor.transpose(turned[:, k, :], h[u][:, k * P:(k + 1) * P], c["id32"][:])
        ins.then_inc(turn_done, 1)

    def act_hT(act, i, u, hT_used):
        act.wait_ge(turn_done, 2 * i + u + 3)
        act.wait_ge(hT_used, 2 * i + u + 1)
        nc.scalar.copy(hT[u][:], turned[:]).then_inc(hT_done, 1)

    f.update(x=x, h=h, hT=hT, h_done=h_done, turn_done=turn_done, hT_done=hT_done, std_done=std_done,
             load=load, dve_stats=dve_stats, dve_norm=dve_norm, act_std=act_std, pe_turn=pe_turn, act_hT=act_hT)
    return f


def heads_project(pr, c, x_dram, w, a1, a2, seq_dram, scores, H, DH):
    nc = pr.nc
    with pr.stage():
        f = norm_and_turn(pr, c, x_dram)
        wsb = pr.sb("w", [P, KC, D])
        arow = pr.sb("arow", [P, 2, D])
        seq = [pr.sb(f"seq{u}", [P, D]) for u in range(2)]
        prod = [pr.sb(f"prod{v}", [P, H, DH]) for v in range(2)]
        proj = [pr.ps(f"proj{u}", [P, D]) for u in range(2)]
        w_loaded, a_loaded = pr.sem("w_loaded"), pr.sem("a_loaded")
        proj_done, seq_done, scored = pr.sem("proj_done"), pr.sem("seq_done"), pr.sem("scored")
        stored = [pr.sem(f"stored{u}") for u in range(2)]
        order = pr.sem("order_scores")
        block = pr.block()

        @block.sync
        def _(sp):
            def weights():
                sp.dma_start(wsb[:], w.rearrange("(k p) n -> p k n", p=P)).then_inc(w_loaded, 16)
                for v, a in enumerate((a1, a2)):
                    sp.dma_start(arow[:, v, :], a.broadcast_to([P, D])).then_inc(a_loaded, 16)

            f["load"](sp, weights)

        @block.gpsimd
        def _(pool):
            with pool.Fori(0, NT // 2) as i:
                for u in range(2):
                    pool.wait_ge(seq_done, 2 * i + u + 3)
                    pool.dma_start(seq_dram[cols(2 * i + u, P), :], seq[u][:]).then_inc(stored[u], 16)
            for u in range(2):
                pool.wait_ge(stored[u], 16 * (NT // 2))

        @block.vector
        def _(dve):
            dve.sem_inc(f["h_done"], 2)
            dve.sem_inc(scored, 2)

            def score(i, u):
                t = 2 * i + u
                dve.wait_ge(a_loaded, 32)
                dve.wait_ge(seq_done, t + 3)
                link = Link(dve, order, t * 3)
                for v in range(2):
                    ins = nc.vector.tensor_tensor(prod[v][:].rearrange("p h d -> p (h d)"), seq[u][:],
                                                  arow[:, v, :], ALU.mult)
                    if v == 0:
                        ins.then_inc(order, 1)
                        link.k += 1
                    else:
                        link(ins)
                nc.vector.tensor_reduce(scores[:, 0, t, :], prod[0][:], AX.X, ALU.add)
                link(nc.vector.tensor_reduce(scores[:, 1, t, :], prod[1][:], AX.X, ALU.add))
                dve.sem_inc(scored, 1)

            in_chunks(dve, 2, lambda q: f["dve_stats"](dve, q), lambda i, u: f["dve_norm"](dve, i, u, f["turn_done"]), score)

        @block.tensor
        def _(pe):
            pe.sem_inc(f["turn_done"], 2)
            pe.sem_inc(proj_done, 2)

            def project(i, u):
                t = 2 * i + u
                pe.wait_ge(w_loaded, 16)
                pe.wait_ge(f["hT_done"], t + 3)
                pe.wait_ge(seq_done, t + 1)
                for k in range(KC):
                    ins = nc.tensor.matmul(proj[u][:], f["hT"][u][:, k, :], wsb[:, k, :],
                                           start=(k == 0), stop=(k == KC - 1))
                ins.then_inc(proj_done, 1)

            one_ahead(pe, lambda i, u: f["pe_turn"](pe, i, u), project)

        @block.scalar
        def _(act):
            act.sem_inc(f["hT_done"], 2)
            act.sem_inc(seq_done, 2)

            def copy_out(i, u):
                t = 2 * i + u
                act.wait_ge(proj_done, t + 3)
                act.wait_ge(scored, t + 1)
                act.wait_ge(stored[u], 16 * i)
                nc.scalar.copy(seq[u][:], proj[u][:]).then_inc(seq_done, 1)

            in_chunks(act, 1, lambda q: f["act_std"](act, q), lambda i, u: f["act_hT"](act, i, u, proj_done), copy_out)


STEEP = 2.0 ** 60


def heads_factors(pr, c, scores, fac, arow_dram, H):
    nc = pr.nc
    with pr.stage():
        top = pr.sb("top", [P, H])
        top_all = pr.sb("top_all", [P, H])
        work = [pr.sb(f"work{v}", [P, NT, H]) for v in range(3)]
        rows = pr.sb("rows", [H, N])
        turned = pr.ps("turned", [H, NT, P])
        order, top_done, all_done = pr.sem("order"), pr.sem("top_done"), pr.sem("all_done")
        turn_done, rows_done, stored = pr.sem("turn_done"), pr.sem("rows_done"), pr.sem("stored")
        a, b = scores[:, 0], scores[:, 1]
        wide = top_all[:].unsqueeze(1).broadcast_to([P, NT, H])
        block = pr.block()

        @block.vector
        def _(dve):
            link = Link(dve, order)
            nc.vector.tensor_reduce(top[:], b.rearrange("p t h -> p h t"), AX.X, ALU.max).then_inc(top_done, 1)
            nc.vector.tensor_scalar(fac[:, 4], b, -1.0, None, ALU.mult)
            nc.vector.tensor_scalar(fac[:, 5], b, STEEP, None, ALU.mult)
            dve.wait_ge(all_done, 1)
            nc.vector.tensor_tensor(work[0][:], b, wide, ALU.subtract).then_inc(order, 1)
            link.k += 1
            link(nc.vector.tensor_tensor(work[1][:], a, wide, ALU.add))
            link(nc.vector.tensor_scalar(work[2][:], work[1][:], 0.0, None, ALU.min))
            link(nc.vector.tensor_scalar(work[1][:], work[1][:], 0.0, None, ALU.max))

        @block.gpsimd
        def _(pool):
            pool.wait_ge(top_done, 1)
            nc.gpsimd.partition_all_reduce(top_all[:], top[:], P, bass.bass_isa.ReduceOp.max).then_inc(all_done, 1)

        @block.tensor
        def _(pe):
            for t in range(NT):
                ins = nc.tensor.transpose(turned[:, t, :], scores[:, 0, t, :], c["id32"][:])
            ins.then_inc(turn_done, 1)

        @block.scalar
        def _(act):
            act.wait_ge(order, 4)
            nc.scalar.activation(fac[:, 0], work[0][:], ACT.Exp)
            nc.scalar.activation(fac[:, 1], work[0][:], ACT.Exp, scale=0.2)
            nc.scalar.activation(fac[:, 2], work[2][:], ACT.Exp, scale=0.8)
            nc.scalar.activation(fac[:, 3], work[1][:], ACT.Exp, scale=-0.8)
            act.wait_ge(turn_done, 1)
            nc.scalar.copy(rows[:], turned[:].rearrange("h t p -> h (t p)")).then_inc(rows_done, 1)

        @block.sync
        def _(sp):
            sp.wait_ge(rows_done, 1)
            sp.dma_start(arow_dram[0:H, :], rows[:]).then_inc(stored, 16)
            sp.wait_ge(stored, 16)


def heads_attend(pr, c, fac, seq_dram, arow_dram, hid_dram, H, DH, g, HG):
    nc = pr.nc
    adjT = c["adjT"]
    W = DH + 1
    CG = HG * DH
    per = 512 // (2 * W)
    banks = -(-NT // per)
    h0 = g * HG
    with pr.stage():
        R = pr.sb("R", [P, NT, PARTS, HG * 2 * W], BF16)
        T = pr.sb("T", [P, NT, HG, W])

        with ExitStack() as split:
            rest = [split.enter_context(nc.sbuf_tensor(f"split{b}_{pr.n}", [P, HG, 2, W], F32)) for b in range(4)]
            seq = [split.enter_context(nc.sbuf_tensor(f"seq{b}_{pr.n}", [P, HG, DH], F32)) for b in range(4)]
            loaded, rest_done, hi_done = ([pr.sem(f"{n}{b}") for b in range(4)] for n in ("loaded", "rest_done", "hi_done"))
            STEPS = 1 + PARTS
            HALF = 8
            total = [split.enter_context(nc.psum_tensor(f"total{k}_{pr.n}", [P, HG * W], F32)) for k in range(HALF)]
            total_done, T_done = pr.sem("total_done"), pr.sem("T_done")
            R5 = R[:].rearrange("p t s (h v w) -> p t s h v w", v=2, w=W)
            with nc.Block() as block:
                @block.sync
                def _(sp):
                    def load(i, b):
                        sp.dma_start(seq[b][:], seq_dram[cols(4 * i + b, P), g * CG:(g + 1) * CG]
                                     .rearrange("p (h d) -> p h d", d=DH)).then_inc(loaded[b], 16)

                    for b in range(4):
                        load(0, b)
                    with sp.Fori(1, NT // 4) as i:
                        for b in range(4):
                            sp.wait_ge(rest_done[b], (i - 1) * STEPS + 2)
                            load(i, b)

                @block.vector
                def _(dve):
                    with dve.Fori(0, NT // 4) as i:
                        for pair in ((0, 1), (2, 3)):
                            for b in pair:
                                t = 4 * i + b
                                dve.wait_ge(loaded[b], 16 * i + 16)
                                dve.wait_ge(hi_done[b], i * PARTS)
                                factor = fac[:, 0:2, t, h0:h0 + HG].rearrange("p v h -> p h v").unsqueeze(3)
                                nc.vector.tensor_tensor(rest[b][:, :, :, 0:DH],
                                                        seq[b][:].unsqueeze(2).broadcast_to([P, HG, 2, DH]),
                                                        factor.broadcast_to([P, HG, 2, DH]), ALU.mult).then_inc(rest_done[b], 1)
                                nc.vector.tensor_copy(rest[b][:, :, :, DH:W], factor).then_inc(rest_done[b], 1)
                            for p in range(1, PARTS):
                                for b in pair:
                                    dve.wait_ge(hi_done[b], i * PARTS + p)
                                    nc.vector.tensor_tensor(rest[b][:].rearrange("p h v w -> p (h v w)"),
                                                            rest[b][:].rearrange("p h v w -> p (h v w)"),
                                                            R[:, 4 * i + b, p - 1, :], ALU.subtract).then_inc(rest_done[b], 1)

                @block.scalar
                def _(act):
                    act.sem_inc(T_done, HALF)
                    with act.Fori(0, NT // 4) as i:
                        for pair in ((0, 1), (2, 3)):
                            for p in range(PARTS):
                                for b in pair:
                                    act.wait_ge(rest_done[b], i * STEPS + 2 + p)
                                    nc.scalar.copy(R[:, 4 * i + b, p, :], rest[b][:].rearrange("p h v w -> p (h v w)")) \
                                        .then_inc(hi_done[b], 1)
                    with act.Fori(0, NT // HALF) as half:
                        for k in range(HALF):
                            act.wait_ge(total_done, half * HALF + k + 1)
                            nc.scalar.copy(T[:, HALF * half + k].rearrange("p h w -> p (h w)"), total[k][:]).then_inc(T_done, 1)

                @block.tensor
                def _(pe):
                    with pe.Fori(0, NT // HALF) as half:
                        for k in range(HALF):
                            pe.wait_ge(T_done, half * HALF + k + 1)
                            nc.tensor.matmul(total[k][:], c["zero16"][:, 0:P], c["zero16"][:, 0:HG * W],
                                             start=True, stop=False, skip_group_check=True)
                        with pe.Fori(0, NT // 4) as i:
                            for b in range(4):
                                pe.wait_ge(hi_done[b], i * PARTS + PARTS)
                                for k in range(HALF):
                                    for p in range(PARTS):
                                        nc.tensor.matmul(total[k][:].rearrange("p (h w) -> p h w", w=W),
                                                         adjT[:, 4 * i + b, cols(HALF * half + k, P)],
                                                         R5[:, 4 * i + b, p, :, 1, :],
                                                         start=False, stop=False, skip_group_check=True)
                        for k in range(HALF):
                            nc.tensor.matmul(total[k][:], c["zero16"][:, 0:P], c["zero16"][:, 0:HG * W],
                                             start=False, stop=True, skip_group_check=True).then_inc(total_done, 1)

        NM = 8
        BY_ACT = [j for j in range(NT) if j % 4 != 3]
        LEAD = 4
        arow = [pr.sb(f"arow{u}", [P, N]) for u in range(2)]
        M = [pr.sb(f"M{m}", [P, N], BF16) for m in range(NM)]
        S = pr.sb("S", [P, NT, 2, W])
        q = pr.sb("q", [P, NT, W])
        den = pr.sb("den", [P, NT, 1])
        acc = [pr.ps(f"acc{k}", [P, per, 2, W]) for k in range(banks)]
        a_loaded = [pr.sem(f"a_loaded{u}") for u in range(2)]
        raw_done, mask_done, mask_used = pr.sem("raw_done"), pr.sem("mask_done"), pr.sem("mask_used")
        sums_done, sums_read, mixed = pr.sem("sums_done"), pr.sem("sums_read"), pr.sem("mixed")
        order = pr.sem("order_mix")
        block = pr.block()
        hid_stored = pr.sem("hid_stored")

        def in_heads(eng, start, rest, end):
            start(0, 0)
            with eng.Fori(0, HG // 2 - 1) as i:
                rest(2 * i, 0)
                start(2 * i + 1, 1)
                end(2 * i)
                rest(2 * i + 1, 1)
                start(2 * i + 2, 0)
                end(2 * i + 1)
            rest(HG - 2, 0)
            start(HG - 1, 1)
            end(HG - 2)
            rest(HG - 1, 1)
            end(HG - 1)

        def loads_of(h, u):
            return 8 * h + 16 - 8 * u

        @block.sync
        def _(sp):
            for u in range(2):
                sp.dma_start(arow[u][:], arow_dram[h0 + u:h0 + u + 1, :].broadcast_to([P, N])).then_inc(a_loaded[u], 16)

            def store(h):
                sp.wait_ge(mixed, h + 1)
                sp.dma_start(hid_dram.rearrange("(t p) n -> p t n", p=P)[:, :, cols(h + h0, DH)],
                             T[:, :, bass.ds(h, 1), 0:DH].rearrange("p t h w -> p t (h w)")).then_inc(hid_stored, 16)

            with sp.Fori(0, HG // 2 - 1) as i:
                for u in range(2):
                    h = 2 * i + u
                    sp.wait_ge(mask_done, (h + 1) * NT)
                    sp.dma_start(arow[u][:], arow_dram[bass.ds(h + h0 + 2, 1), :].broadcast_to([P, N])) \
                        .then_inc(a_loaded[u], 16)
                    store(h)
            store(HG - 2)
            store(HG - 1)
            sp.wait_ge(hid_stored, 16 * HG)

        @block.vector
        def _(dve):
            def masks(h, u, js):
                for j in js:
                    if j in BY_ACT:
                        dve.wait_ge(raw_done, h * len(BY_ACT) + BY_ACT.index(j) + 1)
                        ins = nc.vector.tensor_tensor(M[j % NM][:], M[j % NM][:], adjT[:, j, :], ALU.min)
                    else:
                        dve.wait_ge(mask_used, h * NT + j + 1)
                        ins = nc.vector.scalar_tensor_tensor(out=M[j % NM][:], in0=arow[u][:],
                                                             scalar=fac[:, 4, j, bass.ds(h0 + h, 1)],
                                                             in1=adjT[:, j, :], op0=ALU.is_gt, op1=ALU.mult)
                    ins.then_inc(mask_done, 1)

            def start(h, u):
                dve.wait_ge(a_loaded[u], loads_of(h, u))
                masks(h, u, range(LEAD))

            def rest(h, u):
                masks(h, u, range(LEAD, NT))

            def mix(h):
                dve.wait_ge(sums_read, (h + 2) * banks)
                link = Link(dve, order, h * 5)
                Th = T[:, :, bass.ds(h, 1), :].rearrange("p t h w -> p t (h w)")
                link(nc.vector.tensor_tensor(q[:], Th, S[:, :, 1, :], ALU.subtract))
                nc.vector.tensor_tensor(q[:], q[:], fac[:, 3, :, bass.ds(h0 + h, 1)].broadcast_to([P, NT, W]),
                                        ALU.mult).then_inc(order, 1)
                link.k += 1
                link(nc.vector.tensor_tensor(S[:, :, 0, :], S[:, :, 0, :],
                                             fac[:, 2, :, bass.ds(h0 + h, 1)].broadcast_to([P, NT, W]), ALU.mult))
                link(nc.vector.tensor_tensor(q[:], q[:], S[:, :, 0, :], ALU.add))
                link(nc.vector.reciprocal(den[:], q[:, :, DH:W]))
                nc.vector.tensor_tensor(Th[:, :, 0:DH], q[:, :, 0:DH], den[:].broadcast_to([P, NT, DH]), ALU.mult) \
                    .then_inc(mixed, 1)
                dve.wait_ge(mixed, h + 1)

            in_heads(dve, start, rest, mix)

        @block.tensor
        def _(pe):
            pe.sem_inc(mask_used, NM)
            with pe.Fori(0, HG) as h:
                for k in range(banks):
                    pe.wait_ge(sums_read, h * banks + k + 1)
                    nc.tensor.matmul(acc[k][:].rearrange("p i v w -> p (i v w)"), c["zero16"][:, 0:P],
                                     c["zero16"][:, 0:per * 2 * W], start=True, stop=False, skip_group_check=True)
                with pe.Fori(0, NT // NM) as jq:
                    for m in range(NM):
                        j = NM * jq + m
                        pe.wait_ge(mask_done, h * NT + j + 1)
                        for t in range(NT):
                            for p in range(PARTS):
                                ins = nc.tensor.matmul(acc[t // per][:, t % per].rearrange("p v w -> p (v w)"),
                                                       M[m][:, t * P:(t + 1) * P],
                                                       R[:, bass.ds(j, 1), p, cols(h, 2 * W)].rearrange("p t w -> p (t w)"),
                                                       start=False, stop=False, skip_group_check=True)
                        ins.then_inc(mask_used, 1)
                for k in range(banks):
                    nc.tensor.matmul(acc[k][:].rearrange("p i v w -> p (i v w)"), c["zero16"][:, 0:P],
                                     c["zero16"][:, 0:per * 2 * W], start=False, stop=True,
                                     skip_group_check=True).then_inc(sums_done, 1)

        @block.scalar
        def _(act):
            def raw(h, u, js):
                for j in js:
                    if j in BY_ACT:
                        act.wait_ge(mask_used, h * NT + j + 1)
                        nc.scalar.activation(M[j % NM][:], arow[u][:], ACT.Relu,
                                             bias=fac[:, 5, j, bass.ds(h0 + h, 1)], scale=STEEP).then_inc(raw_done, 1)

            def start(h, u):
                act.wait_ge(a_loaded[u], loads_of(h, u))
                raw(h, u, range(LEAD))

            def rest(h, u):
                raw(h, u, range(LEAD, NT))

            def copy_sums(h):
                act.wait_ge(mixed, h)
                for k in range(banks):
                    n = min(per, NT - k * per)
                    act.wait_ge(sums_done, h * banks + k + 1)
                    nc.scalar.copy(S[:, k * per:k * per + n], acc[k][:, 0:n]).then_inc(sums_read, 1)

            act.sem_inc(sums_read, banks)
            in_heads(act, start, rest, copy_sums)


def tile_loads(pr, sp_loads):
    def run(eng, freed):
        for u in range(2):
            for buf, src, sem in sp_loads:
                eng.dma_start(buf[u][:], src(u)).then_inc(sem[u], 16)
        with eng.Fori(1, NT // 2) as i:
            for u in range(2):
                for s in freed:
                    eng.wait_ge(s, 2 * i + u + 1)
                for buf, src, sem in sp_loads:
                    eng.dma_start(buf[u][:], src(2 * i + u)).then_inc(sem[u], 16)
    return run


def pair_loads(pr, sp, *loads):
    with sp.Fori(0, NT // 2) as i:
        for buf, src, sem in loads:
            sp.wait_ge(sem, 16 * i)
            pr.passed(sp)
            sp.dma_start(buf[:, cols(i, 2), :], src[cols(i, 2 * P), :].rearrange("(t p) n -> p t n", p=P)).then_inc(sem, 16)


def heads_out(pr, c, hid_dram, x_dram, out_dram, w, brow):
    nc = pr.nc
    with pr.stage():
        wsb, bsb = pr.sb("w", [P, KC, D]), pr.sb("b", [P, D])
        x = pr.sb("x", [P, NT, D])
        hid, y, low, e = ([pr.sb(f"{n}{u}", [P, D]) for u in range(2)] for n in ("hid", "y", "low", "e"))
        hT = [pr.sb(f"hT{u}", [P, KC, P]) for u in range(2)]
        turned = pr.ps("turned", [P, KC, P])
        prod = [pr.ps(f"prod{u}", [P, D]) for u in range(2)]
        w_loaded = pr.sem("w_loaded")
        x_loaded = pr.sem("x_loaded")
        hid_loaded, stored = ([pr.sem(f"{n}{u}") for u in range(2)] for n in ("hid_loaded", "stored"))
        turn_done, hT_done, prod_done, low_done, e_done, out_done, order, order2 = (
            pr.sem(n) for n in ("turn_done", "hT_done", "prod_done", "low_done", "e_done", "out_done", "order", "order_sum"))
        block = pr.block()

        @block.sync
        def _(sp):
            sp.dma_start(wsb[:], w.rearrange("(k p) n -> p k n", p=P)).then_inc(w_loaded, 16)
            sp.dma_start(bsb[:], brow.broadcast_to([P, D])).then_inc(w_loaded, 16)
            with sp.Fori(0, NT // 2) as i:
                for u in range(2):
                    sp.wait_ge(turn_done, 2 * i + u + 1)
                    sp.dma_start(hid[u][:], hid_dram[cols(2 * i + u, P), :]).then_inc(hid_loaded[u], 16)
                sp.wait_ge(x_loaded, 16 * i)
                pr.passed(sp)
                sp.dma_start(x[:, cols(i, 2), :], x_dram[cols(i, 2 * P), :].rearrange("(t p) n -> p t n", p=P)) \
                    .then_inc(x_loaded, 16)

        @block.gpsimd
        def _(pool):
            with pool.Fori(0, NT // 2) as i:
                for u in range(2):
                    pool.wait_ge(out_done, 2 * i + u + 3)
                    pool.dma_start(out_dram[cols(2 * i + u, P), :], y[u][:]).then_inc(stored[u], 16)
            for u in range(2):
                pool.wait_ge(stored[u], 16 * (NT // 2))

        @block.tensor
        def _(pe):
            pe.sem_inc(turn_done, 2)
            pe.sem_inc(prod_done, 2)
            pe.wait_ge(w_loaded, 32)

            def turn(i, u):
                pe.wait_ge(hid_loaded[u], 16 * i + 16)
                pe.wait_ge(hT_done, 2 * i + u + 2)
                for k in range(KC):
                    ins = nc.tensor.transpose(turned[:, k, :], hid[u][:, k * P:(k + 1) * P], c["id32"][:])
                ins.then_inc(turn_done, 1)

            def product(i, u):
                t = 2 * i + u
                pe.wait_ge(hT_done, t + 3)
                pe.wait_ge(low_done, t + 1)
                for k in range(KC):
                    ins = nc.tensor.matmul(prod[u][:], hT[u][:, k, :], wsb[:, k, :], start=(k == 0), stop=(k == KC - 1))
                ins.then_inc(prod_done, 1)

            one_ahead(pe, turn, product)

        @block.scalar
        def _(act):
            act.sem_inc(hT_done, 2)
            act.sem_inc(e_done, 2)

            def copy_out(i, u):
                act.wait_ge(turn_done, 2 * i + u + 3)
                act.wait_ge(prod_done, 2 * i + u + 1)
                nc.scalar.copy(hT[u][:], turned[:]).then_inc(hT_done, 1)

            def exps(i, u):
                act.wait_ge(low_done, 2 * i + u + 3)
                act.wait_ge(out_done, 2 * i + u + 1)
                nc.scalar.activation(e[u][:], low[u][:], ACT.Exp).then_inc(e_done, 1)

            one_ahead(act, copy_out, exps)

        @block.vector
        def _(dve):
            dve.sem_inc(low_done, 2)
            dve.sem_inc(out_done, 2)
            dve.wait_ge(w_loaded, 32)

            def parts(i, u):
                t = 2 * i + u
                link = Link(dve, order, t * 2)
                dve.wait_ge(prod_done, t + 3)
                dve.wait_ge(stored[u], 16 * i)
                dve.wait_ge(e_done, t + 1)
                link(nc.vector.tensor_tensor(y[u][:], prod[u][:], bsb[:], ALU.add))
                nc.vector.tensor_scalar(low[u][:], y[u][:], 0.0, None, ALU.min).then_inc(low_done, 1)
                link(nc.vector.tensor_scalar(y[u][:], y[u][:], 0.0, None, ALU.max))

            def result(i, u):
                t = 2 * i + u
                link = Link(dve, order2, t)
                dve.wait_ge(e_done, t + 3)
                link(nc.vector.scalar_tensor_tensor(out=y[u][:], in0=e[u][:], scalar=-1.0, in1=y[u][:],
                                                    op0=ALU.add, op1=ALU.add))
                dve.wait_ge(x_loaded, 16 * i + 16)
                nc.vector.tensor_tensor(y[u][:], y[u][:], x[:, t, :], ALU.add).then_inc(out_done, 1)

            one_ahead(dve, parts, result)


def features_keys(pr, c, x_dram, h_dram, w1, w2, w3, QW, K):
    nc = pr.nc
    with pr.stage():
        f = norm_and_turn(pr, c, x_dram)
        w1s, w3s, w2s = pr.sb("w1", [P, KC, 64]), pr.sb("w3", [P, KC, 64]), pr.sb("w2", [64, 64])
        qT = pr.sb("qT", [64, P])
        kq = pr.ps("kq", [64, 2, P])
        qw = pr.ps("qw", [64, P])
        w_loaded = pr.sem("w_loaded")
        stored = [pr.sem(f"stored{u}") for u in range(2)]
        kq_done, q_done, qw_done, copied = (pr.sem(n) for n in ("kq_done", "q_done", "qw_done", "copied"))
        block = pr.block()

        @block.sync
        def _(sp):
            def weights():
                sp.dma_start(w1s[:], w1.rearrange("(k p) n -> p k n", p=P)).then_inc(w_loaded, 16)
                sp.dma_start(w3s[:], w3.rearrange("(k p) n -> p k n", p=P)).then_inc(w_loaded, 16)
                sp.dma_start(w2s[:], w2).then_inc(w_loaded, 16)

            f["load"](sp, weights)

        @block.gpsimd
        def _(pool):
            with pool.Fori(0, NT // 2) as i:
                for u in range(2):
                    pool.wait_ge(f["h_done"], 2 * i + u + 3)
                    pool.dma_start(h_dram[cols(2 * i + u, P), :], f["h"][u][:]).then_inc(stored[u], 16)
            for u in range(2):
                pool.wait_ge(stored[u], 16 * (NT // 2))

        @block.vector
        def _(dve):
            dve.sem_inc(f["h_done"], 2)
            in_chunks(dve, 2, lambda q: f["dve_stats"](dve, q),
                      lambda i, u: f["dve_norm"](dve, i, u, f["turn_done"], stored), lambda i, u: None)

        @block.tensor
        def _(pe):
            pe.sem_inc(f["turn_done"], 2)
            pe.sem_inc(kq_done, 2)

            def product(i, u):
                t = 2 * i + u
                pe.wait_ge(w_loaded, 48)
                pe.wait_ge(f["hT_done"], t + 3)
                pe.wait_ge(copied, t)
                for v, ws in enumerate((w3s, w1s)):
                    for k in range(KC):
                        ins = nc.tensor.matmul(kq[:, v, :], ws[:, k, :], f["hT"][u][:, k, :],
                                               start=(k == 0), stop=(k == KC - 1))
                ins.then_inc(kq_done, 1)
                pe.wait_ge(q_done, t + 1)
                pr.passed(pe)
                nc.tensor.matmul(qw[:], w2s[:], qT[:], start=True, stop=True).then_inc(qw_done, 1)

            one_ahead(pe, lambda i, u: f["pe_turn"](pe, i, u), product)

        @block.scalar
        def _(act):
            act.sem_inc(f["hT_done"], 2)

            def copy_out(i, u):
                t = 2 * i + u
                act.wait_ge(kq_done, t + 3)
                nc.scalar.copy(qT[:], kq[:, 1, :]).then_inc(q_done, 1)
                nc.scalar.copy(K[:, cols(t, P)], kq[:, 0, :])
                act.wait_ge(qw_done, t + 1)
                nc.scalar.copy(QW[:, cols(t, P)], qw[:]).then_inc(copied, 1)

            in_chunks(act, 1, lambda q: f["act_std"](act, q), lambda i, u: f["act_hT"](act, i, u, kq_done), copy_out)


def walk(pr, c, s, xf_dram, xf_new, z_dram, z_new, u1):
    nc = pr.nc
    adjT = c["adjT"]
    LAG = 1
    with pr.stage():
        XP = pr.sb("XP", [P, NT, PARTS, D], BF16)
        rest = [pr.sb(f"rest{b}", [P, D]) for b in range(4)]
        loaded, rest_done, cast_done = ([pr.sem(f"{n}{b}") for b in range(4)] for n in ("loaded", "rest_done", "cast_done"))
        usb = pr.sb("u1", [P, KC, D])
        xf, z, new, zo = ([pr.sb(f"{n}{u}", [P, D]) for u in range(2)] for n in ("xf", "z", "new", "zo"))
        nT = [pr.sb(f"nT{u}", [P, KC, P]) for u in range(2)]
        inv = [pr.sb(f"inv{u}", [P, 1]) for u in range(2)]
        acc = [pr.ps(f"acc{b}", [P, D]) for b in range(4)]
        deg = [pr.ps(f"deg{u}", [P, 2, 2]) for u in range(2)]
        turned = pr.ps("turned", [P, KC, P])
        prod = pr.ps("prod", [P, D])
        u_loaded = pr.sem("u_loaded")
        xf_loaded, z_loaded, n_stored, z_stored = ([pr.sem(f"{n}{u}") for u in range(2)]
                                                   for n in ("xf_loaded", "z_loaded", "n_stored", "z_stored"))
        acc_done, new_done, turn_done, nT_done, prod_done, z_done, order = (
            pr.sem(n) for n in ("acc_done", "new_done", "turn_done", "nT_done", "prod_done", "z_done", "order_walk"))
        block = pr.block()

        @block.sync
        def _(sp):
            for b in range(4):
                sp.dma_start(rest[b][:], xf_dram[cols(b, P), :]).then_inc(loaded[b], 16)
            with sp.Fori(1, NT // 4) as i:
                for b in range(4):
                    sp.wait_ge(cast_done[b], i * PARTS)
                    sp.dma_start(rest[b][:], xf_dram[cols(4 * i + b, P), :]).then_inc(loaded[b], 16)
            sp.dma_start(usb[:], u1.rearrange("(k p) n -> p k n", p=P)).then_inc(u_loaded, 16)
            tile_loads(pr, [(xf, lambda t: xf_dram[cols(t, P), :], xf_loaded),
                            (z, lambda t: z_dram[cols(t, P), :], z_loaded)])(sp, [new_done, z_done])

        @block.gpsimd
        def _(pool):
            with pool.Fori(0, NT // 2) as i:
                for u in range(2):
                    t = 2 * i + u
                    pool.wait_ge(new_done, t + 3)
                    pool.dma_start(xf_new[cols(t, P), :], new[u][:]).then_inc(n_stored[u], 16)
                    pool.wait_ge(z_done, t + 3)
                    pr.passed(pool)
                    pool.dma_start(z_new[cols(t, P), :], zo[u][:]).then_inc(z_stored[u], 16)
            for u in range(2):
                pool.wait_ge(n_stored[u], 16 * (NT // 2))
                pool.wait_ge(z_stored[u], 16 * (NT // 2))

        @block.tensor
        def _(pe):
            def first_products():
                for b in range(4):
                    nc.tensor.matmul(acc[b][:], c["zero16"][:, 0:P], c["zero16"][:], start=True, stop=False, skip_group_check=True)
                for u in range(2):
                    nc.tensor.matmul(deg[u][:].rearrange("p i v -> p (i v)"), c["zero16"][:, 0:P], c["zero16"][:, 0:4],
                                     start=True, stop=False, skip_group_check=True)
                with pe.Fori(0, NT // 4) as i:
                    for j in range(4):
                        pe.wait_ge(cast_done[j], i * PARTS + PARTS)
                        for b in range(4):
                            lhs = adjT[:, 4 * i + j, b * P:(b + 1) * P]
                            nc.tensor.matmul(deg[b % 2][:, b // 2, :], lhs, c["ones16"][:], start=False, stop=False,
                                             skip_group_check=True)
                            for p in range(PARTS):
                                nc.tensor.matmul(acc[b][:], lhs, XP[:, 4 * i + j, p, :], start=False, stop=False,
                                                 skip_group_check=True)
                for u in range(2):
                    nc.tensor.matmul(deg[u][:].rearrange("p i v -> p (i v)"), c["zero16"][:, 0:P], c["zero16"][:, 0:4],
                                     start=False, stop=True, skip_group_check=True)
                for b in range(4):
                    nc.tensor.matmul(acc[b][:], c["zero16"][:, 0:P], c["zero16"][:], start=False, stop=True,
                                     skip_group_check=True).then_inc(acc_done, 1)

            def product(i, b):
                t = 4 * i + b
                pe.wait_ge(new_done, t + 1)
                for j in range(NT):
                    lhs = adjT[:, j, cols(t, P)]
                    nc.tensor.matmul(deg[b % 2][:, b // 2, :], lhs, c["ones16"][:], start=(j == 0), stop=(j == NT - 1))
                    for p in range(PARTS):
                        ins = nc.tensor.matmul(acc[b][:], lhs, XP[:, j, p, :], start=(j + p == 0),
                                               stop=(j == NT - 1 and p == PARTS - 1))
                ins.then_inc(acc_done, 1)

            def project(t, u):
                pe.wait_ge(new_done, t + 3)
                pe.wait_ge(nT_done, t + 2)
                for k in range(KC):
                    ins = nc.tensor.transpose(turned[:, k, :], new[u][:, k * P:(k + 1) * P], c["id32"][:])
                ins.then_inc(turn_done, 1)
                pe.wait_ge(nT_done, t + 3)
                pe.wait_ge(z_done, t + 2)
                for k in range(KC):
                    ins = nc.tensor.matmul(prod[:], nT[u][:, k, :], usb[:, k, :], start=(k == 0), stop=(k == KC - 1))
                ins.then_inc(prod_done, 1)

            pe.sem_inc(turn_done, 2)
            pe.sem_inc(prod_done, 2)
            first_products()
            pe.wait_ge(u_loaded, 16)
            for t in range(4 - LAG):
                project(t, t % 2)
            with pe.Fori(1, NT // 4) as i:
                for b in range(4):
                    product(i, b)
                    project(4 * i + b - LAG, (b - LAG) % 2)
            for t in range(NT - LAG, NT):
                project(t, t % 2)

        @block.scalar
        def _(act):
            with act.Fori(0, NT // 4) as i:
                for pair in ((0, 1), (2, 3)):
                    for p in range(PARTS):
                        for b in pair:
                            if p:
                                act.wait_ge(rest_done[b], i * (PARTS - 1) + p)
                            else:
                                act.wait_ge(loaded[b], 16 * i + 16)
                            nc.scalar.copy(XP[:, 4 * i + b, p, :], rest[b][:]).then_inc(cast_done[b], 1)
            act.sem_inc(nT_done, 2)
            with act.Fori(0, NT // 2) as i:
                for u in range(2):
                    t = 2 * i + u
                    act.wait_ge(turn_done, t + 3)
                    act.wait_ge(prod_done, t + 1)
                    nc.scalar.copy(nT[u][:], turned[:]).then_inc(nT_done, 1)

        @block.vector
        def _(dve):
            with dve.Fori(0, NT // 4) as i:
                for pair in ((0, 1), (2, 3)):
                    for p in range(1, PARTS):
                        for b in pair:
                            dve.wait_ge(cast_done[b], i * PARTS + p)
                            nc.vector.tensor_tensor(rest[b][:], rest[b][:], XP[:, 4 * i + b, p - 1, :],
                                                    ALU.subtract).then_inc(rest_done[b], 1)
            dve.sem_inc(new_done, 2)
            dve.sem_inc(z_done, 2)
            with dve.Fori(0, NT // 4) as i:
                for b in range(4):
                    t, u = 4 * i + b, b % 2
                    link = Link(dve, order, t * 3)
                    dve.wait_ge(acc_done, t + 1)
                    link(nc.vector.tensor_scalar(inv[u][:], deg[u][:, b // 2, 0:1], 1.0, 1e-12, ALU.add, ALU.max))
                    link(nc.vector.reciprocal(inv[u][:], inv[u][:]))
                    dve.wait_ge(xf_loaded[u], 32 * i + 16 * (b // 2) + 16)
                    dve.wait_ge(n_stored[u], 32 * i + 16 * (b // 2))
                    dve.wait_ge(turn_done, t + 1)
                    link(nc.vector.tensor_tensor(new[u][:], acc[b][:], xf[u][:], ALU.add))
                    nc.vector.tensor_scalar(new[u][:], new[u][:], inv[u][:, 0:1], None, ALU.mult).then_inc(new_done, 1)
                    dve.wait_ge(prod_done, t + 3)
                    dve.wait_ge(z_loaded[u], 32 * i + 16 * (b // 2) + 16)
                    dve.wait_ge(z_stored[u], 32 * i + 16 * (b // 2))
                    nc.vector.tensor_tensor(zo[u][:], prod[:], z[u][:], ALU.add).then_inc(z_done, 1)


P_TOP = 0.9
ALL = 24
WIDTH = 9.94


def top_attention(pr, c, first, last, xa_dram, xa_new, z_dram, z_new, u2, QW, K, w1, w2, w3, QWn, Kn):
    nc = pr.nc
    G = 4
    NG = NT // G
    with pr.stage():
        Xa = pr.sb("Xa", [P, NT, D])
        E = [pr.sb(f"E{u}", [P, G, N]) for u in range(2)]
        below = [pr.sb(f"below{u}", [P, N]) for u in range(3)]
        junk = [below[k // 2][:].bitcast(BF16)[:, (k % 2) * N:(k % 2 + 1) * N] for k in range(4)]
        WT = [pr.sb(f"WT{u}", [P, NT, P]) for u in range(2)]
        usb = pr.sb("u2", [P, KC, D])
        w1s, w3s, w2s = pr.sb("w1", [P, KC, 64]), pr.sb("w3", [P, KC, 64]), pr.sb("w2", [64, 64])
        qs = [pr.sb(f"qs{u}", [64, P]) for u in range(G)]
        qT = pr.sb("qT", [64, P])
        ratio = pr.sb("ratio", [P, ALL])
        mx, nmx, S, goal, lo, th, F, hit, kept, low_sum, unres, thr = (
            pr.sb(n, [P, G]) for n in ("mx", "nmx", "S", "goal", "lo", "th", "F", "hit", "kept", "low_sum", "unres", "thr"))
        inv = [pr.sb(f"inv{u}", [P, G]) for u in range(2)]
        top8, sum8a, sum8b, in8 = (pr.sb(n, [P, G, 8]) for n in ("top8", "sum8a", "sum8b", "in8"))
        flag, flagT = pr.sb("flag", [P, 32]), pr.sb("flagT", [P, 32])
        flag1, flag4 = pr.sb("flag1", [P, 1]), pr.sb("flag4", [1, 4])
        flagi = pr.sb("flagi", [1, 1], mybir.dt.int32)
        z, zo, new, ys = ([pr.sb(f"{n}{u}", [P, D]) for u in range(2)] for n in ("z", "zo", "new", "ys"))
        nT = pr.sb("nT", [P, KC, P])
        zps = pr.ps("zps", [P, N])
        tw = [pr.ps(f"tw{u}", [P, 4, P]) for u in range(2)]
        o = pr.ps("o", [P, D])
        y = pr.ps("y", [P, D])
        w_loaded, x_loaded, steps_set = pr.sem("w_loaded"), pr.sem("x_loaded"), pr.sem("steps_set")
        z_loaded, n_stored, z_stored = ([pr.sem(f"{n}{u}") for u in range(2)] for n in ("z_loaded", "n_stored", "z_stored"))
        (qs_done, logits_done, logits_kept, max_done, exp_done, masked, inv_done, order, order2, order3, order4, turn_done, quad_done,
         pv_done, new_done, y_done, ys_done, z_done, kq_done, q_done, qw_done, copied) = (pr.sem(n) for n in (
             "qs_done", "logits_done", "logits_kept", "max_done", "exp_done", "masked", "inv_done", "order_group",
             "order_rounds", "order_next8", "order_rest", "turn_done", "quad_done", "pv_done", "new_done", "y_done", "ys_done", "z_done",
             "kq_done", "q_done", "qw_done", "copied"))
        QUADS = NT // 4
        PLACES = G * (QUADS + 1)

        def weights_at(u, q):
            return q if u == 0 else (QUADS + 1) * u - 1 + q

        def result_at(u):
            return min(QUADS * (u + 2) + u, PLACES - 1)

        block = pr.block()

        def in_groups(eng, ahead, behind):
            ahead(0, 0)
            with eng.Fori(0, NG // 2 - 1) as i:
                ahead(2 * i + 1, 1)
                behind(2 * i, 0)
                ahead(2 * i + 2, 0)
                behind(2 * i + 1, 1)
            ahead(NG - 1, 1)
            behind(NG - 2, 0)
            behind(NG - 1, 1)

        @block.sync
        def _(sp):
            sp.dma_start(w1s[:], w1.rearrange("(k p) n -> p k n", p=P)).then_inc(w_loaded, 16)
            sp.dma_start(w3s[:], w3.rearrange("(k p) n -> p k n", p=P)).then_inc(w_loaded, 16)
            sp.dma_start(w2s[:], w2).then_inc(w_loaded, 16)
            sp.dma_start(usb[:], u2.rearrange("(k p) n -> p k n", p=P)).then_inc(w_loaded, 16)
            sp.dma_start(Xa[:], xa_dram.rearrange("(t p) n -> p t n", p=P)).then_inc(x_loaded, 16)
            tile_loads(pr, [(z, lambda t: z_dram[cols(t, P), :], z_loaded)])(sp, [z_done])

        @block.gpsimd
        def _(pool):
            for k in range(ALL):
                ins = nc.gpsimd.memset(ratio[:, k:k + 1], float(np.exp(WIDTH / 2 ** (k + 1))))
            nc.gpsimd.memset(flag[:], 0.0).then_inc(steps_set, 1)
            pool.sem_inc(z_done, 2)
            with pool.Fori(0, NT // 2) as i:
                for u in range(2):
                    t = 2 * i + u
                    pool.wait_ge(new_done, t + 3)
                    pool.dma_start(xa_new[cols(t, P), :], new[u][:]).then_inc(n_stored[u], 16)
                    pool.wait_ge(ys_done, t + 3)
                    pool.wait_ge(z_loaded[u], 16 * i + 16)
                    pool.wait_ge(z_stored[u], 16 * i)
                    nc.gpsimd.tensor_tensor(zo[u][:], ys[u][:], z[u][:], ALU.add).then_inc(z_done, 1)
                    pool.wait_ge(z_done, t + 3)
                    pr.passed(pool)
                    pool.dma_start(z_new[cols(t, P), :], zo[u][:]).then_inc(z_stored[u], 16)
            for u in range(2):
                pool.wait_ge(n_stored[u], 16 * (NT // 2))
                pool.wait_ge(z_stored[u], 16 * (NT // 2))

        @block.tensor
        def _(pe):
            def logits(g, v):
                for u in range(G):
                    t = G * g + u
                    pe.wait_ge(qs_done, t + 1)
                    pe.wait_ge(logits_kept, t)
                    for n in range(4):
                        ins = nc.tensor.matmul(zps[:, n * 512:(n + 1) * 512], qs[u][:], K[:, n * 512:(n + 1) * 512],
                                               start=True, stop=True)
                    ins.then_inc(logits_done, 1)

            def turn_weights(g, v, u):
                pe.wait_ge(masked, G * g + u + 1)
                for q in range(QUADS):
                    at = weights_at(u, q)
                    pe.wait_ge(quad_done, g * PLACES + at + 1)
                    for k in range(4):
                        b = 4 * q + k
                        ins = nc.tensor.transpose(tw[at % 2][:, k, :], E[v][:, u, b * P:(b + 1) * P], c["id32"][:])
                    ins.then_inc(turn_done, 1)

            def values(g, v):
                turn_weights(g, v, 0)
                pe.wait_ge(x_loaded, 16)
                pe.wait_ge(w_loaded, 64)
                for u in range(G):
                    t = G * g + u
                    pe.wait_ge(copied, t)
                    for q in range(QUADS):
                        pe.wait_ge(quad_done, g * PLACES + weights_at(u, q) + 3)
                        for j in range(4 * q, 4 * q + 4):
                            ins = nc.tensor.matmul(o[:], WT[u % 2][:, j, :], Xa[:, j, :], start=(j == 0), stop=(j == NT - 1))
                    ins.then_inc(pv_done, 1)
                    if u + 1 < G:
                        turn_weights(g, v, u + 1)
                    at = result_at(u)
                    pe.wait_ge(new_done, t + 3)
                    pe.wait_ge(quad_done, g * PLACES + at + 1)
                    for k in range(KC):
                        ins = nc.tensor.transpose(tw[at % 2][:, k, :], new[u % 2][:, k * P:(k + 1) * P], c["id32"][:])
                    ins.then_inc(turn_done, 1)
                    pe.wait_ge(quad_done, g * PLACES + at + 3)
                    if not last:
                        for w, ws in enumerate((w3s, w1s)):
                            for k in range(KC):
                                ins = nc.tensor.matmul(o[0:64, w * P:(w + 1) * P], ws[:, k, :], nT[:, k, :],
                                                       start=(k == 0), stop=(k == KC - 1))
                        ins.then_inc(kq_done, 1)
                    pe.wait_ge(ys_done, t + 2)
                    for k in range(KC):
                        ins = nc.tensor.matmul(y[:], nT[:, k, :], usb[:, k, :], start=(k == 0), stop=(k == KC - 1))
                    ins.then_inc(y_done, 1)
                    if not last:
                        pe.wait_ge(q_done, t + 1)
                        pr.passed(pe)
                        nc.tensor.matmul(o[0:64, 2 * P:3 * P], w2s[:], qT[:], start=True, stop=True).then_inc(qw_done, 1)

            in_groups(pe, logits, values)

        @block.scalar
        def _(act):
            def keep_logits(g, v):
                for u in range(G):
                    nc.scalar.copy(qs[u][:], QW[:, cols(G * g + u, P)]).then_inc(qs_done, 1)
                for u in range(G):
                    t = G * g + u
                    act.wait_ge(logits_done, t + 1)
                    nc.scalar.copy(E[v][:, u, :], zps[:]).then_inc(logits_kept, 1)

            def exps(g, v):
                for u in range(G):
                    t = G * g + u
                    act.wait_ge(max_done, t + 1)
                    nc.scalar.activation(E[v][:, u, :], E[v][:, u, :], ACT.Exp, bias=nmx[:, u:u + 1],
                                         accum_out=S[:, u:u + 1]).then_inc(exp_done, 1)

            def copy_weights(g, u):
                for q in range(QUADS):
                    at = weights_at(u, q)
                    act.wait_ge(turn_done, g * PLACES + at + 1)
                    nc.scalar.copy(WT[u % 2][:, 4 * q:4 * q + 4, :], tw[at % 2][:]).then_inc(quad_done, 1)

            def serve(g, v):
                act.wait_ge(inv_done, g + 1)
                copy_weights(g, 0)
                for u in range(G):
                    t = G * g + u
                    act.wait_ge(pv_done, t + 1)
                    act.wait_ge(n_stored[u % 2], (G // 2 * g + u // 2) * 16)
                    nc.scalar.activation(new[u % 2][:], o[:], ACT.Copy, scale=inv[v][:, u:u + 1]).then_inc(new_done, 1)
                    if last:
                        act.wait_ge(new_done, t + 3)
                        act.sem_inc(copied, 1)
                    if u + 1 < G:
                        copy_weights(g, u + 1)
                    at = result_at(u)
                    act.wait_ge(turn_done, g * PLACES + at + 1)
                    nc.scalar.copy(nT[:], tw[at % 2][:]).then_inc(quad_done, 1)
                    if not last:
                        act.wait_ge(kq_done, t + 1)
                        nc.scalar.copy(Kn[:, cols(t, P)], o[0:64, 0:P])
                        nc.scalar.copy(qT[:], o[0:64, P:2 * P]).then_inc(q_done, 1)
                    act.wait_ge(y_done, t + 1)
                    act.wait_ge(z_done, t + 1)
                    nc.scalar.copy(ys[u % 2][:], y[:]).then_inc(ys_done, 1)
                    if not last:
                        act.wait_ge(qw_done, t + 1)
                        nc.scalar.copy(QWn[:, cols(t, P)], o[0:64, 2 * P:3 * P]).then_inc(copied, 1)

            act.sem_inc(quad_done, 2)
            act.sem_inc(new_done, 2)
            act.sem_inc(ys_done, 2)
            keep_logits(0, 0)
            exps(0, 0)
            with act.Fori(0, NG // 2 - 1) as i:
                keep_logits(2 * i + 1, 1)
                exps(2 * i + 1, 1)
                serve(2 * i, 0)
                keep_logits(2 * i + 2, 0)
                exps(2 * i + 2, 0)
                serve(2 * i + 1, 1)
            keep_logits(NG - 1, 1)
            exps(NG - 1, 1)
            serve(NG - 2, 0)
            serve(NG - 1, 1)

        @block.vector
        def _(dve):
            def halve(Ev, k, link):
                link(nc.vector.tensor_scalar(th[:], lo[:], ratio[:, bass.ds(k, 1)], None, ALU.mult))
                for u in range(G):
                    ins = nc.vector.scalar_tensor_tensor(out=junk[u], in0=Ev[:, u, :], scalar=th[:, u:u + 1],
                                                         in1=Ev[:, u, :], op0=ALU.is_ge, op1=ALU.mult,
                                                         accum_out=F[:, u:u + 1])
                link(ins)
                link(nc.vector.tensor_tensor(hit[:], F[:], goal[:], ALU.is_ge))
                link(nc.vector.tensor_tensor(hit[:], hit[:], th[:], ALU.mult))
                link(nc.vector.tensor_tensor(lo[:], lo[:], hit[:], ALU.max))

            def bracket_end(halvings):
                return nc.vector.tensor_scalar(th[:], lo[:], float(np.exp(WIDTH / 2 ** halvings)) * (1 + 1e-6), None, ALU.mult)

            def single_out(Ev, link):
                for u in range(G + 1):
                    if u < G:
                        if u >= 3:
                            link.upto(1)
                        link.signals(nc.vector.scalar_tensor_tensor(out=below[u % 3][:], in0=Ev[:, u, :],
                                                                    scalar=th[:, u:u + 1], in1=Ev[:, u, :],
                                                                    op0=ALU.is_lt, op1=ALU.mult,
                                                                    accum_out=low_sum[:, u:u + 1]))
                    if u > 0:
                        link.upto(1 if u < G else 0)
                        pr.passed(dve)
                        link.signals(nc.vector.max(top8[:, u - 1, :], below[(u - 1) % 3][:]))
                link.upto(0)
                link.signals(nc.vector.tensor_copy(sum8a[:, :, 0:1], top8[:, :, 0:1]))
                link(nc.vector.tensor_tensor(sum8a[:, :, 1:8], top8[:, :, 1:8], top8[:, :, 0:7], ALU.add))
                link.signals(nc.vector.tensor_copy(sum8b[:, :, 0:2], sum8a[:, :, 0:2]))
                link(nc.vector.tensor_tensor(sum8b[:, :, 2:8], sum8a[:, :, 2:8], sum8a[:, :, 0:6], ALU.add))
                link.signals(nc.vector.tensor_copy(sum8a[:, :, 0:4], sum8b[:, :, 0:4]))
                link.signals(nc.vector.tensor_tensor(sum8a[:, :, 4:8], sum8b[:, :, 4:8], sum8b[:, :, 0:4], ALU.add))
                link(nc.vector.tensor_tensor(F[:], goal[:], S[:], ALU.subtract))
                link(nc.vector.tensor_tensor(F[:], F[:], low_sum[:], ALU.add))
                link(nc.vector.tensor_tensor(in8[:], sum8a[:], F[:].unsqueeze(2).broadcast_to([P, G, 8]), ALU.is_lt))
                link.signals(nc.vector.tensor_copy(unres[:].unsqueeze(2), in8[:, :, 7:8]))
                link.signals(nc.vector.tensor_copy(sum8b[:, :, 0:1], top8[:, :, 0:1]))
                link(nc.vector.tensor_scalar(in8[:, :, 0:7], in8[:, :, 0:7], -4.0, 4.0, ALU.mult, ALU.add))
                link.signals(nc.vector.tensor_tensor(sum8b[:, :, 1:8], in8[:, :, 0:7], top8[:, :, 1:8], ALU.max))
                link.signals(nc.vector.tensor_scalar(F[:], F[:], 0.0, None, ALU.is_le))
                link.upto(1)
                link(nc.vector.tensor_reduce(thr[:], sum8b[:], AX.X, ALU.min))
                link(nc.vector.tensor_tensor(F[:], F[:], th[:], ALU.mult))
                link(nc.vector.tensor_tensor(thr[:], thr[:], F[:], ALU.max))

            def any_unresolved(link):
                link(nc.vector.tensor_reduce(flag[:, 0:1], unres[:], AX.X, ALU.max))
                link(nc.vector.transpose(flagT[:], flag[:]))
                link(nc.vector.tensor_reduce(flag1[:], flagT[:], AX.X, ALU.max))
                for q in range(4):
                    (link if q == 3 else link.signals)(nc.vector.tensor_copy(flag4[0:1, q:q + 1], flag1[32 * q:32 * q + 1, :]))
                link(nc.vector.tensor_reduce(flagi[:], flag4[:], AX.X, ALU.max))
                pr.passed(dve)
                return dve.value_load(flagi[0:1, 0:1], min_val=0, max_val=1) > 0

            HALVE, SINGLE, ANY = 5, 2 * G + 17, 8
            BODY = G + 3 + SINGLE + ANY + 1

            def search(g, v):
                Ev = E[v]
                link = Link(dve, order, g * BODY)
                for u in range(G + 1):
                    if u < G:
                        dve.wait_ge(logits_kept, G * g + u + 1)
                        link.signals(nc.vector.tensor_reduce(mx[:, u:u + 1], Ev[:, u, :], AX.X, ALU.max))
                    if u > 0:
                        link.upto(1 if u < G else 0)
                        nc.vector.tensor_scalar(nmx[:, u - 1:u], mx[:, u - 1:u], -1.0, None, ALU.mult).then_inc(max_done, 1)
                dve.wait_ge(exp_done, G * (g + 1))
                link.signals(nc.vector.memset(lo[:], float(np.exp(-WIDTH))))
                link(nc.vector.tensor_scalar(goal[:], S[:], P_TOP, None, ALU.mult))
                pr.passed(dve)
                with dve.Fori(0, first) as k:
                    inner = Link(dve, order2, (g * first + k) * HALVE)
                    halve(Ev, k, inner)
                    assert inner.k == HALVE
                link(bracket_end(first))
                n = link.k
                single_out(Ev, link)
                assert link.k - n == SINGLE, link.k - n
                with dve.If(any_unresolved(link)):
                    inner = Link(dve, order3)
                    inner(nc.vector.tensor_tensor(hit[:].unsqueeze(2), top8[:, :, 7:8], unres[:].unsqueeze(2), ALU.mult))
                    inner(nc.vector.tensor_scalar(unres[:], unres[:], -1.0, 1.0, ALU.mult, ALU.add))
                    inner(nc.vector.tensor_tensor(th[:], th[:], unres[:], ALU.mult))
                    inner(nc.vector.tensor_tensor(th[:], th[:], hit[:], ALU.max))
                    single_out(Ev, inner)
                    with dve.If(any_unresolved(inner)):
                        with dve.Fori(first, ALL) as k:
                            halve(Ev, k, Link(dve, order4, (k - first) * HALVE))
                        rest = Link(dve, order4, (ALL - first) * HALVE)
                        rest(bracket_end(ALL))
                        single_out(Ev, rest)
                        rest(nc.vector.tensor_tensor(hit[:], lo[:], unres[:], ALU.mult))
                        rest(nc.vector.tensor_scalar(unres[:], unres[:], -1.0, 1.0, ALU.mult, ALU.add))
                        rest(nc.vector.tensor_tensor(thr[:], thr[:], unres[:], ALU.mult))
                        rest(nc.vector.tensor_tensor(thr[:], thr[:], hit[:], ALU.max))
                        dve.sem_clear(order4)
                    dve.sem_clear(order3)
                for u in range(G):
                    ins = nc.vector.scalar_tensor_tensor(out=Ev[:, u, :], in0=Ev[:, u, :], scalar=thr[:, u:u + 1],
                                                         in1=Ev[:, u, :], op0=ALU.is_ge, op1=ALU.mult,
                                                         accum_out=kept[:, u:u + 1]).then_inc(masked, 1)
                dve.wait_ge(masked, G * (g + 1))
                nc.vector.reciprocal(inv[v][:], kept[:]).then_inc(inv_done, 1)
                dve.wait_ge(inv_done, g + 1)
                link.k += 1
                dve.sem_inc(order, 1)
                assert link.k == BODY, (link.k, BODY)

            dve.wait_ge(steps_set, 1)
            with dve.Fori(0, NG // 2) as i:
                search(2 * i, 0)
                search(2 * i + 1, 1)


def norm_add(pr, c, z_dram, x_dram, out_dram, gamma, beta):
    nc = pr.nc
    with pr.stage():
        rows = pr.sb("rows", [P, 2, D])
        z, x, y = pr.sb("z", [P, NT, D]), pr.sb("x", [P, NT, D]), [pr.sb(f"y{u}", [P, D]) for u in range(2)]
        stats = [pr.sb(f"stats{u}", [P, 6]) for u in range(2)]
        mv = [pr.sb(f"mv{u}", [P, 2]) for u in range(2)]
        std, rstd = ([pr.sb(f"{n}{u}", [P, 1]) for u in range(2)] for n in ("std", "rstd"))
        z_loaded, x_loaded, stored = pr.sem("z_loaded"), pr.sem("x_loaded"), [pr.sem(f"stored{u}") for u in range(2)]
        r_loaded, mv_done, std_done, out_done, order, order2 = (
            pr.sem(n) for n in ("r_loaded", "mv_done", "std_done", "out_done", "order", "order_stats"))
        block = pr.block()

        @block.sync
        def _(sp):
            sp.dma_start(rows[:, 0, :], gamma.broadcast_to([P, D])).then_inc(r_loaded, 16)
            sp.dma_start(rows[:, 1, :], beta.broadcast_to([P, D])).then_inc(r_loaded, 16)
            pair_loads(pr, sp, (z, z_dram, z_loaded), (x, x_dram, x_loaded))

        @block.gpsimd
        def _(pool):
            with pool.Fori(0, NT // 2) as i:
                for u in range(2):
                    pool.wait_ge(out_done, 2 * i + u + 3)
                    pool.dma_start(out_dram[cols(2 * i + u, P), :], y[u][:]).then_inc(stored[u], 16)
            for u in range(2):
                pool.wait_ge(stored[u], 16 * (NT // 2))

        @block.scalar
        def _(act):
            with act.Fori(0, NT // 2) as i:
                for u in range(2):
                    act.wait_ge(mv_done, 2 * i + u + 1)
                    nc.scalar.activation(std[u][:], mv[u][:, 1:2], ACT.Sqrt, bias=c["eps"][:, 0:1]).then_inc(std_done, 1)

        @block.vector
        def _(dve):
            dve.sem_inc(out_done, 2)
            dve.wait_ge(r_loaded, 32)

            def stat(i, u):
                dve.wait_ge(z_loaded, 16 * i + 16)
                Link(dve, order2, 2 * i + u)(nc.vector.bn_stats(stats[u][:], z[:, 2 * i + u, :]))
                pr.passed(dve)
                nc.vector.bn_aggr(mv[u][:], stats[u][:]).then_inc(mv_done, 1)

            def norm(i, u):
                t = 2 * i + u
                link = Link(dve, order, t * 4)
                dve.wait_ge(mv_done, t + 1)
                dve.wait_ge(std_done, t + 1)
                link(nc.vector.reciprocal(rstd[u][:], std[u][:]))
                dve.wait_ge(stored[u], 16 * i)
                link(nc.vector.tensor_scalar(y[u][:], z[:, t, :], mv[u][:, 0:1], rstd[u][:, 0:1], ALU.subtract, ALU.mult))
                link(nc.vector.tensor_tensor(y[u][:], y[u][:], rows[:, 0, :], ALU.mult))
                link(nc.vector.tensor_tensor(y[u][:], y[u][:], rows[:, 1, :], ALU.add))
                dve.wait_ge(x_loaded, 16 * i + 16)
                nc.vector.tensor_tensor(y[u][:], y[u][:], x[:, t, :], ALU.add).then_inc(out_done, 1)

            one_ahead(dve, stat, norm)


def heads_mlp(pr, c, hid_dram, x_dram, out_dram, w1, w2, w3, w4, b1, b2, b3, b4):
    nc = pr.nc
    PAIRS = NT // 2
    with pr.stage():
        w1s, w2s, w3s, w4s = (pr.sb("w1", [P, KC, 256]), pr.sb("w2", [P, 2, 128]), pr.sb("w3", [P, 256]),
                              pr.sb("w4", [P, 2, D]))
        b1s, b2s, b3s, b4s = pr.sb("b1", [P, 2]), pr.sb("b2", [P, 1]), pr.sb("b3", [P, 2]), pr.sb("b4", [P, D])
        hid, x = pr.sb("hid", [P, NT, D]), pr.sb("x", [P, NT, D])
        low, e, elu_out, y = ([pr.sb(f"{n}{u}", [P, 2, D]) for u in range(2)] for n in ("low", "e", "elu_out", "y"))
        hT = [pr.sb(f"hT{u}", [P, 2, KC, P]) for u in range(2)]
        o1s, o2s, o3s = pr.sb("o1s", [P, 2, 2 * P]), pr.sb("o2s", [P, 2 * P]), pr.sb("o3s", [P, 2, 2 * P])
        turned, o1, o2, o3, o4 = (pr.ps("turned", [P, 2, KC, P]), pr.ps("o1", [P, 2, 2 * P]), pr.ps("o2", [P, 2 * P]),
                                  pr.ps("o3", [P, 2, 2 * P]), pr.ps("o4", [P, 2, D]))
        w_loaded, hid_loaded, x_loaded = pr.sem("w_loaded"), pr.sem("hid_loaded"), pr.sem("x_loaded")
        stored = [pr.sem(f"stored{u}") for u in range(2)]
        low_done, e_done, elu_done, turn_done, hT_done, out_done, order, order2 = (
            pr.sem(n) for n in ("low_done", "e_done", "elu_done", "turn_done", "hT_done", "out_done", "order", "order_sum"))
        l_done = [pr.sem(f"l{k}_done") for k in range(1, 5)]
        r_done = [pr.sem(f"r{k}_done") for k in range(1, 4)]
        block = pr.block()

        @block.sync
        def _(sp):
            pair_loads(pr, sp, (hid, hid_dram, hid_loaded), (x, x_dram, x_loaded))

        @block.gpsimd
        def _(pool):
            for dst, src in ((w1s, w1.rearrange("(k p) n -> p k n", p=P)), (w2s, w2.rearrange("(k p) n -> p k n", p=P)),
                             (w3s, w3), (w4s, w4.rearrange("(k p) n -> p k n", p=P)), (b1s, b1), (b2s, b2), (b3s, b3),
                             (b4s, b4.broadcast_to([P, D]))):
                pool.dma_start(dst[:], src).then_inc(w_loaded, 16)
            with pool.Fori(0, PAIRS // 2) as i:
                for u in range(2):
                    t = 2 * i + u
                    pool.wait_ge(out_done, t + 3)
                    pool.dma_start(out_dram[cols(t, 2 * P), :].rearrange("(v p) n -> p v n", p=P), y[u][:]).then_inc(stored[u], 16)
            for u in range(2):
                pool.wait_ge(stored[u], 16 * (PAIRS // 2))

        @block.tensor
        def _(pe):
            pe.sem_inc(turn_done, 2)

            def turn(i, u):
                t = 2 * i + u
                pe.wait_ge(elu_done, t + 1)
                pe.wait_ge(hT_done, t)
                for v in range(2):
                    for k in range(KC):
                        ins = nc.tensor.transpose(turned[:, v, k, :], elu_out[u][:, v, k * P:(k + 1) * P], c["id32"][:])
                ins.then_inc(turn_done, 1)

            def layers(i, u):
                t = 2 * i + u
                pe.wait_ge(w_loaded, 128)
                pe.wait_ge(hT_done, t + 1)
                for m in range(2):
                    for k in range(KC):
                        ins = nc.tensor.matmul(o1[:, m, :], w1s[:, k, m * P:(m + 1) * P], hT[u][:, :, k, :],
                                               start=(k == 0), stop=(k == KC - 1))
                ins.then_inc(l_done[0], 1)
                pe.wait_ge(r_done[0], t + 1)
                for k in range(2):
                    ins = nc.tensor.matmul(o2[:], w2s[:, k, :], o1s[:, k, :], start=(k == 0), stop=(k == 1))
                ins.then_inc(l_done[1], 1)
                pe.wait_ge(r_done[1], t + 1)
                for m in range(2):
                    ins = nc.tensor.matmul(o3[:, m, :], w3s[:, m * P:(m + 1) * P], o2s[:], start=True, stop=True)
                ins.then_inc(l_done[2], 1)
                pe.wait_ge(r_done[2], t + 1)
                pe.wait_ge(out_done, t + 2)
                for v in range(2):
                    for k in range(2):
                        ins = nc.tensor.matmul(o4[:, v, :], o3s[:, k, v * P:(v + 1) * P], w4s[:, k, :],
                                               start=(k == 0), stop=(k == 1))
                ins.then_inc(l_done[3], 1)

            pipelined(pe, PAIRS, (1, turn), (0, layers))

        @block.scalar
        def _(act):

            def exps(i, u):
                t = 2 * i + u
                act.wait_ge(low_done, t + 1)
                nc.scalar.activation(e[u][:], low[u][:], ACT.Exp).then_inc(e_done, 1)

            def copy_out(i, u):
                act.wait_ge(turn_done, 2 * i + u + 3)
                nc.scalar.copy(hT[u][:], turned[:]).then_inc(hT_done, 1)

            def relus(i, u):
                t = 2 * i + u
                act.wait_ge(w_loaded, 128)
                act.wait_ge(l_done[0], t + 1)
                for m in range(2):
                    ins = nc.scalar.activation(o1s[:, m, :], o1[:, m, :], ACT.Relu, bias=b1s[:, m:m + 1])
                ins.then_inc(r_done[0], 1)
                act.wait_ge(l_done[1], t + 1)
                nc.scalar.activation(o2s[:], o2[:], ACT.Relu, bias=b2s[:, 0:1]).then_inc(r_done[1], 1)
                act.wait_ge(l_done[2], t + 1)
                for m in range(2):
                    ins = nc.scalar.activation(o3s[:, m, :], o3[:, m, :], ACT.Relu, bias=b3s[:, m:m + 1])
                ins.then_inc(r_done[2], 1)

            pipelined(act, PAIRS, (2, exps), (1, copy_out), (0, relus))

        @block.vector
        def _(dve):
            dve.sem_inc(out_done, 2)

            def elu(i, u):
                t = 2 * i + u
                pair = hid[:, cols(t, 2), :]
                dve.wait_ge(hid_loaded, 16 * t + 16)
                dve.wait_ge(elu_done, t)
                nc.vector.tensor_scalar(low[u][:], pair, 0.0, None, ALU.min).then_inc(low_done, 1)
                dve.wait_ge(e_done, t + 1)
                Link(dve, order, t)(nc.vector.tensor_scalar(pair, pair, 0.0, None, ALU.max))
                dve.wait_ge(turn_done, t + 1)
                nc.vector.scalar_tensor_tensor(out=elu_out[u][:], in0=e[u][:], scalar=-1.0, in1=pair,
                                               op0=ALU.add, op1=ALU.add).then_inc(elu_done, 1)

            def result(i, u):
                t = 2 * i + u
                dve.wait_ge(w_loaded, 128)
                dve.wait_ge(l_done[3], t + 1)
                dve.wait_ge(stored[u], 16 * i)
                Link(dve, order2, t)(nc.vector.tensor_tensor(y[u][:], o4[:], b4s[:].unsqueeze(1).broadcast_to([P, 2, D]), ALU.add))
                dve.wait_ge(x_loaded, 16 * t + 16)
                nc.vector.tensor_tensor(y[u][:], y[u][:], x[:, cols(t, 2), :], ALU.add).then_inc(out_done, 1)

            pipelined(dve, PAIRS, (2, elu), (0, result))


def project_qkv(pr, c, x_dram, wq, wk, wv, bq, bk, bv, q_dram, kT, V):
    nc = pr.nc
    with pr.stage():
        f = norm_and_turn(pr, c, x_dram)
        w = [pr.sb(f"w{n}", [P, KC, D]) for n in "qkv"]
        bqs, bks, bvs = pr.sb("bq", [P, KC]), pr.sb("bk", [P, KC]), pr.sb("bv", [P, D])
        qT = [pr.sb(f"qT{u}", [P, KC, P]) for u in range(2)]
        qp, kp, vp = pr.ps("qp", [P, KC, P]), pr.ps("kp", [P, KC, P]), pr.ps("vp", [P, D])
        w_loaded = pr.sem("w_loaded")
        stored = [pr.sem(f"stored{u}") for u in range(2)]
        q_done, k_done, v_done, q_out, k_out, v_out = (pr.sem(n) for n in ("q_done", "k_done", "v_done", "q_out", "k_out", "v_out"))
        block = pr.block()

        @block.sync
        def _(sp):
            def weights():
                for dst, src in zip(w, (wq, wk, wv)):
                    sp.dma_start(dst[:], src.rearrange("(k p) n -> p k n", p=P)).then_inc(w_loaded, 16)
                sp.dma_start(bqs[:], bq).then_inc(w_loaded, 16)
                sp.dma_start(bks[:], bk).then_inc(w_loaded, 16)
                sp.dma_start(bvs[:], bv.broadcast_to([P, D])).then_inc(w_loaded, 16)

            f["load"](sp, weights)

        @block.gpsimd
        def _(pool):
            with pool.Fori(0, NT // 2) as i:
                for u in range(2):
                    t = 2 * i + u
                    pool.wait_ge(q_out, t + 1)
                    pool.dma_start(q_dram[cols(t, P), :], qT[u][:].rearrange("p k n -> p (k n)")).then_inc(stored[u], 16)
            for u in range(2):
                pool.wait_ge(stored[u], 16 * (NT // 2))

        @block.vector
        def _(dve):
            dve.sem_inc(f["h_done"], 2)

            def values(i, u):
                dve.wait_ge(w_loaded, 96)
                dve.wait_ge(v_done, 2 * i + u + 3)
                nc.vector.tensor_tensor(V[:, 2 * i + u, :], vp[:], bvs[:], ALU.add).then_inc(v_out, 1)

            in_chunks(dve, 2, lambda q: f["dve_stats"](dve, q), lambda i, u: f["dve_norm"](dve, i, u, f["turn_done"]), values)

        @block.tensor
        def _(pe):
            pe.sem_inc(f["turn_done"], 2)
            pe.sem_inc(v_done, 2)

            def products(i, u):
                t = 2 * i + u
                pe.wait_ge(w_loaded, 96)
                pe.wait_ge(f["hT_done"], t + 3)
                for ws, dst, done, out in ((w[0], qp, q_done, q_out), (w[1], kp, k_done, k_out)):
                    pe.wait_ge(out, t)
                    for m in range(KC):
                        for k in range(KC):
                            ins = nc.tensor.matmul(dst[:, m, :], ws[:, k, m * P:(m + 1) * P], f["hT"][u][:, k, :],
                                                   start=(k == 0), stop=(k == KC - 1))
                    ins.then_inc(done, 1)
                pe.wait_ge(v_out, t)
                for k in range(KC):
                    ins = nc.tensor.matmul(vp[:], f["hT"][u][:, k, :], w[2][:, k, :], start=(k == 0), stop=(k == KC - 1))
                ins.then_inc(v_done, 1)

            one_ahead(pe, lambda i, u: f["pe_turn"](pe, i, u), products)

        @block.scalar
        def _(act):
            act.sem_inc(f["hT_done"], 2)

            def copies(i, u):
                t = 2 * i + u
                act.wait_ge(w_loaded, 96)
                act.wait_ge(q_done, t + 1)
                act.wait_ge(stored[u], 16 * i)
                for m in range(KC):
                    ins = nc.scalar.activation(qT[u][:, m, :], qp[:, m, :], ACT.Identity, bias=bqs[:, m:m + 1])
                ins.then_inc(q_out, 1)
                act.wait_ge(k_done, t + 1)
                for m in range(KC):
                    ins = nc.scalar.activation(kT[:, m, cols(t, P)], kp[:, m, :], ACT.Identity, bias=bks[:, m:m + 1])
                ins.then_inc(k_out, 1)

            in_chunks(act, 1, lambda q: f["act_std"](act, q), lambda i, u: f["act_hT"](act, i, u, v_done), copies)


def masked_attention(pr, c, q_dram, kT, V, adj, x_dram, out_dram):
    nc = pr.nc
    SCALE = float(D) ** -0.5
    with pr.stage():
        qT = [pr.sb(f"qT{u}", [P, KC, P]) for u in range(2)]
        a = [pr.sb(f"a{u}", [P, N]) for u in range(2)]
        z, zero, e = pr.sb("z", [P, N]), pr.sb("zero", [P, N]), [pr.sb(f"e{u}", [P, N]) for u in range(2)]
        eT = pr.sb("eT", [P, NT, P])
        x, y = ([pr.sb(f"{n}{u}", [P, D]) for u in range(2)] for n in ("x", "y"))
        mx, nmx, S, inv = ([pr.sb(f"{n}{u}", [P, 1]) for u in range(2)] for n in ("mx", "nmx", "S", "inv"))
        zps = pr.ps("zps", [P, N])
        tw = [pr.ps(f"tw{u}", [P, 4, P]) for u in range(2)]
        o = pr.ps("o", [P, D])
        q_loaded, a_loaded, x_loaded, stored = ([pr.sem(f"{n}{u}") for u in range(2)]
                                                for n in ("q_loaded", "a_loaded", "x_loaded", "stored"))
        z_done, z_read, max_done, exp_done, turn_done, quad_done, pv_done, out_done, order, order2 = (
            pr.sem(n) for n in ("z_done", "z_read", "max_done", "exp_done", "turn_done", "quad_done", "pv_done",
                                "out_done", "order", "order_result"))
        block = pr.block()

        @block.sync
        def _(sp):
            def load_q(t, u):
                sp.dma_start(qT[u][:], q_dram[cols(t, P), :].rearrange("p (k n) -> p k n", n=P)).then_inc(q_loaded[u], 16)

            def load_a(t, u):
                sp.dma_start(a[u][:], adj[cols(t, P), :]).then_inc(a_loaded[u], 16)

            def load_x(t, u):
                sp.dma_start(x[u][:], x_dram[cols(t, P), :]).then_inc(x_loaded[u], 16)

            for u in range(2):
                load_q(u, u)
                load_a(u, u)
                load_x(u, u)
            with sp.Fori(1, NT // 2) as i:
                for u in range(2):
                    t = 2 * i + u
                    sp.wait_ge(z_done, t + 1)
                    load_q(t, u)
                    sp.wait_ge(z_read, t - 1)
                    load_a(t, u)
                    sp.wait_ge(out_done, t + 1)
                    load_x(t, u)

        @block.gpsimd
        def _(pool):
            with pool.Fori(0, NT // 2) as i:
                for u in range(2):
                    pool.wait_ge(out_done, 2 * i + u + 3)
                    pool.dma_start(out_dram[cols(2 * i + u, P), :], y[u][:]).then_inc(stored[u], 16)
            for u in range(2):
                pool.wait_ge(stored[u], 16 * (NT // 2))

        @block.tensor
        def _(pe):
            def logits(i, u, n):
                t = 2 * i + u
                if n == 0:
                    pe.wait_ge(q_loaded[u], 16 * i + 16)
                    pe.wait_ge(z_read, t)
                for k in range(KC):
                    ins = nc.tensor.matmul(zps[:, n * 512:(n + 1) * 512], qT[u][:, k, :], kT[:, k, n * 512:(n + 1) * 512],
                                           start=(k == 0), stop=(k == KC - 1))
                if n == 3:
                    ins.then_inc(z_done, 1)

            def turn(i, u, q):
                t = 2 * i + u
                pe.wait_ge(exp_done, t + 3)
                pe.wait_ge(quad_done, 4 * t + q + 1)
                for k in range(4):
                    b = 4 * q + k
                    ins = nc.tensor.transpose(tw[q % 2][:, k, :], e[u][:, b * P:(b + 1) * P], c["id32"][:])
                ins.then_inc(turn_done, 1)

            def values(i, u):
                t = 2 * i + u
                pe.wait_ge(out_done, t + 2)
                for q in range(4):
                    pe.wait_ge(quad_done, 4 * t + q + 3)
                    for j in range(4 * q, 4 * q + 4):
                        ins = nc.tensor.matmul(o[:], eT[:, j, :], V[:, j, :], start=(j == 0), stop=(j == NT - 1))
                ins.then_inc(pv_done, 1)

            def step(i, u):
                for n in range(4):
                    logits(i + u, 1 - u, n)
                    turn(i, u, n)
                values(i, u)

            pe.sem_inc(z_done, 2)
            pe.sem_inc(pv_done, 2)
            for n in range(4):
                logits(0, 0, n)
            with pe.Fori(0, NT // 2 - 1) as i:
                step(i, 0)
                step(i, 1)
            step(NT // 2 - 1, 0)
            for q in range(4):
                turn(NT // 2 - 1, 1, q)
            values(NT // 2 - 1, 1)

        @block.scalar
        def _(act):
            def exps(i, u):
                t = 2 * i + u
                act.wait_ge(max_done, t + 1)
                act.wait_ge(pv_done, t + 1)
                act.wait_ge(out_done, t + 1)
                nc.scalar.activation(e[u][:], z[:], ACT.Exp, bias=nmx[u][:, 0:1], accum_out=S[u][:, 0:1]).then_inc(exp_done, 1)

            def copies(i, u):
                t = 2 * i + u
                act.wait_ge(pv_done, t + 2)
                for q in range(4):
                    act.wait_ge(turn_done, 4 * t + q + 1)
                    nc.scalar.copy(eT[:, 4 * q:4 * q + 4, :], tw[q % 2][:]).then_inc(quad_done, 1)

            act.sem_inc(exp_done, 2)
            act.sem_inc(quad_done, 2)
            exps(0, 0)
            with act.Fori(0, NT // 2 - 1) as i:
                copies(i, 0)
                exps(i, 1)
                copies(i, 1)
                exps(i + 1, 0)
            copies(NT // 2 - 1, 0)
            exps(NT // 2 - 1, 1)
            copies(NT // 2 - 1, 1)

        @block.vector
        def _(dve):
            def scores(i, u):
                t = 2 * i + u
                link = Link(dve, order, t * 3)
                dve.wait_ge(z_done, t + 3)
                dve.wait_ge(a_loaded[u], 16 * i + 16)
                dve.wait_ge(exp_done, t + 2)
                nc.vector.scalar_tensor_tensor(out=z[:], in0=zps[:], scalar=SCALE, in1=a[u][:], op0=ALU.mult,
                                               op1=ALU.mult).then_inc(z_read, 1)
                dve.wait_ge(z_read, t + 1)
                link(nc.vector.tensor_scalar(zero[:], z[:], 0.0, -10000.0, ALU.is_equal, ALU.mult))
                link(nc.vector.tensor_tensor(z[:], z[:], zero[:], ALU.add))
                link(nc.vector.tensor_reduce(mx[u][:], z[:], AX.X, ALU.max))
                nc.vector.tensor_scalar(nmx[u][:], mx[u][:], -1.0, None, ALU.mult).then_inc(max_done, 1)

            def result(i, u):
                t = 2 * i + u
                link = Link(dve, order2, t * 2)
                dve.wait_ge(pv_done, t + 3)
                link(nc.vector.reciprocal(inv[u][:], S[u][:]))
                dve.wait_ge(stored[u], 16 * i)
                link(nc.vector.tensor_scalar(y[u][:], o[:], inv[u][:, 0:1], 0.0, ALU.mult, ALU.max))
                dve.wait_ge(x_loaded[u], 16 * i + 16)
                nc.vector.tensor_tensor(y[u][:], y[u][:], x[u][:], ALU.add).then_inc(out_done, 1)

            dve.sem_inc(out_done, 2)
            one_ahead(dve, scores, result)


def layout(inputs):
    a = {k: np.asarray(v) for k, v in inputs.items()}
    ins = {"x": a["x"], "adj": a["adj"]}
    ins["w0"] = a["L0_gnn_W_seq"]
    ins["a01"] = np.tile(a["L0_gnn_a1"], 16).reshape(1, D)
    ins["a02"] = np.tile(a["L0_gnn_a2"], 16).reshape(1, D)
    ins["w0o"] = a["L0_gnn_W_out"]
    ins["b0o"] = a["L0_gnn_b_out"].reshape(1, D)
    for n in ("W1", "W2", "W3", "U1_0", "U1_1", "U2_0", "U2_1"):
        ins[f"l1_{n}"] = a[f"L1_gnn_{n}"]
    ins["gamma"] = a["L1_gnn_gamma"].reshape(1, D)
    ins["beta"] = a["L1_gnn_beta"].reshape(1, D)
    ins["w2h"] = np.transpose(a["L2_gnn_W"], (1, 0, 2)).reshape(D, D)
    ins["a21"] = a["L2_gnn_a1"].reshape(1, D)
    ins["a22"] = a["L2_gnn_a2"].reshape(1, D)
    for n in ("W1", "W2", "W3", "W4"):
        ins[f"l2_{n}"] = a[f"L2_gnn_{n}"].T
    for n in ("b1", "b2", "b3"):
        ins[f"l2_{n}"] = a[f"L2_gnn_{n}"].reshape(-1, P).T
    ins["l2_b4"] = a["L2_gnn_b4"].reshape(1, D)
    for n in "qkv":
        ins[f"l3_W{n}"] = a[f"L3_gnn_W_{n}"].T
    for n in "qk":
        ins[f"l3_b{n}"] = a[f"L3_gnn_b_{n}"].reshape(KC, P).T
    ins["l3_bv"] = a["L3_gnn_b_v"].reshape(1, D)
    return {k: np.ascontiguousarray(v) for k, v in ins.items()}


def build(nc, ins, out):
    pr = Program(nc)
    root = ExitStack()
    with root:
        def sb(name, shape, dt=F32):
            return root.enter_context(nc.sbuf_tensor(name, shape, dt))

        def dram(name, shape=(N, D), dt=F32):
            return nc.dram_tensor(name, list(shape), dt, kind="Internal").ap()
        c = dict(id32=sb("id32", [P, P]), id16=sb("id16", [P, P], BF16), ones16=sb("ones16", [P, 2], BF16),
                 zero16=sb("zero16", [P, 512], BF16), eps=sb("eps", [P, 1]))
        adjT_dram = dram("adjT_dram", [N, N], BF16)
        seq_dram, hid_dram = dram("seq_dram"), dram("hid_dram")
        arow_dram = dram("arow_dram", [16, N])
        x1, x2, x3 = dram("x1"), dram("x2"), dram("x3")
        h_dram, xf1, xf2, xa1, xa2 = (dram(n) for n in ("h_dram", "xf1", "xf2", "xa1", "xa2"))
        z1, z2, z3, z4 = (dram(n) for n in ("z1", "z2", "z3", "z4"))
        q_dram, keys_dram = dram("q_dram"), dram("keys_dram", [64, 2 * N])
        constants(pr, c)

        def heads_layer(x, w, a1, a2, H, DH, groups):
            with nc.sbuf_tensor(f"scores_{pr.n}", [P, 2, NT, H], F32) as scores, \
                    nc.sbuf_tensor(f"fac_{pr.n}", [P, 6, NT, H], F32) as fac:
                heads_project(pr, c, x, w, a1, a2, seq_dram, scores, H, DH)
                heads_factors(pr, c, scores, fac, arow_dram, H)
                for g in range(groups):
                    heads_attend(pr, c, fac, seq_dram, arow_dram, hid_dram, H, DH, g, H // groups)

        with nc.sbuf_tensor("adjT", [P, NT, N], BF16) as adjT:
            c["adjT"] = adjT
            transpose_adjacency(pr, c, ins["adj"], adjT_dram)
            heads_layer(ins["x"], ins["w0"], ins["a01"], ins["a02"], 16, 32, 2)
            heads_out(pr, c, hid_dram, ins["x"], x1, ins["w0o"], ins["b0o"])
            w = [ins[f"l1_{n}"] for n in ("W1", "W2", "W3")]
            with nc.sbuf_tensor("keys", [64, 2, N], F32) as ks:
                features_keys(pr, c, x1, h_dram, *w, ks[:, 0], ks[:, 1])
                carry(pr, keys_dram, ks[:].rearrange("p v n -> p (v n)"))
            walk(pr, c, 0, h_dram, xf1, h_dram, z1, ins["l1_U1_0"])
            walk(pr, c, 1, xf1, xf2, z1, z2, ins["l1_U1_1"])
        with nc.sbuf_tensor("keys2", [64, 4, N], F32) as ks:
            carry(pr, ks[:, 0:2, :].rearrange("p v n -> p (v n)"), keys_dram)
            top_attention(pr, c, 7, False, h_dram, xa1, z2, z3, ins["l1_U2_0"], ks[:, 0], ks[:, 1], *w, ks[:, 2], ks[:, 3])
            top_attention(pr, c, 10, True, xa1, xa2, z3, z4, ins["l1_U2_1"], ks[:, 2], ks[:, 3], *w, None, None)
        norm_add(pr, c, z4, x1, x2, ins["gamma"], ins["beta"])
        with nc.sbuf_tensor("adjT2", [P, NT, N], BF16) as adjT:
            c["adjT"] = adjT
            reload_adjacency(pr, c, adjT_dram)
            heads_layer(x2, ins["w2h"], ins["a21"], ins["a22"], 8, 64, 2)
        heads_mlp(pr, c, hid_dram, x2, x3, *(ins[f"l2_{n}"] for n in ("W1", "W2", "W3", "W4", "b1", "b2", "b3", "b4")))
        with nc.sbuf_tensor("kT", [P, KC, N], F32) as kT, nc.sbuf_tensor("V", [P, NT, D], F32) as V:
            project_qkv(pr, c, x3, *(ins[f"l3_W{n}"] for n in "qkv"), *(ins[f"l3_b{n}"] for n in "qkv"), q_dram, kT, V)
            masked_attention(pr, c, q_dram, kT, V, ins["adj"], x3, out)


def kernel(**inputs):
    import concourse.bacc as bacc
    from concourse.bass_utils import run_bass_kernel_spmd

    nc = bacc.Bacc("TRN2", target_bir_lowering=False, num_devices=1)
    arrays = {f"in_{k}": v for k, v in layout(inputs).items()}
    ins = {k[3:]: nc.dram_tensor(k, v.shape, mybir.dt.from_np(v.dtype), kind="ExternalInput").ap()
           for k, v in arrays.items()}
    out = nc.dram_tensor("out_0", (N, D), F32, kind="ExternalOutput").ap()
    build(nc, ins, out)
    r = run_bass_kernel_spmd(nc, [arrays], core_ids=[0])
    return r.results[0]["out_0"]
```
